# Optimizing a Trainium2 kernel written in Bass

```python
import numpy as np
import jax
import jax.numpy as jnp

def _softmax(x, axis=-1):
    return jax.nn.softmax(x, axis=axis)

def _gelu(x):
    return jax.nn.gelu(x, approximate=True)

def _silu(x):
    return jax.nn.silu(x)

def _sigmoid(x):
    return jax.nn.sigmoid(x)

def _layernorm(x, axis=-1, eps=1e-05):
    m = jnp.mean(x, axis=axis, keepdims=True)
    v = jnp.var(x, axis=axis, keepdims=True)
    return (x - m) / jnp.sqrt(v + eps)

def _scatter_add(tgt, idx, src, axis=0):
    return tgt.at[idx].add(src)

def _segment_sum(src, seg, n):
    return jax.ops.segment_sum(src, seg, n)
kernel_name = 'mk_macaron_d1_jaxref_r8_affb2e'

def setup_inputs(seed: int=0):
    np.random.seed(seed)
    _w = jnp.asarray

    def _L0_attn_setup():
        import jax, jax.numpy as jnp
        import numpy as np
        B, S, D = (1, 256, 512)
        H = 32
        QL = 192
        KVL = 64
        DN = 128
        DR = 64
        DV = 128
        BASE = 10000.0
        FACTOR = 40.0
        BFAST, BSLOW = (32.0, 1.0)
        OLD_CTX = 4096.0
        MSCALE = 1.0

        def _yarn_inv_freq():
            freqs = 1.0 / BASE ** (jnp.arange(0, DR, 2, dtype=jnp.float32) / DR)
            wavelengths = 2.0 * jnp.pi / freqs
            ramp = jnp.clip((wavelengths / OLD_CTX - BSLOW) / (BFAST - BSLOW), 0.0, 1.0)
            scale = 1.0 - ramp + ramp * FACTOR
            return (freqs / scale, MSCALE)

        def _apply_rope(x, inv_freq, mscale):
            seq = x.shape[-2]
            pos = jnp.arange(seq, dtype=jnp.float32)
            f = jnp.concatenate([pos[:, None] * inv_freq[None, :]] * 2, axis=-1)
            cos = jnp.cos(f) * mscale
            sin = jnp.sin(f) * mscale
            half = DR // 2
            x1, x2 = (x[..., :half], x[..., half:])
            c1, c2 = (cos[:, :half], cos[:, half:])
            s2 = sin[:, half:]
            return jnp.concatenate([x1 * c1 - x2 * s2, x1 * s2 + x2 * c2], axis=-1)
        key = jax.random.key(seed)
        ks = jax.random.split(key, 10)

        def glorot(k, shape):
            lim = np.sqrt(6.0 / (shape[0] + shape[1])).astype(np.float32)
            return jax.random.uniform(k, shape, jnp.float32, -lim, lim)
        return {'hidden_states': jax.random.normal(ks[0], (B, S, D), jnp.float32), 'w_q_down': glorot(ks[1], (D, QL)), 'w_q_up_nope': glorot(ks[2], (QL, H * DN)), 'w_q_up_rope': glorot(ks[3], (QL, H * DR)), 'w_kv_down': glorot(ks[4], (D, KVL)), 'w_k_rope': glorot(ks[5], (D, DR)), 'w_uk': glorot(ks[6], (H * DN, KVL)), 'w_uv': glorot(ks[7], (H * DV, KVL)), 'w_out': glorot(ks[8], (H * DV, D))}
    _L0_attn_in = _L0_attn_setup()

    def _L0_ffn_setup():
        import jax, jax.numpy as jnp
        import numpy as np
        SCALING = 16.0 / 8.0
        GAMMA = 1.0
        EPS = 1e-12
        key = jax.random.key(seed)
        ks = jax.random.split(key, 8)
        B, T, H, O = (4, 256, 512, 512)
        E_tot, E_act, r = (16, 4, 8)
        return {'x': jax.random.normal(ks[0], (B, T, H), jnp.float32), 'W_base': jax.random.normal(ks[1], (O, H), jnp.float32) * 0.02, 'b_base': jax.random.normal(ks[2], (O,), jnp.float32) * 0.02, 'lora_A': jax.random.normal(ks[3], (E_tot, r, H), jnp.float32) * 0.02, 'lora_B': jax.random.normal(ks[4], (E_tot, O, r), jnp.float32) * 0.02, 'router_W': jax.random.normal(ks[5], (E_tot, H), jnp.float32) * 0.02, 'router_b': jax.random.normal(ks[6], (E_tot,), jnp.float32) * 0.02, 'domain_prior': jax.random.uniform(ks[7], (E_tot,), jnp.float32), 'active': jnp.arange(E_act, dtype=jnp.int32)}
    _L0_ffn_in = _L0_ffn_setup()
    _d = {'L0_attn_hidden_states': _L0_attn_in['hidden_states'], 'L0_attn_w_q_down': _L0_attn_in['w_q_down'], 'L0_attn_w_q_up_nope': _L0_attn_in['w_q_up_nope'], 'L0_attn_w_q_up_rope': _L0_attn_in['w_q_up_rope'], 'L0_attn_w_kv_down': _L0_attn_in['w_kv_down'], 'L0_attn_w_k_rope': _L0_attn_in['w_k_rope'], 'L0_attn_w_uk': _L0_attn_in['w_uk'], 'L0_attn_w_uv': _L0_attn_in['w_uv'], 'L0_attn_w_out': _L0_attn_in['w_out'], 'L0_ffn_W_base': _L0_ffn_in['W_base'], 'L0_ffn_b_base': _L0_ffn_in['b_base'], 'L0_ffn_lora_A': _L0_ffn_in['lora_A'], 'L0_ffn_lora_B': _L0_ffn_in['lora_B'], 'L0_ffn_router_W': _L0_ffn_in['router_W'], 'L0_ffn_router_b': _L0_ffn_in['router_b'], 'L0_ffn_domain_prior': _L0_ffn_in['domain_prior'], 'L0_ffn_active': _L0_ffn_in['active']}
    _x0 = _d['L0_attn_hidden_states']
    _d['L0_attn_hidden_states'] = jax.random.normal(jax.random.fold_in(jax.random.key(seed), 1), (4, 512, 512), dtype=_x0.dtype)
    del _x0
    return _d

def reference(L0_attn_hidden_states, L0_attn_w_q_down, L0_attn_w_q_up_nope, L0_attn_w_q_up_rope, L0_attn_w_kv_down, L0_attn_w_k_rope, L0_attn_w_uk, L0_attn_w_uv, L0_attn_w_out, L0_ffn_W_base, L0_ffn_b_base, L0_ffn_lora_A, L0_ffn_lora_B, L0_ffn_router_W, L0_ffn_router_b, L0_ffn_domain_prior, L0_ffn_active):

    def _L0_attn_ref(hidden_states, w_q_down, w_q_up_nope, w_q_up_rope, w_kv_down, w_k_rope, w_uk, w_uv, w_out):
        import jax, jax.numpy as jnp
        import numpy as np
        B, S, D = (1, 256, 512)
        H = 32
        QL = 192
        KVL = 64
        DN = 128
        DR = 64
        DV = 128
        BASE = 10000.0
        FACTOR = 40.0
        BFAST, BSLOW = (32.0, 1.0)
        OLD_CTX = 4096.0
        MSCALE = 1.0

        def _yarn_inv_freq():
            freqs = 1.0 / BASE ** (jnp.arange(0, DR, 2, dtype=jnp.float32) / DR)
            wavelengths = 2.0 * jnp.pi / freqs
            ramp = jnp.clip((wavelengths / OLD_CTX - BSLOW) / (BFAST - BSLOW), 0.0, 1.0)
            scale = 1.0 - ramp + ramp * FACTOR
            return (freqs / scale, MSCALE)

        def _apply_rope(x, inv_freq, mscale):
            seq = x.shape[-2]
            pos = jnp.arange(seq, dtype=jnp.float32)
            f = jnp.concatenate([pos[:, None] * inv_freq[None, :]] * 2, axis=-1)
            cos = jnp.cos(f) * mscale
            sin = jnp.sin(f) * mscale
            half = DR // 2
            x1, x2 = (x[..., :half], x[..., half:])
            c1, c2 = (cos[:, :half], cos[:, half:])
            s2 = sin[:, half:]
            return jnp.concatenate([x1 * c1 - x2 * s2, x1 * s2 + x2 * c2], axis=-1)
        b, s, _ = hidden_states.shape
        c_q = hidden_states @ w_q_down
        q_nope = (c_q @ w_q_up_nope).reshape(b, s, H, DN).transpose(0, 2, 1, 3)
        q_rope = (c_q @ w_q_up_rope).reshape(b, s, H, DR).transpose(0, 2, 1, 3)
        c_kv = hidden_states @ w_kv_down
        k_rope = (hidden_states @ w_k_rope)[:, None]
        inv_freq, mscale = _yarn_inv_freq()
        q_rope = _apply_rope(q_rope, inv_freq, mscale)
        k_rope = _apply_rope(k_rope, inv_freq, mscale)
        wuk = w_uk.reshape(H, DN, KVL)
        q_lat = jnp.einsum('bhsd,hdr->bhsr', q_nope, wuk)
        scores = jnp.einsum('bhsr,btr->bhst', q_lat, c_kv) + jnp.einsum('bhsd,btd->bhst', q_rope, k_rope[:, 0])
        scores = scores / jnp.sqrt(jnp.float32(DN + DR))
        causal = jnp.tril(jnp.ones((s, s), dtype=bool))
        scores = jnp.where(causal, scores, jnp.finfo(scores.dtype).min)
        probs = jax.nn.softmax(scores, axis=-1)
        out_lat = jnp.einsum('bhst,btr->bhsr', probs, c_kv)
        wuv = w_uv.reshape(H, DV, KVL)
        out = jnp.einsum('bhsr,hdr->bhsd', out_lat, wuv)
        out = out.transpose(0, 2, 1, 3).reshape(b, s, H * DV)
        return out @ w_out

    def _L0_ffn_ref(x, W_base, b_base, lora_A, lora_B, router_W, router_b, domain_prior, active):
        import jax, jax.numpy as jnp
        import numpy as np
        SCALING = 16.0 / 8.0
        GAMMA = 1.0
        EPS = 1e-12
        y = jnp.einsum('bth,oh->bto', x, W_base) + b_base
        A = lora_A[active]
        Bm = lora_B[active]
        z = jnp.einsum('bth,erh->bter', x, A)
        contribs = jnp.einsum('bter,eor->bteo', z, Bm) * SCALING
        logits = jnp.einsum('bth,eh->bte', x, router_W) + router_b
        logits = logits[..., active]
        prior = domain_prior[active]
        alpha = jax.nn.softmax(jnp.log(prior + EPS) + logits / GAMMA, axis=-1)
        return y + jnp.einsum('bteo,bte->bto', contribs, alpha)
    x = L0_attn_hidden_states
    x = x + 0.5 * _L0_ffn_ref(_layernorm(x, axis=-1), L0_ffn_W_base, L0_ffn_b_base, L0_ffn_lora_A, L0_ffn_lora_B, L0_ffn_router_W, L0_ffn_router_b, L0_ffn_domain_prior, L0_ffn_active)
    x = x + _L0_attn_ref(_layernorm(x, axis=-1), L0_attn_w_q_down, L0_attn_w_q_up_nope, L0_attn_w_q_up_rope, L0_attn_w_kv_down, L0_attn_w_k_rope, L0_attn_w_uk, L0_attn_w_uv, L0_attn_w_out)
    x = x + 0.5 * _L0_ffn_ref(_layernorm(x, axis=-1), L0_ffn_W_base, L0_ffn_b_base, L0_ffn_lora_A, L0_ffn_lora_B, L0_ffn_router_W, L0_ffn_router_b, L0_ffn_domain_prior, L0_ffn_active)
    return x

_drawn_inputs = setup_inputs


def setup_inputs(seed=0):
    import zlib

    import numpy as np

    out = dict(_drawn_inputs(seed))
    spreads = {}
    factors = {'L0_attn_w_q_down': 4.698,
     'L0_attn_w_q_up_nope': 8.0,
     'L0_attn_w_q_up_rope': 4.882,
     'L0_attn_w_k_rope': 4.86,
     'L0_attn_w_uk': 8.0,
     'L0_ffn_b_base': 3.144,
     'L0_ffn_router_W': 6.679,
     'L0_ffn_router_b': 184.647,
     'L0_ffn_domain_prior': 200.0}
    for name, (base, spread) in spreads.items():
        noise = np.random.default_rng([zlib.crc32(name.encode()), seed]).standard_normal(out[name].shape)
        drawn = base * np.exp(spread * noise) if base else spread * noise
        out[name] = jnp.asarray(drawn.astype(out[name].dtype))
    for name, factor in factors.items():
        out[name] = (out[name] * factor).astype(out[name].dtype)
    return out
```

```python
from contextlib import ExitStack

import numpy as np

import concourse.bass as bass
from concourse import mybir

F32 = mybir.dt.float32
F32R = mybir.dt.float32r
BF16 = mybir.dt.bfloat16
I32 = mybir.dt.int32
ALU = mybir.AluOpType
ACT = mybir.ActivationFunctionType
AX = mybir.AxisListType.X

P = 128
NB, S, D = 4, 512, 512
ST = S // P
KC = D // P
H = 32
QL, KVL, DN, DR, DV = 192, 64, 128, 64, 128
HD = KVL + DR
HALF = DR // 2
NE, R = 4, 8
NZ = NE * R
EPS_LN = 1e-5
EPS_PRIOR = 1e-12
LORA_SCALE = 16.0 / 8.0
SCORE_SCALE = float(np.float32(1.0) / np.sqrt(np.float32(DN + DR)))
MASKED = -1e30
PAIRS = H // 2
OH = D // 2
W0 = OH + NZ + NE
WB = W0 + OH
DC = QL + KVL + DR

UNITS = 5
BODY_PAIRS = 4
BODY = UNITS * BODY_PAIRS
BODIES = PAIRS // BODY_PAIRS
MEMBERS = (
    ((0, 3, 0),),
    ((1, 3, 0),),
    ((0, 2, 0), (0, 0, 384)),
    ((1, 2, 0), (1, 0, 384)),
    ((0, 1, 0), (1, 1, 256)),
)
RING = 4
T_LAG = 3
PV_SLOT = {1: 0, 3: 1, 4: 2}
PV_GROUP = (0, 0, 1, 1, 2)
OUT_SLOT = {0: 0, 1: 1, 2: 2, 4: 3}
TAIL = UNITS + 1
ACT_BANKS = (0, 2, 4)
ACT_COPIES = (1, 1, 2, 2, 3)
DVE_COPIES = (0, 1, 1, 2, 2)


_INS = ["L0_attn_hidden_states", "L0_attn_w_q_down", "L0_attn_w_q_up_nope", "L0_attn_w_q_up_rope",
        "L0_attn_w_kv_down", "L0_attn_w_k_rope", "L0_attn_w_uk", "L0_attn_w_uv", "L0_attn_w_out",
        "L0_ffn_W_base", "L0_ffn_b_base", "L0_ffn_lora_A", "L0_ffn_lora_B", "L0_ffn_router_W",
        "L0_ffn_router_b", "L0_ffn_domain_prior", "L0_ffn_active"]


def rope_tables():
    f = np.float32
    freqs = f(1.0) / f(10000.0) ** (np.arange(0, DR, 2, dtype=f) / f(DR))
    wavelengths = f(2.0 * np.pi) / freqs
    ramp = np.clip((wavelengths / f(4096.0) - f(1.0)) / f(32.0 - 1.0), f(0.0), f(1.0))
    inv_freq = freqs / (f(1.0) - ramp + ramp * f(40.0))
    angle = np.arange(S, dtype=f)[:, None] * inv_freq[None, :]
    cos = np.cos(angle).astype(f).reshape(ST, P, HALF).transpose(1, 0, 2)
    sin = np.sin(angle).astype(f).reshape(ST, P, HALF).transpose(1, 0, 2)
    return np.ascontiguousarray(cos), np.ascontiguousarray(np.stack([sin, -sin], axis=2))


def build(nc, hidden, w_q_down, w_q_up_nope, w_q_up_rope, w_kv_down, w_k_rope, w_uk, w_uv, w_out,
          W_base, b_base, lora_A, lora_B, router_W, router_b, domain_prior, active,
          rope_cos, rope_sin, out):
    with ExitStack() as ctx:
        def sem(name):
            return ctx.enter_context(nc.semaphore(name))

        sbuf_start = (nc.sbuf_base + 31) // 32 * 32
        sbuf_end = nc.sbuf_usable_end
        cursor = [sbuf_start]

        def place(name, shape, dt, at=None):
            size = int(np.prod(shape[1:])) * mybir.dt.size(dt)
            size = (size + 31) // 32 * 32
            where = cursor if at is None else at
            t = nc.alloc_sbuf_tensor_at(name, list(shape), dt, offset=where[0])
            where[0] += size
            assert where[0] <= sbuf_end, (name, where[0] - sbuf_end)
            return t

        wb_hi = place("wb_hi", [P, KC, WB], F32R)
        wb_lo = place("wb_lo", [P, KC, WB], F32R)
        lora_up = place("lora_up", [P, D], F32R)
        wd_hi = place("wd_hi", [P, KC, DC], F32R)
        wd_lo = place("wd_lo", [P, KC, DC], F32R)
        wq1_hi = place("wq1_hi", [P, H, HD], F32R)
        wq1_lo = place("wq1_lo", [P, H, HD], F32R)
        wq2 = place("wq2", [P, H, HD], F32R)
        x_sb = place("x_sb", [P, ST, D], F32)
        cq_hi = place("cq_hi", [P, 2, S], F32R)
        cq_lo = place("cq_lo", [P, 2, S], F32R)
        kT_hi = place("kT_hi", [P, S], F32R)
        kT_lo = place("kT_lo", [P, S], F32R)
        ckv = place("ckv", [P, ST, KVL], F32)
        cos_sb = place("cos_sb", [P, ST, HALF], F32)
        sin_sb = place("sin_sb", [P, ST, 2, HALF], F32)
        ident = place("ident", [P, P], F32)
        ident_bf = place("ident_bf", [P, P], BF16)
        causal = place("causal", [P, P], BF16)
        small = place("small", [P, 56], F32)

        def columns(at, n):
            return small[:, at:at + n]

        prior_row = columns(9, 4)
        logit, neg_logit_max, logit_exp, logit_sum = columns(13, 4), columns(17, 1), columns(18, 4), columns(22, 1)
        inv_logit_sum, alpha = columns(23, 1), columns(24, 4)
        neg_max = columns(28, 2 * RING).rearrange("p (r m) -> p r m", m=2)
        row_sum = columns(36, 2 * RING).rearrange("p (r m) -> p r m", m=2)
        inv_sum = columns(44, 2 * RING).rearrange("p (r m) -> p r m", m=2)
        ones, minus_half = columns(52, 2), columns(54, 2)
        region_a = [cursor[0]]
        wo_hi = place("wo_hi", [P, PAIRS, D], F32R)
        wo_lo = place("wo_lo", [P, PAIRS, D], F32R)
        region_b0 = cursor[0]

        nope_a = [place(f"nope_a{i}", [P, 4, DN], F32, region_a) for i in range(2)]
        nope_b = [place(f"nope_b{i}", [64, 4, DN], F32, region_a) for i in range(2)]
        nopeT_a = place("nopeT_a", [P, 4, P], F32, region_a)
        nopeT_b = place("nopeT_b", [P, 4, 2, 64], F32, region_a)
        uk_sb = place("uk_sb", [P, H, KVL], F32, region_a)
        rope_a = place("rope_a", [P, H, DR], F32, region_a)
        rope_bb = place("rope_bb", [P, H, DR], F32, region_a)
        rb = [region_b0]
        wbase_nat = place("wbase_nat", [P, KC, D], F32, rb)
        lora_nat = place("lora_nat", [NZ + NE, D], F32, rb)
        up_nat = place("up_nat", [P, KC, P], F32, rb)
        up_b = place("up_b", [P, KC, NE, R], F32, rb)
        down_nat = place("down_nat", [P, KC, DC], F32, rb)
        uv_nat = [place(f"uv_nat{i}", [P, 4, KVL], F32, rb) for i in range(2)]
        wout_nat = [place(f"wout_nat{i}", [P, 4, D], F32, rb) for i in range(2)]
        active_sb = place("active_sb", [1, NE], I32, rb)
        router_row = place("router_row", [P, NE], F32, rb)
        prior_raw = place("prior_raw", [P, NE], F32, rb)
        bias_nat = place("bias_nat", [P, KC], F32, rb)
        rb = [region_b0]
        xn = [place(f"xn{i}", [P, D], F32, rb) for i in range(2)]
        xT_hi = [place(f"xT_hi{i}", [P, KC, P], F32R, rb) for i in range(2)]
        xT_lo = [place(f"xT_lo{i}", [P, KC, P], F32R, rb) for i in range(2)]
        za = [place(f"za{i}", [P, 2, 64], F32, rb) for i in range(2)]
        zT_hi = [place(f"zT_hi{i}", [P, P], F32R, rb) for i in range(2)]
        zT_lo = [place(f"zT_lo{i}", [P, P], F32R, rb) for i in range(2)]
        down = [place(f"down{i}", [P, 3, P], F32, rb) for i in range(2)]
        stats = place("stats", [P, 2, 6], F32, rb)
        mean, gap, devs, var_eps, rough, newton, rstd = (
            place(n, [P, 2], F32, rb) for n in
            ("mean", "gap", "devs", "var_eps", "rough", "newton", "rstd"))
        k_sin = place("k_sin", [P, 2, HALF], F32, rb)
        rb = [region_b0]
        q_tok = place("q_tok", [P, 2, 2, HD], F32, rb)
        q_sin = place("q_sin", [P, 4, 2, HALF], F32, rb)
        qT_hi = [place(f"qT_hi{i}", [P, 2, S], F32R, rb) for i in range(2)]
        qT_lo = [place(f"qT_lo{i}", [P, 2, S], F32R, rb) for i in range(2)]
        prob = [place(f"prob{i}", [P, S], F32, rb) for i in range(RING)]
        probT = [place(f"probT{i}", [P, S], F32, rb) for i in range(RING)]
        oT_hi = [place(f"oT_hi{i}", [P, S], F32R, rb) for i in range(2)]
        oT_lo = [place(f"oT_lo{i}", [P, S], F32R, rb) for i in range(2)]

        Y = [ctx.enter_context(nc.psum_tensor(f"Y{i}", [P, 2, 512], F32)) for i in range(2)]
        X = [ctx.enter_context(nc.psum_tensor(f"X{i}", [P, 512], F32)) for i in range(2)]
        Z = [ctx.enter_context(nc.psum_tensor(f"Z{i}", [P, 512], F32)) for i in range(2)]
        score_ps, probT_ps = X, Z
        o_ps, out_ps, q_ps, qT_ps = Y[0][:, 0, :], Y[0][:, 1, :], Y[1][:, 0, :], Y[1][:, 1, :]

        def f32(t):
            return t.bitcast(F32)

        active_in, x_in = sem("active_in"), [sem(f"x_in{t}") for t in range(ST)]
        tables_in, ffn_in, gather_in = sem("tables_in"), sem("ffn_in"), sem("gather_in")
        down_in, qside_in = sem("down_in"), sem("qside_in")
        nope_in = [sem(f"nope_in{i}") for i in range(2)]
        out_in = [sem(f"out_in{i}") for i in range(2)]
        ident_set, masks_set, up_zeroed = sem("ident_set"), sem("masks_set"), sem("up_zeroed")
        up_filled = sem("up_filled")
        ffnT_ps, ffn_hi, ffn_lo = sem("ffnT_ps"), sem("ffn_hi"), sem("ffn_lo")
        upT_ps, up_hi, up_lo = sem("upT_ps"), sem("up_hi"), sem("up_lo")
        prior_eps, prior_ln, prior_done = sem("prior_eps"), sem("prior_ln"), sem("prior_done")
        down_hi_set, rope_hi_set, prep_dve = sem("down_hi_set"), sem("rope_hi_set"), sem("prep_dve")
        nopeT_ps, nopeTa_set, nopeTb_set = sem("nopeT_ps"), sem("nopeTa_set"), sem("nopeTb_set")
        fold_ps, fold_hi, fold_lo = sem("fold_ps"), sem("fold_hi"), sem("fold_lo")
        outw_ps, outw_hi, outw_lo = sem("outw_ps"), sem("outw_hi"), sem("outw_lo")

        G4 = H // 4
        GATHERED = 5 * NE + 1

        def loop(eng, start, end):
            return nc.Fori(start, end, engines=(eng.engine,), hint_back_edge=True)

        def rounds(eng, n, body):
            body(0)
            with loop(eng, 1, n) as i:
                body(i)

        def first(i):
            return isinstance(i, int) and i == 0

        with nc.Block() as block:
            @block.sync
            def _(sp):
                sp.dma_start(active_sb[:], active.unsqueeze(0)).then_inc(active_in, 16)
                for t in range(ST):
                    sp.dma_start(x_sb[:, t, :], hidden[0, t * P:(t + 1) * P, :]).then_inc(x_in[t], 16)
                sp.dma_start(wbase_nat[:], W_base.rearrange("(c p) h -> p c h", p=P)).then_inc(ffn_in, 16)
                sp.dma_start(bias_nat[:], b_base.rearrange("(c p) -> p c", p=P),
                             allow_slow_non_contiguous=True).then_inc(gather_in, 16)
                sp.wait_ge(active_in, 16)
                for e in range(NE):
                    a = sp.value_load(active_sb[0:1, e:e + 1], min_val=0, max_val=lora_A.shape[0] - 1)
                    sp.dma_start(lora_nat[e * R:(e + 1) * R, :],
                                 lora_A[bass.ds(a, 1), :, :].rearrange("e r h -> (e r) h")).then_inc(gather_in, 16)
                    sp.dma_start(lora_nat[NZ + e:NZ + e + 1, :], router_W[bass.ds(a, 1), :]).then_inc(gather_in, 16)
                    sp.dma_start(up_b[:, :, e, :],
                                 lora_B[bass.ds(a, 1), :, :].rearrange("e (c p) r -> p (e c) r", p=P)
                                 ).then_inc(gather_in, 16)
                    sp.dma_start(router_row[:, e:e + 1],
                                 router_b[bass.ds(a, 1)].unsqueeze(0).broadcast_to([P, 1])).then_inc(gather_in, 16)
                    sp.dma_start(prior_raw[:, e:e + 1],
                                 domain_prior[bass.ds(a, 1)].unsqueeze(0).broadcast_to([P, 1])).then_inc(gather_in, 16)
                def load_nope(i):
                    for j in range(2):
                        g = 2 * i + j
                        if not first(i):
                            sp.wait_ge(nopeT_ps, g - 1)
                        cols = bass.ds(g * (4 * DN), 4 * DN)
                        sp.dma_start(nope_a[j][:], w_q_up_nope[0:P, cols]
                                     .rearrange("q (h d) -> q h d", d=DN)).then_inc(nope_in[j], 16)
                        sp.dma_start(nope_b[j][:], w_q_up_nope[P:QL, cols]
                                     .rearrange("q (h d) -> q h d", d=DN)).then_inc(nope_in[j], 16)
                rounds(sp, G4 // 2, load_nope)

                def load_out(i):
                    for j in range(2):
                        g = 2 * i + j
                        if not first(i):
                            sp.wait_ge(outw_ps, g - 1)
                        rows = bass.ds(g * (4 * DV), 4 * DV)
                        sp.dma_start(uv_nat[j][:], w_uv[rows, :]
                                     .rearrange("(h d) r -> d h r", d=DV)).then_inc(out_in[j], 16)
                        sp.dma_start(wout_nat[j][:], w_out[rows, :]
                                     .rearrange("(h d) o -> d h o", d=DV)).then_inc(out_in[j], 16)
                rounds(sp, G4 // 2, load_out)

            @block.gpsimd
            def _(pool):
                pool.memset(ident[:], 0.0).then_inc(ident_set, 1)
                pool.memset(causal[:], 0.0).then_inc(ident_set, 1)
                pool.memset(ones, 1.0)
                pool.memset(minus_half, -0.5)
                pool.memset(up_nat[:], 0.0).then_inc(up_zeroed, 1)
                pool.wait_ge(ident_set, 2)
                pool.affine_select(out=ident[:], in_=ident[:], compare_op=ALU.not_equal, fill=1.0, base=0,
                                   pattern=[[-1, P]], channel_multiplier=1).then_inc(ident_set, 1)
                pool.affine_select(out=causal[:], in_=causal[:], compare_op=ALU.is_ge, fill=MASKED, base=0,
                                   pattern=[[-1, P]], channel_multiplier=1).then_inc(masks_set, 1)
                pool.wait_ge(ident_set, 3)
                pool.tensor_copy(ident_bf[:], ident[:]).then_inc(masks_set, 1)

            @block.scalar
            def _(act):
                act.dma_start(cos_sb[:], rope_cos).then_inc(tables_in, 16)
                act.dma_start(sin_sb[:], rope_sin).then_inc(tables_in, 16)
                act.dma_start(down_nat[:, :, 0:QL], w_q_down.rearrange("(c p) n -> p c n", p=P)).then_inc(down_in, 16)
                act.dma_start(down_nat[:, :, QL:QL + KVL],
                              w_kv_down.rearrange("(c p) n -> p c n", p=P)).then_inc(down_in, 16)
                act.dma_start(down_nat[:, :, QL + KVL:DC],
                              w_k_rope.rearrange("(c p) n -> p c n", p=P)).then_inc(down_in, 16)
                act.dma_start(uk_sb[:], w_uk.rearrange("(h d) r -> d h r", d=DN)).then_inc(qside_in, 16)
                act.dma_start(rope_a[:], w_q_up_rope[0:P, :].rearrange("q (h d) -> q h d", d=DR)).then_inc(qside_in, 16)
                for j in range(2):
                    act.dma_start(rope_bb[64 * j:64 * j + 64, :, :],
                                  w_q_up_rope[P:QL, :].rearrange("q (h d) -> q h d", d=DR)).then_inc(qside_in, 16)

                for c in range(KC):
                    act.wait_ge(ffnT_ps, c + 1)
                    nc.scalar.activation(wb_hi[:, c, 0:OH], Y[c % 2][:, 0, 0:OH], ACT.Copy)
                    nc.scalar.activation(wb_hi[:, c, W0:WB], Y[c % 2][:, 0, OH:D], ACT.Copy)
                    nc.scalar.activation(wb_hi[:, c, OH:W0], Y[c % 2][:, 1, 0:NZ + NE], ACT.Copy).then_inc(ffn_hi, 1)
                act.wait_ge(upT_ps, 1)
                nc.scalar.activation(lora_up[:], Z[0][:], ACT.Copy).then_inc(up_hi, 1)
                act.wait_ge(down_in, 48)
                nc.scalar.activation(wd_hi[:], down_nat[:], ACT.Copy).then_inc(down_hi_set, 1)
                act.wait_ge(qside_in, 64)
                nc.scalar.activation(wq1_hi[:, :, KVL:HD], rope_a[:], ACT.Copy)
                nc.scalar.activation(wq2[:, :, KVL:HD], rope_bb[:], ACT.Copy).then_inc(rope_hi_set, 1)
                def query_hi(g):
                    act.wait_ge(nopeT_ps, g + 1)
                    nc.scalar.activation(nopeT_a[:], X[0][:].rearrange("p (h q) -> p h q", h=4),
                                         ACT.Copy).then_inc(nopeTa_set, 1)
                    act.wait_ge(fold_ps, g + 1)
                    nc.scalar.activation(wq1_hi[:, bass.ds(4 * g, 4), 0:KVL],
                                         Z[1][:, 0:256].rearrange("p (h r) -> p h r", h=4), ACT.Copy)
                    nc.scalar.activation(wq2[:, bass.ds(4 * g, 4), 0:KVL],
                                         Z[1][:, 256:512].rearrange("p (h r) -> p h r", h=4),
                                         ACT.Copy).then_inc(fold_hi, 1)
                rounds(act, G4, query_hi)
                act.wait_ge(fold_lo, G4)

                def output_hi(i):
                    for j in range(2):
                        act.wait_ge(outw_ps, 2 * i + j + 1)
                        nc.scalar.activation(wo_hi[:, bass.ds(4 * i + 2 * j, 2), :], Y[j][:],
                                             ACT.Copy).then_inc(outw_hi, 1)
                rounds(act, G4 // 2, output_hi)
                act.wait_ge(prior_eps, 1)
                nc.scalar.activation(prior_row, prior_raw[:], ACT.Ln).then_inc(prior_ln, 1)

            @block.tensor
            def _(pe):
                pe.wait_ge(ident_set, 3)
                pe.wait_ge(ffn_in, 16)
                pe.wait_ge(gather_in, 16 * GATHERED)
                for c in range(KC):
                    if c >= 2:
                        pe.wait_ge(ffn_hi, c - 1)
                        pe.wait_ge(ffn_lo, c - 1)
                    for o in range(KC):
                        nc.tensor.transpose(Y[c % 2][:, 0, o * P:(o + 1) * P],
                                            wbase_nat[:, o, c * P:(c + 1) * P], ident[:])
                    nc.tensor.transpose(Y[c % 2][:, 1, 0:NZ + NE], lora_nat[:, c * P:(c + 1) * P],
                                        ident[0:NZ + NE, 0:NZ + NE]).then_inc(ffnT_ps, 1)
                pe.wait_ge(up_filled, 1)
                for o in range(KC):
                    last = nc.tensor.transpose(Z[0][:, o * P:(o + 1) * P], up_nat[:, o, :], ident[:])
                last.then_inc(upT_ps, 1)
                pe.wait_ge(qside_in, 64)

                def fold_query(i):
                    for j in range(2):
                        g = 2 * i + j
                        pe.wait_ge(nope_in[j], 32 * (i + 1))
                        for h in range(4):
                            nc.tensor.transpose(X[0][:, h * P:(h + 1) * P], nope_a[j][:, h, :], ident[:])
                        for h in range(4):
                            last = nc.tensor.transpose(X[1][:, h * 64:(h + 1) * 64], nope_b[j][:, h, :],
                                                       ident[0:64, 0:64])
                        last.then_inc(nopeT_ps, 1)
                        pe.wait_ge(nopeTa_set, g + 1)
                        pe.wait_ge(nopeTb_set, g + 1)
                        if not (first(i) and j == 0):
                            pe.wait_ge(fold_hi, g)
                            pe.wait_ge(fold_lo, g)
                        for h in range(4):
                            uk = uk_sb[:, bass.ds(4 * g + h, 1), :].rearrange("p a r -> p (a r)")
                            nc.tensor.matmul(Z[1][:, h * KVL:(h + 1) * KVL], nopeT_a[:, h, :], uk,
                                             start=True, stop=True)
                            last = nc.tensor.matmul(Z[1][:, 256 + h * KVL:256 + (h + 1) * KVL],
                                                    nopeT_b[:, h, :, :].rearrange("p a q -> p (a q)"), uk,
                                                    start=True, stop=True)
                        last.then_inc(fold_ps, 1)
                rounds(pe, G4 // 2, fold_query)

                def fold_output(i):
                    for j in range(2):
                        g = 2 * i + j
                        pe.wait_ge(out_in[j], 32 * (i + 1))
                        if not first(i):
                            pe.wait_ge(outw_hi, g - 1)
                            pe.wait_ge(outw_lo, g - 1)
                        for h in range(4):
                            c = 64 * (h % 2)
                            last = nc.tensor.matmul(Y[j][c:c + 64, h // 2, :], uv_nat[j][:, h, :],
                                                    wout_nat[j][:, h, :], start=True, stop=True,
                                                    tile_position=(0, c))
                        last.then_inc(outw_ps, 1)
                rounds(pe, G4 // 2, fold_output)

            @block.vector
            def _(dve):
                nc.vector.memset(f32(cq_lo[64:P, 1, :]), 0.0)
                dve.wait_ge(gather_in, 16 * GATHERED)
                dve.wait_ge(up_zeroed, 1)
                for j in range(2):
                    nc.vector.tensor_copy(up_nat[:, :, 64 * j:64 * j + NZ], up_b[:].rearrange("p c e r -> p c (e r)"))
                    last = nc.vector.tensor_copy(up_nat[:, :, 64 * j + NZ:64 * j + NZ + 1], bias_nat[:].unsqueeze(2))
                last.then_inc(up_filled, 1)
                nc.vector.tensor_scalar(prior_raw[:], prior_raw[:], EPS_PRIOR, None, ALU.add).then_inc(prior_eps, 1)
                for c in range(KC):
                    dve.wait_ge(ffn_hi, c + 1)
                    nc.vector.tensor_tensor(wb_lo[:, c, 0:OH], Y[c % 2][:, 0, 0:OH], f32(wb_hi[:, c, 0:OH]), ALU.subtract)
                    nc.vector.tensor_tensor(wb_lo[:, c, W0:WB], Y[c % 2][:, 0, OH:D], f32(wb_hi[:, c, W0:WB]),
                                            ALU.subtract)
                    nc.vector.tensor_tensor(wb_lo[:, c, OH:W0], Y[c % 2][:, 1, 0:NZ + NE], f32(wb_hi[:, c, OH:W0]),
                                            ALU.subtract).then_inc(ffn_lo, 1)
                dve.wait_ge(up_hi, 1)
                nc.vector.tensor_tensor(lora_up[64:P, :], Z[0][64:P, :], f32(lora_up[64:P, :]),
                                        ALU.subtract).then_inc(up_lo, 1)
                dve.wait_ge(down_hi_set, 1)
                nc.vector.tensor_tensor(wd_lo[:], down_nat[:], f32(wd_hi[:]), ALU.subtract)
                dve.wait_ge(rope_hi_set, 1)
                nc.vector.tensor_tensor(wq1_lo[:, :, KVL:HD], rope_a[:], f32(wq1_hi[:, :, KVL:HD]), ALU.subtract)
                nc.vector.tensor_tensor(wq2[64:P, :, KVL:HD], rope_bb[64:P, :, :], f32(wq2[64:P, :, KVL:HD]), ALU.subtract)

                def query_lo(g):
                    dve.wait_ge(nopeT_ps, g + 1)
                    nc.vector.tensor_copy(nopeT_b[:], X[1][:, 0:256].rearrange("p (h q) -> p h q", h=4).unsqueeze(2)
                                          .broadcast_to([P, 4, 2, 64])).then_inc(nopeTb_set, 1)
                    dve.wait_ge(fold_hi, g + 1)
                    heads = bass.ds(4 * g, 4)
                    nc.vector.tensor_tensor(wq1_lo[:, heads, 0:KVL],
                                            Z[1][:, 0:256].rearrange("p (h r) -> p h r", h=4),
                                            f32(wq1_hi[:, heads, 0:KVL]), ALU.subtract)
                    nc.vector.tensor_tensor(wq2[64:P, heads, 0:KVL],
                                            Z[1][64:P, 256:512].rearrange("p (h r) -> p h r", h=4),
                                            f32(wq2[64:P, heads, 0:KVL]), ALU.subtract).then_inc(fold_lo, 1)
                rounds(dve, G4, query_lo)

                def output_lo(i):
                    for j in range(2):
                        dve.wait_ge(outw_hi, 2 * i + j + 1)
                        pairs = bass.ds(4 * i + 2 * j, 2)
                        nc.vector.tensor_tensor(wo_lo[:, pairs, :], Y[j][:], f32(wo_hi[:, pairs, :]),
                                                ALU.subtract).then_inc(outw_lo, 1)
                rounds(dve, G4 // 2, output_lo)
                dve.wait_ge(prior_ln, 1)
                nc.vector.tensor_tensor(prior_row, prior_row, router_row[:], ALU.add).then_inc(prior_done, 1)

        stats_set, aggr_set, xn_set = sem("stats_set"), sem("aggr_set"), sem("xn_set")
        var_set, rough_set = sem("var_set"), sem("rough_set")
        newton_set, rstd_set = sem("newton_set"), sem("rstd_set")
        xT_ps, xT_hi_set, xT_lo_set = sem("xT_ps"), sem("xT_hi_set"), sem("xT_lo_set")
        ffn_ps, logit_set, max_set, logit_exp_set = sem("ffn_ps"), sem("logit_set"), sem("max_set"), sem("logit_exp_set")
        sum_inv_set, alpha_set, za_set = sem("sum_inv_set"), sem("alpha_set"), sem("za_set")
        zT_ps, zT_hi_set, zT_lo_set = sem("zT_ps"), sem("zT_hi_set"), sem("zT_lo_set")
        y_done, x_updated, z_static = sem("y_done"), sem("x_updated"), sem("z_static")
        x_out = [sem(f"x_out{t}") for t in range(ST)]
        down_ps, down_set, k_cos_set, k_rot_set = sem("down_ps"), sem("down_set"), sem("k_cos_set"), sem("k_rot_set")
        ckT_ps, ckT_hi, ckT_lo = sem("ckT_ps"), sem("ckT_hi"), sem("ckT_lo")
        scores_ps, neg_max_set, prob_set = sem("scores_ps"), sem("neg_max_set"), sem("prob_set")
        inv_sum_set, prob_scaled, probT_done = sem("inv_sum_set"), sem("prob_scaled"), sem("probT_done")
        probT_by_act, probT_by_dve = sem("probT_by_act"), sem("probT_by_dve")
        pv_done = sem("pv_done")
        oT_hi_set, oT_lo_set = sem("oT_hi_set"), sem("oT_lo_set")
        q_done, q_lat_set, q_rot_set, q_tok_set = sem("q_done"), sem("q_lat_set"), sem("q_rot_set"), sem("q_tok_set")
        qT_done, qT_hi_set, qT_lo_set = sem("qT_done"), sem("qT_hi_set"), sem("qT_lo_set")
        y_ps, y_added = sem("y_ps"), sem("y_added")

        def attention(b, slot_work, tail):
            for u in range(BODY):
                slot_work(0, u)
            with loop(b[1], 1, BODIES - 1) as g:
                for u in range(BODY):
                    slot_work(g, u)
            for u in range(BODY + tail):
                slot_work(BODIES - 1, u)

        def known(g, u, least):
            return not isinstance(g, int) or BODY * g + u >= least

        def within(g, u, most):
            return not isinstance(g, int) or BODY * g + u <= most

        def output_index(g, p):
            return (BODY_PAIRS // 2) * g + (p - 3) // 2

        def copy_probT(eng, do, b, g, v):
            pair = 16 * b + BODY_PAIRS * g + v // UNITS
            eng.wait_ge(probT_done, 80 * b + BODY * g + v + 1)
            if known(g, v, RING):
                w = v - RING
                eng.wait_ge(pv_done, 3 * (16 * b + BODY_PAIRS * g + w // UNITS) + PV_GROUP[w % UNITS] + 1)
            if eng.engine == nc.scalar.engine:
                do.activation(probT[v % RING][:], probT_ps[v % 2][:], ACT.Copy).then_inc(probT_by_act, 1)
            else:
                do.tensor_copy(probT[v % RING][:], probT_ps[v % 2][:]).then_inc(probT_by_dve, 1)

        SLOTS = UNITS * PAIRS
        LAST_PAIR = PAIRS - 1

        with nc.Block() as block:
            @block.sync
            def _(sp):
                def sequence(b, last):
                    for t in range(ST):
                        sp.wait_ge(x_updated, 8 * b + 4 + t + 1)
                        sp.dma_start(out[bass.ds(b, 1), t * P:(t + 1) * P, :].rearrange("a p d -> (a p) d"),
                                     x_sb[:, t, :]).then_inc(x_out[t], 16)
                    for t in range(ST):
                        sp.wait_ge(x_out[t], 16 * (b + 1))
                        if not last:
                            sp.dma_start(x_sb[:, t, :], hidden[bass.ds(b + 1, 1), t * P:(t + 1) * P, :]
                                         .rearrange("a p d -> (a p) d")).then_inc(x_in[t], 16)
                with loop(sp, 0, NB - 1) as b:
                    sequence(b, False)
                sequence(NB - 1, True)

            @block.gpsimd
            def _(pool):
                def z_constants(after=None):
                    if after is not None:
                        pool.wait_ge(y_added, after)
                    for i in range(2):
                        pad = ident[:, 0:2 * (63 - NZ)].rearrange("p (a z) -> p a z", a=2)
                        nc.gpsimd.tensor_tensor(za[i][:, :, NZ + 1:64], pad, pad, ALU.subtract)
                        nc.gpsimd.tensor_tensor(za[i][:, :, NZ], ones, ones, ALU.mult)
                        last = nc.gpsimd.tensor_tensor(zT_lo[i][:], ident[:], ident[:], ALU.subtract)
                    last.then_inc(z_static, 1)

                def rough_deviations(two):
                    pool.wait_ge(var_set, two + 1)
                    nc.gpsimd.tensor_tensor(rough[:], var_eps[:], minus_half, ALU.pow).then_inc(rough_set, 1)

                z_constants()
                with loop(pool, 0, NB) as b:
                    for two in range(4):
                        rough_deviations(6 * b + two)

                    def halves(n, half):
                        m = 32 * b + 2 * n + half
                        pool.wait_ge(q_rot_set, m + 1)
                        rot = q_tok[:, :, :, KVL:HD].rearrange("p t h (k f) -> p (t h) k f", k=2)
                        nc.gpsimd.tensor_tensor(rot, rot, q_sin[:, :, ::-1, :], ALU.add).then_inc(q_tok_set, 1)

                    halves(0, 0)
                    halves(0, 1)

                    def work(g, u):
                        if within(g, u, SLOTS - 1):
                            v = u
                            n = 80 * b + BODY * g + v
                            pool.wait_ge(inv_sum_set, n + 1)
                            for m, (_, i, c) in enumerate(MEMBERS[v % UNITS]):
                                w = (i + 1) * P
                                last = nc.gpsimd.tensor_tensor(prob[v % RING][:, c:c + w], prob[v % RING][:, c:c + w],
                                                               inv_sum[:, v % RING, m:m + 1].broadcast_to([P, w]),
                                                               ALU.mult)
                            last.then_inc(prob_scaled, 1)
                        if u % UNITS in (0, 2) and within(g, u, UNITS * LAST_PAIR - 1):
                            halves(BODY_PAIRS * g + u // UNITS + 1, (u % UNITS) // 2)
                    attention((b, pool), work, 0)
                    z_constants(32 * (b + 1))
                    for two in range(4, 6):
                        rough_deviations(6 * b + two)

            @block.tensor
            def _(pe):
                def transpose_x(m, t):
                    pe.wait_ge(xn_set, m + 1)
                    for c in range(KC):
                        last = nc.tensor.transpose(X[t % 2][:, c * P:(c + 1) * P],
                                                   xn[t % 2][:, c * P:(c + 1) * P], ident[:])
                    last.then_inc(xT_ps, 1)

                def ffn(b, which):
                    def main(t):
                        m, f = 12 * b + 8 * which + t, 8 * b + 4 * which + t
                        pe.wait_ge(xT_hi_set, m + 1)
                        pe.wait_ge(xT_lo_set, m + 1)
                        if t >= 2:
                            pe.wait_ge(x_updated, f - 1)
                        for c in range(KC):
                            for j, (xt, w) in enumerate(((xT_hi, wb_hi), (xT_hi, wb_lo), (xT_lo, wb_hi))):
                                for half, (a, z) in enumerate(((0, W0), (W0, WB))):
                                    last = nc.tensor.matmul(Y[t % 2][:, half, 0:z - a], xt[t % 2][:, c, :], w[:, c, a:z],
                                                            start=(c == 0 and j == 0), stop=(c == KC - 1 and j == 2))
                        last.then_inc(ffn_ps, 1)

                    def lora(t):
                        f = 8 * b + 4 * which + t
                        pe.wait_ge(za_set, f + 1)
                        nc.tensor.transpose(Z[t % 2][:, 0:P], za[t % 2][:].rearrange("p a z -> p (a z)"),
                                            ident[:]).then_inc(zT_ps, 1)
                        pe.wait_ge(zT_hi_set, f + 1)
                        pe.wait_ge(zT_lo_set, f + 1)
                        for j, zt in enumerate((zT_hi, zT_lo)):
                            for half in range(2):
                                last = nc.tensor.matmul(Y[t % 2][:, half, 0:OH], zt[t % 2][:],
                                                        lora_up[:, half * OH:(half + 1) * OH],
                                                        start=False, stop=(j == 1), skip_group_check=True)
                        last.then_inc(y_done, 1)

                    transpose_x(12 * b + 8 * which, 0)
                    for t in range(ST):
                        if t + 1 < ST:
                            transpose_x(12 * b + 8 * which + t + 1, t + 1)
                        main(t)
                        if t:
                            lora(t - 1)
                    lora(ST - 1)

                def down_projection(b):
                    def main(t):
                        m = 12 * b + 4 + t
                        pe.wait_ge(xT_hi_set, m + 1)
                        pe.wait_ge(xT_lo_set, m + 1)
                        if t >= 2:
                            pe.wait_ge(down_set, 4 * b + t - 1)
                            pe.wait_ge(k_cos_set, 4 * b + t - 1)
                        else:
                            pe.wait_ge(x_updated, 8 * b + t + 3)
                        for c in range(KC):
                            for j, (xt, w) in enumerate(((xT_hi, wd_hi), (xT_hi, wd_lo), (xT_lo, wd_hi))):
                                last = nc.tensor.matmul(Y[t % 2][:, 0, 0:DC], xt[t % 2][:, c, :], w[:, c, :],
                                                        start=(c == 0 and j == 0), stop=(c == KC - 1 and j == 2))
                        last.then_inc(down_ps, 1)

                    def transposes(t):
                        pe.wait_ge(down_set, 4 * b + t + 1)
                        pe.wait_ge(k_rot_set, 4 * b + t + 1)
                        if t >= 2:
                            pe.wait_ge(ckT_hi, 4 * b + t - 1)
                            pe.wait_ge(ckT_lo, 4 * b + t - 1)
                        for a in range(3):
                            last = nc.tensor.transpose(Z[t % 2][:, a * P:(a + 1) * P], down[t % 2][:, a, :], ident[:])
                        last.then_inc(ckT_ps, 1)

                    transpose_x(12 * b + 4, 0)
                    for t in range(ST):
                        if t + 1 < ST:
                            transpose_x(12 * b + 4 + t + 1, t + 1)
                        main(t)
                        if t:
                            transposes(t - 1)
                    transposes(ST - 1)

                def q_products(b, n, half, opening):
                    m = 32 * b + 2 * n + half
                    if not opening:
                        pe.wait_ge(q_lat_set, m)
                        pe.wait_ge(q_rot_set, m)
                    cols = [w[:, bass.ds(2 * n, 2), :].rearrange("p h r -> p (h r)") for w in (wq1_hi, wq1_lo, wq2)]
                    for tt in range(2):
                        rows = slice((2 * half + tt) * P, (2 * half + tt + 1) * P)
                        parts = ((cq_hi[:, 0, rows], cols[0]), (cq_hi[:, 0, rows], cols[1]), (cq_lo[:, 0, rows], cols[0]),
                                 (cq_hi[:, 1, rows], cols[2]), (cq_lo[:, 1, rows], cols[2]))
                        for j, (c, w) in enumerate(parts):
                            last = nc.tensor.matmul(q_ps[:, tt * 256:(tt + 1) * 256], c, w, start=(j == 0), stop=(j == 4))
                    last.then_inc(q_done, 1)

                def q_transposes(b, n, half, opening):
                    m = 32 * b + 2 * n + half
                    pe.wait_ge(q_tok_set, m + 1)
                    pe.wait_ge(q_lat_set, m + 1)
                    if not opening:
                        pe.wait_ge(qT_hi_set, m)
                        pe.wait_ge(qT_lo_set, m)
                    for h in range(2):
                        for tt in range(2):
                            last = nc.tensor.transpose(qT_ps[:, (2 * h + tt) * P:(2 * h + tt + 1) * P],
                                                       q_tok[:, tt, h, :], ident[:])
                    last.then_inc(qT_done, 1)

                def scores(b, g, u):
                    n = 80 * b + BODY * g + u
                    pair = 16 * b + BODY_PAIRS * g + u // UNITS
                    if u % UNITS == 0:
                        pe.wait_ge(qT_hi_set, 2 * pair + 2)
                        pe.wait_ge(qT_lo_set, 2 * pair + 2)
                    if known(g, u, 2):
                        pe.wait_ge(prob_set, n - 1)
                    par = (u // UNITS) % 2
                    for h, i, c in MEMBERS[u % UNITS]:
                        w, rows = (i + 1) * P, slice(i * P, (i + 1) * P)
                        s_out = score_ps[u % 2][:, c:c + w]
                        nc.tensor.matmul(s_out, qT_hi[par][:, h, rows], kT_hi[:, 0:w], start=True, stop=False)
                        nc.tensor.matmul(s_out, qT_hi[par][:, h, rows], kT_lo[:, 0:w], start=False, stop=False)
                        nc.tensor.matmul(score_ps[u % 2][:, c + w - P:c + w], ident_bf[:], causal[:],
                                         start=False, stop=False, skip_group_check=True)
                        last = nc.tensor.matmul(s_out, qT_lo[par][:, h, rows], kT_hi[:, 0:w], start=False, stop=True)
                    last.then_inc(scores_ps, 1)

                def bank_copies(b, g, v):
                    pair = 16 * b + BODY_PAIRS * g + v // UNITS
                    return 3 * pair + ACT_COPIES[v % UNITS], 2 * pair + DVE_COPIES[v % UNITS]

                def transpose_probs(b, g, v):
                    pe.wait_ge(prob_scaled, 80 * b + BODY * g + v + 1)
                    if known(g, v, 2):
                        by_act, by_dve = bank_copies(b, g, v - 2)
                        if (v - 2) % UNITS in ACT_BANKS:
                            pe.wait_ge(probT_by_act, by_act)
                        else:
                            pe.wait_ge(probT_by_dve, by_dve)
                    for h, i, c in MEMBERS[v % UNITS]:
                        for j in range(i + 1):
                            at = slice(c + j * P, c + (j + 1) * P)
                            last = nc.tensor.transpose(probT_ps[v % 2][:, at], prob[v % RING][:, at], ident[:])
                    last.then_inc(probT_done, 1)

                def pv(b, g, p, group):
                    pair = 16 * b + BODY_PAIRS * g + p
                    banks = [k for k in range(UNITS) if PV_GROUP[k] == group]
                    by_act, by_dve = bank_copies(b, g, UNITS * p + banks[-1])
                    pe.wait_ge(probT_by_act, by_act)
                    pe.wait_ge(probT_by_dve, by_dve)
                    if group == 0 and known(g, UNITS * p, UNITS):
                        pe.wait_ge(oT_hi_set, pair)
                        pe.wait_ge(oT_lo_set, pair)
                    where = {}
                    for k in banks:
                        for h, i, c in MEMBERS[k]:
                            where[i, h] = (probT[(UNITS * p + k) % RING], c)
                    for i in sorted({i for i, _ in where}, reverse=True):
                        for j in range(i + 1):
                            for h in range(2):
                                src, c = where[i, h]
                                last = nc.tensor.matmul(o_ps[64 * h:64 * h + 64, i * P:(i + 1) * P], ckv[:, j, :],
                                                        src[:, c + j * P:c + (j + 1) * P], start=(j == 0), stop=(j == i),
                                                        tile_position=(0, 64 * h))
                    last.then_inc(pv_done, 1)

                def output(b, g, two, t):
                    n = 32 * b + 4 * two + t
                    if t == 0:
                        pe.wait_ge(oT_hi_set, 16 * b + 2 * two + 2)
                        pe.wait_ge(oT_lo_set, 16 * b + 2 * two + 2)
                    if not (isinstance(two, int) and two == 0 and t == 0):
                        pe.wait_ge(y_added, n)
                    rows = slice(t * P, (t + 1) * P)
                    for k in range(2):
                        w_hi, w_lo = (w[:, bass.ds(2 * two + k, 1), :].rearrange("p a o -> p (a o)")
                                      for w in (wo_hi, wo_lo))
                        for j, (o, w) in enumerate(((oT_hi, w_hi), (oT_hi, w_lo), (oT_lo, w_hi))):
                            last = nc.tensor.matmul(out_ps, o[k][:, rows], w, start=(k == 0 and j == 0),
                                                    stop=(k == 1 and j == 2))
                    last.then_inc(y_ps, 1)

                with loop(pe, 0, NB) as b:
                    ffn(b, 0)
                    down_projection(b)
                    pe.wait_ge(ckT_hi, 4 * (b + 1))
                    pe.wait_ge(ckT_lo, 4 * (b + 1))
                    q_products(b, 0, 0, True)
                    q_transposes(b, 0, 0, True)
                    q_products(b, 0, 1, False)
                    q_transposes(b, 0, 1, False)

                    def work(g, u):
                        k, p = u % UNITS, u // UNITS
                        if within(g, u, SLOTS - 1):
                            scores(b, g, u)
                        if known(g, u, T_LAG) and within(g, u, SLOTS - 1 + T_LAG):
                            transpose_probs(b, g, u - T_LAG)
                        queries = within(g, u, UNITS * LAST_PAIR - 1)
                        n = BODY_PAIRS * g + p + 1
                        if k in (0, 2) and queries:
                            q_products(b, n, k // 2, False)
                        if k in PV_SLOT and known(g, u, UNITS):
                            pv(b, g, p - 1, PV_SLOT[k])
                        if p % 2 == 1 and k in OUT_SLOT and known(g, u, 3 * UNITS) and within(g, u, SLOTS - 1):
                            output(b, g, output_index(g, p), OUT_SLOT[k])
                        if k in (1, 3) and queries:
                            q_transposes(b, n, k // 2, False)
                    attention((b, pe), work, TAIL)
                    for t in range(ST):
                        output(b, BODIES - 1, PAIRS // 2 - 1, t)
                    ffn(b, 1)

            @block.scalar
            def _(act):
                def xT_high(m, t):
                    act.wait_ge(xT_ps, m + 1)
                    nc.scalar.activation(xT_hi[t % 2][:].rearrange("p c q -> p (c q)"), X[t % 2][:],
                                         ACT.Copy).then_inc(xT_hi_set, 1)

                def ffn(b, which):
                    m0, f0 = 12 * b + 8 * which, 8 * b + 4 * which
                    xT_high(m0, 0)
                    xT_high(m0 + 1, 1)
                    for t in range(ST):
                        act.wait_ge(max_set, f0 + t + 1)
                        nc.scalar.activation(logit_exp, logit, ACT.Exp, bias=neg_logit_max, scale=1.0,
                                             accum_out=logit_sum).then_inc(logit_exp_set, 1)
                        if t + 2 < ST:
                            xT_high(m0 + t + 2, t + 2)
                        act.wait_ge(zT_ps, f0 + t + 1)
                        nc.scalar.activation(zT_hi[t % 2][:], Z[t % 2][:, 0:P], ACT.Copy).then_inc(zT_hi_set, 1)

                def down_projection(b):
                    m0 = 12 * b + 4
                    xT_high(m0, 0)
                    xT_high(m0 + 1, 1)
                    for t in range(ST):
                        act.wait_ge(k_cos_set, 4 * b + t + 1)
                        if t >= 2:
                            act.wait_ge(ckT_ps, 4 * b + t - 1)
                        flat = down[t % 2][:].rearrange("p a r -> p (a r)")
                        nc.scalar.activation(flat[:, 0:QL], Y[t % 2][:, 0, 0:QL], ACT.Copy)
                        nc.scalar.activation(flat[:, QL:2 * P + KVL], Y[t % 2][:, 0, P:QL + KVL], ACT.Copy)
                        nc.scalar.activation(ckv[:, t, :], Y[t % 2][:, 0, QL:QL + KVL], ACT.Copy).then_inc(down_set, 1)
                        if t + 2 < ST:
                            xT_high(m0 + t + 2, t + 2)
                        rows = slice(t * P, (t + 1) * P)
                        act.wait_ge(ckT_ps, 4 * b + t + 1)
                        nc.scalar.activation(cq_hi[:, :, rows], Z[t % 2][:, 0:2 * P].rearrange("p (a q) -> p a q", a=2),
                                             ACT.Copy)
                        nc.scalar.activation(kT_hi[:, rows], Z[t % 2][:, 2 * P:3 * P], ACT.Copy,
                                             scale=SCORE_SCALE).then_inc(ckT_hi, 1)

                def q_latent(b, n, half):
                    m = 32 * b + 2 * n + half
                    act.wait_ge(q_rot_set, m + 1)
                    if not (isinstance(n, int) and n == 0 and half == 0):
                        act.wait_ge(qT_done, m)
                    nc.scalar.activation(q_tok[:, :, :, 0:KVL].rearrange("p t h r -> p (t h) r"),
                                         q_ps.rearrange("p (a r) -> p a r", r=HD)[:, :, 0:KVL],
                                         ACT.Copy).then_inc(q_lat_set, 1)

                def qT_high(b, n, half, par):
                    act.wait_ge(qT_done, 32 * b + 2 * n + half + 1)
                    nc.scalar.activation(qT_hi[par][:, :, half * 256:(half + 1) * 256],
                                         qT_ps.rearrange("p (h q) -> p h q", h=2), ACT.Copy).then_inc(qT_hi_set, 1)

                def oT_high(b, g, p):
                    act.wait_ge(pv_done, 3 * (16 * b + BODY_PAIRS * g + p - 1))
                    if known(g, UNITS * p, 4 * UNITS):
                        act.wait_ge(y_ps, 32 * b + ST * ((BODY_PAIRS // 2) * g + (p - 4) // 2) + ST)
                    nc.scalar.activation(oT_hi[p % 2][:], o_ps, ACT.Copy).then_inc(oT_hi_set, 1)

                with loop(act, 0, NB) as b:
                    ffn(b, 0)
                    down_projection(b)
                    for half in range(2):
                        q_latent(b, 0, half)
                        qT_high(b, 0, half, 0)

                    def work(g, u):
                        k, p = u % UNITS, u // UNITS
                        n1 = BODY_PAIRS * g + p + 1
                        queries = within(g, u, UNITS * LAST_PAIR - 1)
                        if k == 0 and known(g, u, 2 * UNITS):
                            oT_high(b, g, p)
                        if k in (2, 4) and queries:
                            qT_high(b, n1, k // 2 - 1, (p + 1) % 2)
                        if k in (1, 3) and queries:
                            q_latent(b, n1, k // 2)
                        if within(g, u, SLOTS - 1):
                            n = 80 * b + BODY * g + u
                            act.wait_ge(neg_max_set, n + 1)
                            if known(g, u, RING):
                                act.wait_ge(probT_done, n - RING + 1)
                            for m, (_, i, c) in enumerate(MEMBERS[k]):
                                w = (i + 1) * P
                                last = nc.scalar.activation(prob[u % RING][:, c:c + w], score_ps[u % 2][:, c:c + w],
                                                            ACT.Exp, bias=neg_max[:, u % RING, m:m + 1], scale=1.0,
                                                            accum_out=row_sum[:, u % RING, m:m + 1])
                            last.then_inc(prob_set, 1)
                        v = u - T_LAG
                        if known(g, u, T_LAG) and within(g, u, SLOTS - 1 + T_LAG) and v % UNITS in ACT_BANKS:
                            copy_probT(act, nc.scalar, b, g, v)
                    attention((b, act), work, TAIL)
                    ffn(b, 1)

            @block.vector
            def _(dve):
                def deviations(m, two, t, loaded=None):
                    for k in range(2):
                        if loaded is not None:
                            dve.wait_ge(x_in[t + k], loaded)
                        nc.vector.bn_stats(stats[:, k, :], x_sb[:, t + k, :]).then_inc(stats_set, 1)
                    mean_e, dev_e, mean_o, dev_o = stats[:, :, 1], stats[:, :, 2], stats[:, :, 4], stats[:, :, 5]
                    dve.wait_ge(stats_set, m + 2)
                    nc.vector.tensor_tensor(mean[:], mean_e, mean_o, ALU.add)
                    nc.vector.tensor_tensor(gap[:], mean_e, mean_o, ALU.subtract)
                    nc.vector.tensor_tensor(devs[:], dev_e, dev_o, ALU.add).then_inc(aggr_set, 1)
                    dve.wait_ge(aggr_set, 3 * two + 1)
                    nc.vector.tensor_scalar(mean[:], mean[:], 0.5, None, ALU.mult)
                    nc.vector.tensor_scalar(devs[:], devs[:], 1.0 / D, EPS_LN, ALU.mult, ALU.add)
                    nc.vector.tensor_tensor(gap[:], gap[:], gap[:], ALU.mult).then_inc(aggr_set, 1)
                    dve.wait_ge(aggr_set, 3 * two + 2)
                    nc.vector.tensor_scalar(gap[:], gap[:], 0.25, None, ALU.mult).then_inc(aggr_set, 1)
                    dve.wait_ge(aggr_set, 3 * two + 3)
                    nc.vector.tensor_tensor(var_eps[:], devs[:], gap[:], ALU.add).then_inc(var_set, 1)
                    dve.wait_ge(rough_set, two + 1)
                    nc.vector.tensor_tensor(newton[:], rough[:], rough[:], ALU.mult).then_inc(newton_set, 1)
                    dve.wait_ge(newton_set, 3 * two + 1)
                    nc.vector.tensor_tensor(newton[:], newton[:], var_eps[:], ALU.mult).then_inc(newton_set, 1)
                    dve.wait_ge(newton_set, 3 * two + 2)
                    nc.vector.tensor_scalar(newton[:], newton[:], -0.5, 1.5, ALU.mult, ALU.add).then_inc(newton_set, 1)
                    dve.wait_ge(newton_set, 3 * two + 3)
                    nc.vector.tensor_tensor(rstd[:], newton[:], rough[:], ALU.mult).then_inc(rstd_set, 1)
                    dve.wait_ge(rstd_set, two + 1)

                def norm(m, t):
                    if t >= 2:
                        dve.wait_ge(xT_ps, m - 1)
                    nc.vector.tensor_scalar(xn[t % 2][:], x_sb[:, t, :], mean[:, t % 2:t % 2 + 1], rstd[:, t % 2:t % 2 + 1],
                                            ALU.subtract, ALU.mult).then_inc(xn_set, 1)

                def xT_low(m, t):
                    dve.wait_ge(xT_hi_set, m + 1)
                    nc.vector.tensor_tensor(xT_lo[t % 2][:].rearrange("p c q -> p (c q)"), X[t % 2][:],
                                            f32(xT_hi[t % 2][:]).rearrange("p c q -> p (c q)"),
                                            ALU.subtract).then_inc(xT_lo_set, 1)

                def ffn(b, which):
                    m0, f0 = 12 * b + 8 * which, 8 * b + 4 * which
                    loaded = None if which else 16 * (b + 1)
                    deviations(m0, 6 * b + 4 * which, 0, loaded)
                    norm(m0, 0)
                    norm(m0 + 1, 1)
                    xT_low(m0, 0)
                    xT_low(m0 + 1, 1)
                    dve.wait_ge(z_static, b + 1 + which)
                    for t in range(ST):
                        f = f0 + t
                        dve.wait_ge(ffn_ps, f + 1)
                        nc.vector.tensor_tensor(logit, Y[t % 2][:, 0, OH + NZ:W0], prior_row,
                                                ALU.add).then_inc(logit_set, 1)
                        dve.wait_ge(logit_set, f + 1)
                        nc.vector.reduce_max(neg_logit_max, logit, AX, negate=True).then_inc(max_set, 1)
                        if t == 0:
                            deviations(m0 + 2, 6 * b + 4 * which + 1, 2, loaded)
                        if t + 2 < ST:
                            norm(m0 + t + 2, t + 2)
                        dve.wait_ge(logit_exp_set, f + 1)
                        nc.vector.reciprocal(inv_logit_sum, logit_sum).then_inc(sum_inv_set, 1)
                        dve.wait_ge(sum_inv_set, f + 1)
                        nc.vector.tensor_scalar(alpha, logit_exp, inv_logit_sum, LORA_SCALE,
                                                ALU.mult, ALU.mult).then_inc(alpha_set, 1)
                        dve.wait_ge(alpha_set, f + 1)
                        if t >= 2:
                            dve.wait_ge(zT_ps, f - 1)
                        gate = alpha.unsqueeze(2).broadcast_to([P, NE, R])
                        for half in range(2):
                            last = nc.vector.tensor_tensor(za[t % 2][:, half, 0:NZ].rearrange("p (e r) -> p e r", e=NE),
                                                           Y[t % 2][:, 0, OH:OH + NZ].rearrange("p (e r) -> p e r", e=NE),
                                                           gate, ALU.mult)
                        last.then_inc(za_set, 1)
                        if t + 2 < ST:
                            xT_low(m0 + t + 2, t + 2)
                        dve.wait_ge(zT_hi_set, f + 1)
                        nc.vector.tensor_tensor(zT_lo[t % 2][0:64, :], Z[t % 2][0:64, 0:P], f32(zT_hi[t % 2][0:64, :]),
                                                ALU.subtract).then_inc(zT_lo_set, 1)
                        dve.wait_ge(y_done, f + 1)
                        row = x_sb[:, t, :].rearrange("p (a o) -> p a o", a=2)
                        nc.vector.scalar_tensor_tensor(out=row, in0=Y[t % 2][:, :, 0:OH], scalar=0.5, in1=row,
                                                       op0=ALU.mult, op1=ALU.add).then_inc(x_updated, 1)

                def down_projection(b):
                    m0 = 12 * b + 4
                    dve.wait_ge(x_updated, 8 * b + 2)
                    deviations(m0, 6 * b + 2, 0)
                    norm(m0, 0)
                    norm(m0 + 1, 1)
                    xT_low(m0, 0)
                    xT_low(m0 + 1, 1)
                    for t in range(ST):
                        d = 4 * b + t
                        dve.wait_ge(down_ps, d + 1)
                        if t >= 2:
                            dve.wait_ge(ckT_ps, d - 1)
                        key = Y[t % 2][:, 0, QL + KVL:DC].rearrange("p (k f) -> p k f", k=2)
                        rot = down[t % 2][:, 2, KVL:HD].rearrange("p (k f) -> p k f", k=2)
                        nc.vector.tensor_tensor(rot, key, cos_sb[:, t, :].unsqueeze(1).broadcast_to([P, 2, HALF]), ALU.mult)
                        nc.vector.tensor_tensor(k_sin[:], key, sin_sb[:, t, :, :], ALU.mult).then_inc(k_cos_set, 1)
                        dve.wait_ge(k_cos_set, d + 1)
                        nc.vector.tensor_tensor(rot, rot, k_sin[:, ::-1, :], ALU.add).then_inc(k_rot_set, 1)
                        if t == 0:
                            dve.wait_ge(x_updated, 8 * b + 4)
                            deviations(m0 + 2, 6 * b + 3, 2)
                        if t + 2 < ST:
                            norm(m0 + t + 2, t + 2)
                            xT_low(m0 + t + 2, t + 2)
                        rows = slice(t * P, (t + 1) * P)
                        dve.wait_ge(ckT_hi, d + 1)
                        nc.vector.tensor_tensor(cq_lo[:, 0, rows], Z[t % 2][:, 0:P], f32(cq_hi[:, 0, rows]), ALU.subtract)
                        nc.vector.tensor_tensor(cq_lo[0:64, 1, rows], Z[t % 2][0:64, P:2 * P], f32(cq_hi[0:64, 1, rows]),
                                                ALU.subtract)
                        nc.vector.scalar_tensor_tensor(out=kT_lo[:, rows], in0=Z[t % 2][:, 2 * P:3 * P], scalar=SCORE_SCALE,
                                                       in1=f32(kT_hi[:, rows]), op0=ALU.mult,
                                                       op1=ALU.subtract).then_inc(ckT_lo, 1)

                def q_rotary(b, n, half):
                    m = 32 * b + 2 * n + half
                    dve.wait_ge(q_done, m + 1)
                    if not (isinstance(n, int) and n == 0 and half == 0):
                        dve.wait_ge(qT_done, m)
                    for tt in range(2):
                        t = 2 * half + tt
                        q = q_ps[:, tt * 256:(tt + 1) * 256].rearrange("p (h r) -> p h r", h=2)[:, :, KVL:HD] \
                            .rearrange("p h (k f) -> p h k f", k=2)
                        nc.vector.tensor_tensor(q_tok[:, tt, :, KVL:HD].rearrange("p h (k f) -> p h k f", k=2), q,
                                                cos_sb[:, t, :].unsqueeze(1).unsqueeze(1).broadcast_to([P, 2, 2, HALF]),
                                                ALU.mult)
                        last = nc.vector.tensor_tensor(q_sin[:, 2 * tt:2 * tt + 2, :, :], q,
                                                       sin_sb[:, t, :, :].unsqueeze(1).broadcast_to([P, 2, 2, HALF]),
                                                       ALU.mult)
                    last.then_inc(q_rot_set, 1)

                def qT_low(b, n, half, par):
                    dve.wait_ge(qT_hi_set, 32 * b + 2 * n + half + 1)
                    at = slice(half * 256, (half + 1) * 256)
                    nc.vector.tensor_tensor(qT_lo[par][:, :, at], qT_ps.rearrange("p (h q) -> p h q", h=2),
                                            f32(qT_hi[par][:, :, at]), ALU.subtract).then_inc(qT_lo_set, 1)

                def inverse_sums(b, g, v):
                    n = 80 * b + BODY * g + v
                    dve.wait_ge(prob_set, n + 1)
                    k = len(MEMBERS[v % UNITS])
                    nc.vector.reciprocal(inv_sum[:, v % RING, 0:k], row_sum[:, v % RING, 0:k]).then_inc(inv_sum_set, 1)

                def add_output(b, two, t):
                    dve.wait_ge(y_ps, 32 * b + 4 * two + t + 1)
                    nc.vector.tensor_tensor(x_sb[:, t, :], out_ps, x_sb[:, t, :], ALU.add).then_inc(y_added, 1)

                with loop(dve, 0, NB) as b:
                    ffn(b, 0)
                    down_projection(b)
                    for half in range(2):
                        q_rotary(b, 0, half)
                        qT_low(b, 0, half, 0)

                    def work(g, u):
                        k, p = u % UNITS, u // UNITS
                        n1 = BODY_PAIRS * g + p + 1
                        queries = within(g, u, UNITS * LAST_PAIR - 1)
                        if k in (2, 4) and queries:
                            qT_low(b, n1, k // 2 - 1, (p + 1) % 2)
                        if within(g, u, SLOTS - 1):
                            dve.wait_ge(scores_ps, 80 * b + BODY * g + u + 1)
                            for m, (_, i, c) in enumerate(MEMBERS[k]):
                                last = nc.vector.reduce_max(neg_max[:, u % RING, m:m + 1],
                                                            score_ps[u % 2][:, c:c + (i + 1) * P], AX, negate=True)
                            last.then_inc(neg_max_set, 1)
                        if k == 0 and known(g, u, 2 * UNITS):
                            dve.wait_ge(oT_hi_set, 16 * b + BODY_PAIRS * g + p - 1)
                            nc.vector.tensor_tensor(oT_lo[p % 2][:], o_ps, f32(oT_hi[p % 2][:]),
                                                    ALU.subtract).then_inc(oT_lo_set, 1)
                        v = u - T_LAG
                        if known(g, u, T_LAG) and within(g, u, SLOTS - 1 + T_LAG) and v % UNITS not in ACT_BANKS:
                            copy_probT(dve, nc.vector, b, g, v)
                        if within(g, u, SLOTS - 1):
                            inverse_sums(b, g, u)
                        if k in (0, 2) and queries:
                            q_rotary(b, n1, k // 2)
                        if p % 2 == 1 and k in OUT_SLOT and known(g, u, 3 * UNITS) and within(g, u, SLOTS - 1):
                            add_output(b, output_index(g, p), OUT_SLOT[k])
                    attention((b, dve), work, TAIL)
                    for t in range(ST):
                        add_output(b, PAIRS // 2 - 1, t)
                    ffn(b, 1)


def kernel(**inputs):
    import numpy as _np
    import concourse.bacc as _bacc
    from concourse import mybir as _mybir
    from concourse.bass_utils import run_bass_kernel_spmd as _run

    nc = _bacc.Bacc("TRN2", target_bir_lowering=False, num_devices=1)
    arrays, args = {}, []
    for name in _INS:
        a = _np.ascontiguousarray(inputs[name])
        arrays[f"in_{name}_dram"] = a
        args.append(nc.dram_tensor(f"in_{name}_dram", a.shape, _mybir.dt.from_np(a.dtype), kind="ExternalInput").ap())
    for name, a in zip(("rope_cos", "rope_sin"), rope_tables()):
        arrays[f"in_{name}_dram"] = a
        args.append(nc.dram_tensor(f"in_{name}_dram", a.shape, F32, kind="ExternalInput").ap())
    args.append(nc.dram_tensor("out_0_dram", (NB, S, D), F32, kind="ExternalOutput").ap())
    build(nc, *args)
    r = _run(nc, [arrays], core_ids=[0])
    return r.results[0]["out_0_dram"]
```

```python
from contextlib import ExitStack

import numpy as np

import concourse.bass as bass
from concourse import mybir

F32 = mybir.dt.float32
F32R = mybir.dt.float32r
BF16 = mybir.dt.bfloat16
I32 = mybir.dt.int32
ALU = mybir.AluOpType
ACT = mybir.ActivationFunctionType
AX = mybir.AxisListType.X

P = 128
NB, S, D = 4, 512, 512
ST = S // P
KC = D // P
H = 32
QL, KVL, DN, DR, DV = 192, 64, 128, 64, 128
HD = KVL + DR
HALF = DR // 2
NE, R = 4, 8
NZ = NE * R
EPS_LN = 1e-5
EPS_PRIOR = 1e-12
LORA_SCALE = 16.0 / 8.0
SCORE_SCALE = float(np.float32(1.0) / np.sqrt(np.float32(DN + DR)))
MASKED = -1e30
PAIRS = H // 2
STEPS = 3 * ST
FIRST, DOWN = ST, 2 * ST
OH = D // 2
W0 = OH + NZ + NE
WB = W0 + OH
DC = QL + KVL + DR

UNITS = 5
BODY_PAIRS = 4
BODY = UNITS * BODY_PAIRS
BODIES = PAIRS // BODY_PAIRS
MEMBERS = (
    ((0, 3, 0),),
    ((1, 3, 0),),
    ((0, 2, 0), (0, 0, 384)),
    ((1, 2, 0), (1, 0, 384)),
    ((0, 1, 0), (1, 1, 256)),
)
RING = 4
T_LAG = 3
PV_SLOT = {1: 0, 3: 1, 4: 2}
PV_GROUP = (0, 0, 1, 1, 2)
OUT_SLOT = {0: 0, 1: 1, 2: 2, 4: 3}
TAIL = UNITS + 1
ACT_BANKS = (0, 2, 4)
ACT_COPIES = (1, 1, 2, 2, 3)
DVE_COPIES = (0, 1, 1, 2, 2)


_INS = ["L0_attn_hidden_states", "L0_attn_w_q_down", "L0_attn_w_q_up_nope", "L0_attn_w_q_up_rope",
        "L0_attn_w_kv_down", "L0_attn_w_k_rope", "L0_attn_w_uk", "L0_attn_w_uv", "L0_attn_w_out",
        "L0_ffn_W_base", "L0_ffn_b_base", "L0_ffn_lora_A", "L0_ffn_lora_B", "L0_ffn_router_W",
        "L0_ffn_router_b", "L0_ffn_domain_prior", "L0_ffn_active"]


def rope_tables():
    f = np.float32
    freqs = f(1.0) / f(10000.0) ** (np.arange(0, DR, 2, dtype=f) / f(DR))
    wavelengths = f(2.0 * np.pi) / freqs
    ramp = np.clip((wavelengths / f(4096.0) - f(1.0)) / f(32.0 - 1.0), f(0.0), f(1.0))
    inv_freq = freqs / (f(1.0) - ramp + ramp * f(40.0))
    angle = np.arange(S, dtype=f)[:, None] * inv_freq[None, :]
    cos = np.cos(angle).astype(f).reshape(ST, P, HALF).transpose(1, 0, 2)
    sin = np.sin(angle).astype(f).reshape(ST, P, HALF).transpose(1, 0, 2)
    return np.ascontiguousarray(cos), np.ascontiguousarray(np.stack([sin, -sin], axis=2))


def build(nc, hidden, w_q_down, w_q_up_nope, w_q_up_rope, w_kv_down, w_k_rope, w_uk, w_uv, w_out,
          W_base, b_base, lora_A, lora_B, router_W, router_b, domain_prior, active,
          rope_cos, rope_sin, out):
    with ExitStack() as ctx:
        def sem(name):
            return ctx.enter_context(nc.semaphore(name))

        sbuf_start = (nc.sbuf_base + 31) // 32 * 32
        sbuf_end = nc.sbuf_usable_end
        cursor = [sbuf_start]

        def place(name, shape, dt, at=None):
            size = int(np.prod(shape[1:])) * mybir.dt.size(dt)
            size = (size + 31) // 32 * 32
            where = cursor if at is None else at
            t = nc.alloc_sbuf_tensor_at(name, list(shape), dt, offset=where[0])
            where[0] += size
            assert where[0] <= sbuf_end, (name, where[0] - sbuf_end)
            return t

        wb_hi = place("wb_hi", [P, KC, WB], F32R)
        wb_lo = place("wb_lo", [P, KC, WB], F32R)
        lora_up = place("lora_up", [P, D], F32R)
        wd_hi = place("wd_hi", [P, KC, DC], F32R)
        wd_lo = place("wd_lo", [P, KC, DC], F32R)
        wq1_hi = place("wq1_hi", [P, H, HD], F32R)
        wq1_lo = place("wq1_lo", [P, H, HD], F32R)
        wq2 = place("wq2", [P, H, HD], F32R)
        x_sb = place("x_sb", [P, ST, D], F32)
        cq_hi = place("cq_hi", [P, 2, S], F32R)
        cq_lo = place("cq_lo", [P, 2, S], F32R)
        kT_hi = place("kT_hi", [P, S], F32R)
        kT_lo = place("kT_lo", [P, S], F32R)
        ckv = place("ckv", [P, ST, KVL], F32)
        cos_sb = place("cos_sb", [P, ST, HALF], F32)
        sin_sb = place("sin_sb", [P, ST, 2, HALF], F32)
        ident = place("ident", [P, P], F32)
        ident_bf = place("ident_bf", [P, P], BF16)
        causal = place("causal", [P, P], BF16)
        small = place("small", [P, 56], F32)

        def columns(at, n):
            return small[:, at:at + n]

        prior_row = columns(9, 4)
        logit, neg_logit_max, logit_exp, logit_sum = columns(13, 4), columns(17, 1), columns(18, 4), columns(22, 1)
        inv_logit_sum, alpha = columns(23, 1), columns(24, 4)
        neg_max = columns(28, 2 * RING).rearrange("p (r m) -> p r m", m=2)
        row_sum = columns(36, 2 * RING).rearrange("p (r m) -> p r m", m=2)
        inv_sum = columns(44, 2 * RING).rearrange("p (r m) -> p r m", m=2)
        ones, eps, minus_half = columns(52, 2), columns(54, 1), columns(55, 1)
        region_a = [cursor[0]]
        wo_hi = place("wo_hi", [P, PAIRS, D], F32R)
        wo_lo = place("wo_lo", [P, PAIRS, D], F32R)
        region_b0 = cursor[0]

        nope_a = [place(f"nope_a{i}", [P, 4, DN], F32, region_a) for i in range(2)]
        nope_b = [place(f"nope_b{i}", [64, 4, DN], F32, region_a) for i in range(2)]
        nopeT_a = place("nopeT_a", [P, 4, P], F32, region_a)
        nopeT_b = place("nopeT_b", [P, 4, 2, 64], F32, region_a)
        uk_sb = place("uk_sb", [P, H, KVL], F32, region_a)
        rope_a = place("rope_a", [P, H, DR], F32, region_a)
        rope_bb = place("rope_bb", [P, H, DR], F32, region_a)
        rb = [region_b0]
        wbase_nat = place("wbase_nat", [P, KC, D], F32, rb)
        lora_nat = place("lora_nat", [NZ + NE, D], F32, rb)
        up_nat = place("up_nat", [P, KC, P], F32, rb)
        up_b = place("up_b", [P, KC, NE, R], F32, rb)
        down_nat = place("down_nat", [P, KC, DC], F32, rb)
        uv_nat = [place(f"uv_nat{i}", [P, 4, KVL], F32, rb) for i in range(2)]
        wout_nat = [place(f"wout_nat{i}", [P, 4, D], F32, rb) for i in range(2)]
        active_sb = place("active_sb", [1, NE], I32, rb)
        router_row = place("router_row", [P, NE], F32, rb)
        prior_raw = place("prior_raw", [P, NE], F32, rb)
        bias_nat = place("bias_nat", [P, KC], F32, rb)
        rb = [region_b0]
        xn = [place(f"xn{i}", [P, D], F32, rb) for i in range(2)]
        xT_hi = [place(f"xT_hi{i}", [P, KC, P], F32R, rb) for i in range(2)]
        xT_lo = [place(f"xT_lo{i}", [P, KC, P], F32R, rb) for i in range(2)]
        za = [place(f"za{i}", [P, 2, 64], F32, rb) for i in range(2)]
        zT_hi = [place(f"zT_hi{i}", [P, P], F32R, rb) for i in range(2)]
        zT_lo = [place(f"zT_lo{i}", [P, P], F32R, rb) for i in range(2)]
        down = [place(f"down{i}", [P, 3, P], F32, rb) for i in range(2)]
        k_sin = place("k_sin", [P, 2, HALF], F32, rb)
        rb = [region_b0]
        prob = [place(f"prob{i}", [P, S], F32, rb) for i in range(RING)]
        probT = [place(f"probT{i}", [P, S], F32, rb) for i in range(RING)]
        oT_hi = [place(f"oT_hi{i}", [P, S], F32R, rb) for i in range(2)]
        oT_lo = [place(f"oT_lo{i}", [P, S], F32R, rb) for i in range(2)]
        after_outputs = [rb[0]]
        q_tok = place("q_tok", [P, 2, 2, HD], F32, rb)
        q_sin = place("q_sin", [P, 4, 2, HALF], F32, rb)
        after_scores = [rb[0]]
        qT_hi = [place(f"qT_hi{i}", [P, 2, S], F32R, rb) for i in range(2)]
        qT_lo = [place(f"qT_lo{i}", [P, 2, S], F32R, rb) for i in range(2)]
        stats = place("stats", [P, ST, 6], F32, after_outputs)
        moments = place("moments", [P, STEPS, 2], F32, after_outputs)
        var_eps, rough, newton, rstd = (place(n, [P, STEPS], F32, after_outputs) for n in
                                        ("var_eps", "rough", "newton", "rstd"))
        assert after_outputs[0] <= after_scores[0]
        x_next = place("x_next", [P, ST, D], F32, after_scores)

        Y = [ctx.enter_context(nc.psum_tensor(f"Y{i}", [P, 2, 512], F32)) for i in range(2)]
        XZ = [ctx.enter_context(nc.psum_tensor(f"XZ{i}", [P, 2, 512], F32)) for i in range(2)]
        X, Z = [xz[:, 0, :] for xz in XZ], [xz[:, 1, :] for xz in XZ]
        score_ps, probT_ps = X, Z
        o_ps, out_ps, q_ps, qT_ps = Y[0][:, 0, :], Y[0][:, 1, :], Y[1][:, 0, :], Y[1][:, 1, :]

        last_out_ps = (Y[0][:, 1, :], Y[1][:, 0, :], Y[1][:, 1, :], Y[0][:, 0, :])

        def f32(t):
            return t.bitcast(F32)

        active_in, x_in = sem("active_in"), [sem(f"x_in{t}") for t in range(ST)]
        tables_in, ffn_in, gather_in = sem("tables_in"), sem("ffn_in"), sem("gather_in")
        down_in, qside_in = sem("down_in"), sem("qside_in")
        nope_in = [sem(f"nope_in{i}") for i in range(2)]
        out_in = [sem(f"out_in{i}") for i in range(2)]
        ident_set, masks_set, up_zeroed = sem("ident_set"), sem("masks_set"), sem("up_zeroed")
        up_filled = sem("up_filled")
        ffnT_ps, ffn_hi, ffn_lo = sem("ffnT_ps"), sem("ffn_hi"), sem("ffn_lo")
        upT_ps, up_hi, up_lo = sem("upT_ps"), sem("up_hi"), sem("up_lo")
        prior_eps, prior_ln, prior_done = sem("prior_eps"), sem("prior_ln"), sem("prior_done")
        down_hi_set, rope_hi_set, prep_dve = sem("down_hi_set"), sem("rope_hi_set"), sem("prep_dve")
        nopeT_ps, nopeTa_set, nopeTb_set = sem("nopeT_ps"), sem("nopeTa_set"), sem("nopeTb_set")
        fold_ps, fold_hi, fold_lo = sem("fold_ps"), sem("fold_hi"), sem("fold_lo")
        outw_ps, outw_hi, outw_lo = sem("outw_ps"), sem("outw_hi"), sem("outw_lo")

        G4 = H // 4
        GATHERED = 5 * NE + 1

        def loop(eng, start, end):
            return nc.Fori(start, end, engines=(eng.engine,), hint_back_edge=True)

        def rounds(eng, n, body):
            body(0)
            with loop(eng, 1, n) as i:
                body(i)

        def first(i):
            return isinstance(i, int) and i == 0

        with nc.Block() as block:
            @block.sync
            def _(sp):
                sp.dma_start(active_sb[:], active.unsqueeze(0)).then_inc(active_in, 16)
                for t in range(ST):
                    sp.dma_start(x_sb[:, t, :], hidden[0, t * P:(t + 1) * P, :]).then_inc(x_in[t], 16)
                sp.dma_start(wbase_nat[:], W_base.rearrange("(c p) h -> p c h", p=P)).then_inc(ffn_in, 16)
                sp.dma_start(bias_nat[:], b_base.rearrange("(c p) -> p c", p=P),
                             allow_slow_non_contiguous=True).then_inc(gather_in, 16)
                sp.wait_ge(active_in, 16)
                for e in range(NE):
                    a = sp.value_load(active_sb[0:1, e:e + 1], min_val=0, max_val=lora_A.shape[0] - 1)
                    sp.dma_start(lora_nat[e * R:(e + 1) * R, :],
                                 lora_A[bass.ds(a, 1), :, :].rearrange("e r h -> (e r) h")).then_inc(gather_in, 16)
                    sp.dma_start(lora_nat[NZ + e:NZ + e + 1, :], router_W[bass.ds(a, 1), :]).then_inc(gather_in, 16)
                    sp.dma_start(up_b[:, :, e, :],
                                 lora_B[bass.ds(a, 1), :, :].rearrange("e (c p) r -> p (e c) r", p=P)
                                 ).then_inc(gather_in, 16)
                    sp.dma_start(router_row[:, e:e + 1],
                                 router_b[bass.ds(a, 1)].unsqueeze(0).broadcast_to([P, 1])).then_inc(gather_in, 16)
                    sp.dma_start(prior_raw[:, e:e + 1],
                                 domain_prior[bass.ds(a, 1)].unsqueeze(0).broadcast_to([P, 1])).then_inc(gather_in, 16)
                def load_nope(i):
                    for j in range(2):
                        g = 2 * i + j
                        if not first(i):
                            sp.wait_ge(nopeT_ps, g - 1)
                        cols = bass.ds(g * (4 * DN), 4 * DN)
                        sp.dma_start(nope_a[j][:], w_q_up_nope[0:P, cols]
                                     .rearrange("q (h d) -> q h d", d=DN)).then_inc(nope_in[j], 16)
                        sp.dma_start(nope_b[j][:], w_q_up_nope[P:QL, cols]
                                     .rearrange("q (h d) -> q h d", d=DN)).then_inc(nope_in[j], 16)
                rounds(sp, G4 // 2, load_nope)

                def load_out(i):
                    for j in range(2):
                        g = 2 * i + j
                        if not first(i):
                            sp.wait_ge(outw_ps, g - 1)
                        rows = bass.ds(g * (4 * DV), 4 * DV)
                        sp.dma_start(uv_nat[j][:], w_uv[rows, :]
                                     .rearrange("(h d) r -> d h r", d=DV)).then_inc(out_in[j], 16)
                        sp.dma_start(wout_nat[j][:], w_out[rows, :]
                                     .rearrange("(h d) o -> d h o", d=DV)).then_inc(out_in[j], 16)
                rounds(sp, G4 // 2, load_out)

            @block.gpsimd
            def _(pool):
                pool.memset(ident[:], 0.0).then_inc(ident_set, 1)
                pool.memset(causal[:], 0.0).then_inc(ident_set, 1)
                pool.memset(ones, 1.0)
                pool.memset(eps, EPS_LN)
                pool.memset(minus_half, -0.5)
                pool.memset(up_nat[:], 0.0).then_inc(up_zeroed, 1)
                pool.wait_ge(ident_set, 2)
                pool.affine_select(out=ident[:], in_=ident[:], compare_op=ALU.not_equal, fill=1.0, base=0,
                                   pattern=[[-1, P]], channel_multiplier=1).then_inc(ident_set, 1)
                pool.affine_select(out=causal[:], in_=causal[:], compare_op=ALU.is_ge, fill=MASKED, base=0,
                                   pattern=[[-1, P]], channel_multiplier=1).then_inc(masks_set, 1)
                pool.wait_ge(ident_set, 3)
                pool.tensor_copy(ident_bf[:], ident[:]).then_inc(masks_set, 1)

            @block.scalar
            def _(act):
                act.dma_start(cos_sb[:], rope_cos).then_inc(tables_in, 16)
                act.dma_start(sin_sb[:], rope_sin).then_inc(tables_in, 16)
                act.dma_start(down_nat[:, :, 0:QL], w_q_down.rearrange("(c p) n -> p c n", p=P)).then_inc(down_in, 16)
                act.dma_start(down_nat[:, :, QL:QL + KVL],
                              w_kv_down.rearrange("(c p) n -> p c n", p=P)).then_inc(down_in, 16)
                act.dma_start(down_nat[:, :, QL + KVL:DC],
                              w_k_rope.rearrange("(c p) n -> p c n", p=P)).then_inc(down_in, 16)
                act.dma_start(uk_sb[:], w_uk.rearrange("(h d) r -> d h r", d=DN)).then_inc(qside_in, 16)
                act.dma_start(rope_a[:], w_q_up_rope[0:P, :].rearrange("q (h d) -> q h d", d=DR)).then_inc(qside_in, 16)
                for j in range(2):
                    act.dma_start(rope_bb[64 * j:64 * j + 64, :, :],
                                  w_q_up_rope[P:QL, :].rearrange("q (h d) -> q h d", d=DR)).then_inc(qside_in, 16)

                for c in range(KC):
                    act.wait_ge(ffnT_ps, c + 1)
                    nc.scalar.activation(wb_hi[:, c, 0:OH], Y[c % 2][:, 0, 0:OH], ACT.Copy)
                    nc.scalar.activation(wb_hi[:, c, W0:WB], Y[c % 2][:, 0, OH:D], ACT.Copy)
                    nc.scalar.activation(wb_hi[:, c, OH:W0], Y[c % 2][:, 1, 0:NZ + NE], ACT.Copy).then_inc(ffn_hi, 1)
                act.wait_ge(upT_ps, 1)
                nc.scalar.activation(lora_up[:], Z[0][:], ACT.Copy).then_inc(up_hi, 1)
                act.wait_ge(down_in, 48)
                nc.scalar.activation(wd_hi[:], down_nat[:], ACT.Copy).then_inc(down_hi_set, 1)
                act.wait_ge(qside_in, 64)
                nc.scalar.activation(wq1_hi[:, :, KVL:HD], rope_a[:], ACT.Copy)
                nc.scalar.activation(wq2[:, :, KVL:HD], rope_bb[:], ACT.Copy).then_inc(rope_hi_set, 1)
                def query_hi(g):
                    act.wait_ge(nopeT_ps, g + 1)
                    nc.scalar.activation(nopeT_a[:], X[0][:].rearrange("p (h q) -> p h q", h=4),
                                         ACT.Copy).then_inc(nopeTa_set, 1)
                    act.wait_ge(fold_ps, g + 1)
                    nc.scalar.activation(wq1_hi[:, bass.ds(4 * g, 4), 0:KVL],
                                         Z[1][:, 0:256].rearrange("p (h r) -> p h r", h=4), ACT.Copy)
                    nc.scalar.activation(wq2[:, bass.ds(4 * g, 4), 0:KVL],
                                         Z[1][:, 256:512].rearrange("p (h r) -> p h r", h=4),
                                         ACT.Copy).then_inc(fold_hi, 1)
                rounds(act, G4, query_hi)
                act.wait_ge(fold_lo, G4)

                def output_hi(i):
                    for j in range(2):
                        act.wait_ge(outw_ps, 2 * i + j + 1)
                        nc.scalar.activation(wo_hi[:, bass.ds(4 * i + 2 * j, 2), :], Y[j][:],
                                             ACT.Copy).then_inc(outw_hi, 1)
                rounds(act, G4 // 2, output_hi)
                act.wait_ge(prior_eps, 1)
                nc.scalar.activation(prior_row, prior_raw[:], ACT.Ln).then_inc(prior_ln, 1)

            @block.tensor
            def _(pe):
                pe.wait_ge(ident_set, 3)
                pe.wait_ge(ffn_in, 16)
                pe.wait_ge(gather_in, 16 * GATHERED)
                for c in range(KC):
                    if c >= 2:
                        pe.wait_ge(ffn_hi, c - 1)
                        pe.wait_ge(ffn_lo, c - 1)
                    for o in range(KC):
                        nc.tensor.transpose(Y[c % 2][:, 0, o * P:(o + 1) * P],
                                            wbase_nat[:, o, c * P:(c + 1) * P], ident[:])
                    nc.tensor.transpose(Y[c % 2][:, 1, 0:NZ + NE], lora_nat[:, c * P:(c + 1) * P],
                                        ident[0:NZ + NE, 0:NZ + NE]).then_inc(ffnT_ps, 1)
                pe.wait_ge(up_filled, 1)
                for o in range(KC):
                    last = nc.tensor.transpose(Z[0][:, o * P:(o + 1) * P], up_nat[:, o, :], ident[:])
                last.then_inc(upT_ps, 1)
                pe.wait_ge(qside_in, 64)

                def fold_query(i):
                    for j in range(2):
                        g = 2 * i + j
                        pe.wait_ge(nope_in[j], 32 * (i + 1))
                        for h in range(4):
                            nc.tensor.transpose(X[0][:, h * P:(h + 1) * P], nope_a[j][:, h, :], ident[:])
                        for h in range(4):
                            last = nc.tensor.transpose(X[1][:, h * 64:(h + 1) * 64], nope_b[j][:, h, :],
                                                       ident[0:64, 0:64])
                        last.then_inc(nopeT_ps, 1)
                        pe.wait_ge(nopeTa_set, g + 1)
                        pe.wait_ge(nopeTb_set, g + 1)
                        if not (first(i) and j == 0):
                            pe.wait_ge(fold_hi, g)
                            pe.wait_ge(fold_lo, g)
                        for h in range(4):
                            uk = uk_sb[:, bass.ds(4 * g + h, 1), :].rearrange("p a r -> p (a r)")
                            nc.tensor.matmul(Z[1][:, h * KVL:(h + 1) * KVL], nopeT_a[:, h, :], uk,
                                             start=True, stop=True)
                            last = nc.tensor.matmul(Z[1][:, 256 + h * KVL:256 + (h + 1) * KVL],
                                                    nopeT_b[:, h, :, :].rearrange("p a q -> p (a q)"), uk,
                                                    start=True, stop=True)
                        last.then_inc(fold_ps, 1)
                rounds(pe, G4 // 2, fold_query)

                def fold_output(i):
                    for j in range(2):
                        g = 2 * i + j
                        pe.wait_ge(out_in[j], 32 * (i + 1))
                        if not first(i):
                            pe.wait_ge(outw_hi, g - 1)
                            pe.wait_ge(outw_lo, g - 1)
                        for h in range(4):
                            c = 64 * (h % 2)
                            last = nc.tensor.matmul(Y[j][c:c + 64, h // 2, :], uv_nat[j][:, h, :],
                                                    wout_nat[j][:, h, :], start=True, stop=True,
                                                    tile_position=(0, c))
                        last.then_inc(outw_ps, 1)
                rounds(pe, G4 // 2, fold_output)

            @block.vector
            def _(dve):
                nc.vector.memset(f32(cq_lo[64:P, 1, :]), 0.0)
                dve.wait_ge(gather_in, 16 * GATHERED)
                dve.wait_ge(up_zeroed, 1)
                for j in range(2):
                    nc.vector.tensor_copy(up_nat[:, :, 64 * j:64 * j + NZ], up_b[:].rearrange("p c e r -> p c (e r)"))
                    last = nc.vector.tensor_copy(up_nat[:, :, 64 * j + NZ:64 * j + NZ + 1], bias_nat[:].unsqueeze(2))
                last.then_inc(up_filled, 1)
                nc.vector.tensor_scalar(prior_raw[:], prior_raw[:], EPS_PRIOR, None, ALU.add).then_inc(prior_eps, 1)
                for c in range(KC):
                    dve.wait_ge(ffn_hi, c + 1)
                    nc.vector.tensor_tensor(wb_lo[:, c, 0:OH], Y[c % 2][:, 0, 0:OH], f32(wb_hi[:, c, 0:OH]), ALU.subtract)
                    nc.vector.tensor_tensor(wb_lo[:, c, W0:WB], Y[c % 2][:, 0, OH:D], f32(wb_hi[:, c, W0:WB]),
                                            ALU.subtract)
                    nc.vector.tensor_tensor(wb_lo[:, c, OH:W0], Y[c % 2][:, 1, 0:NZ + NE], f32(wb_hi[:, c, OH:W0]),
                                            ALU.subtract).then_inc(ffn_lo, 1)
                dve.wait_ge(up_hi, 1)
                nc.vector.tensor_tensor(lora_up[64:P, :], Z[0][64:P, :], f32(lora_up[64:P, :]),
                                        ALU.subtract).then_inc(up_lo, 1)
                dve.wait_ge(down_hi_set, 1)
                nc.vector.tensor_tensor(wd_lo[:], down_nat[:], f32(wd_hi[:]), ALU.subtract)
                dve.wait_ge(rope_hi_set, 1)
                nc.vector.tensor_tensor(wq1_lo[:, :, KVL:HD], rope_a[:], f32(wq1_hi[:, :, KVL:HD]), ALU.subtract)
                nc.vector.tensor_tensor(wq2[64:P, :, KVL:HD], rope_bb[64:P, :, :], f32(wq2[64:P, :, KVL:HD]), ALU.subtract)

                def query_lo(g):
                    dve.wait_ge(nopeT_ps, g + 1)
                    nc.vector.tensor_copy(nopeT_b[:], X[1][:, 0:256].rearrange("p (h q) -> p h q", h=4).unsqueeze(2)
                                          .broadcast_to([P, 4, 2, 64])).then_inc(nopeTb_set, 1)
                    dve.wait_ge(fold_hi, g + 1)
                    heads = bass.ds(4 * g, 4)
                    nc.vector.tensor_tensor(wq1_lo[:, heads, 0:KVL],
                                            Z[1][:, 0:256].rearrange("p (h r) -> p h r", h=4),
                                            f32(wq1_hi[:, heads, 0:KVL]), ALU.subtract)
                    nc.vector.tensor_tensor(wq2[64:P, heads, 0:KVL],
                                            Z[1][64:P, 256:512].rearrange("p (h r) -> p h r", h=4),
                                            f32(wq2[64:P, heads, 0:KVL]), ALU.subtract).then_inc(fold_lo, 1)
                rounds(dve, G4, query_lo)

                def output_lo(i):
                    for j in range(2):
                        dve.wait_ge(outw_hi, 2 * i + j + 1)
                        pairs = bass.ds(4 * i + 2 * j, 2)
                        nc.vector.tensor_tensor(wo_lo[:, pairs, :], Y[j][:], f32(wo_hi[:, pairs, :]),
                                                ALU.subtract).then_inc(outw_lo, 1)
                rounds(dve, G4 // 2, output_lo)
                dve.wait_ge(prior_ln, 1)
                nc.vector.tensor_tensor(prior_row, prior_row, router_row[:], ALU.add).then_inc(prior_done, 1)

        stats_set, xn_set = sem("stats_set"), sem("xn_set")
        var_set, eps_added, rough_set = sem("var_set"), sem("eps_added"), sem("rough_set")
        newton_set, rstd_set = sem("newton_set"), sem("rstd_set")
        xT_ps, xT_hi_set, xT_lo_set = sem("xT_ps"), sem("xT_hi_set"), sem("xT_lo_set")
        z_ps, logit_set, max_set, logit_exp_set = sem("z_ps"), sem("logit_set"), sem("max_set"), sem("logit_exp_set")
        sum_inv_set, alpha_set, za_set = sem("sum_inv_set"), sem("alpha_set"), sem("za_set")
        zT_ps, zT_hi_set, zT_lo_set = sem("zT_ps"), sem("zT_hi_set"), sem("zT_lo_set")
        y_done, x_updated, z_static = sem("y_done"), sem("x_updated"), sem("z_static")
        x_out = [sem(f"x_out{t}") for t in range(ST)]
        down_ps, down_set, k_cos_set, k_rot_set = sem("down_ps"), sem("down_set"), sem("k_cos_set"), sem("k_rot_set")
        ckT_ps, ckT_hi, ckT_lo = sem("ckT_ps"), sem("ckT_hi"), sem("ckT_lo")
        scores_ps, neg_max_set, prob_set = sem("scores_ps"), sem("neg_max_set"), sem("prob_set")
        inv_sum_set, prob_scaled, probT_done = sem("inv_sum_set"), sem("prob_scaled"), sem("probT_done")
        probT_by_act, probT_by_dve = sem("probT_by_act"), sem("probT_by_dve")
        pv_done = sem("pv_done")
        oT_hi_set, oT_lo_set = sem("oT_hi_set"), sem("oT_lo_set")
        q_done, q_lat_set, q_rot_set, q_tok_set = sem("q_done"), sem("q_lat_set"), sem("q_rot_set"), sem("q_tok_set")
        qT_done, qT_hi_set, qT_lo_set = sem("qT_done"), sem("qT_hi_set"), sem("qT_lo_set")
        y_ps, y_added = sem("y_ps"), sem("y_added")

        GROUPS_0, GROUPS = 1 + ST, 3 + ST

        def banks_of(s):
            if s >= DOWN:
                return (Y[0], XZ[1])[s % 2]
            return (XZ[1], Y[1], Y[0])[s % 3]

        def attention(b, slot_work, tail):
            for u in range(BODY):
                slot_work(0, u)
            with loop(b[1], 1, BODIES - 1) as g:
                for u in range(BODY):
                    slot_work(g, u)
            for u in range(BODY + tail):
                slot_work(BODIES - 1, u)

        def known(g, u, least):
            return not isinstance(g, int) or BODY * g + u >= least

        def within(g, u, most):
            return not isinstance(g, int) or BODY * g + u <= most

        def output_index(g, p):
            return (BODY_PAIRS // 2) * g + (p - 3) // 2

        def copy_probT(eng, do, b, g, v):
            pair = 16 * b + BODY_PAIRS * g + v // UNITS
            eng.wait_ge(probT_done, 80 * b + BODY * g + v + 1)
            if known(g, v, RING):
                w = v - RING
                eng.wait_ge(pv_done, 3 * (16 * b + BODY_PAIRS * g + w // UNITS) + PV_GROUP[w % UNITS] + 1)
            if eng.engine == nc.scalar.engine:
                do.activation(probT[v % RING][:], probT_ps[v % 2][:], ACT.Copy).then_inc(probT_by_act, 1)
            else:
                do.tensor_copy(probT[v % RING][:], probT_ps[v % 2][:]).then_inc(probT_by_dve, 1)

        SLOTS = UNITS * PAIRS
        LAST_PAIR = PAIRS - 1

        with nc.Block() as block:
            @block.sync
            def _(sp):
                def sequence(b, last):
                    if not last:
                        sp.wait_ge(scores_ps, SLOTS * (b + 1))
                        for t in range(ST):
                            sp.dma_start(x_next[:, t, :], hidden[bass.ds(b + 1, 1), t * P:(t + 1) * P, :]
                                         .rearrange("a p d -> (a p) d")).then_inc(x_in[t], 16)
                    for t in range(ST):
                        sp.wait_ge(x_updated, 8 * b + 4 + t + 1)
                        sp.dma_start(out[bass.ds(b, 1), t * P:(t + 1) * P, :].rearrange("a p d -> (a p) d"),
                                     x_sb[:, t, :]).then_inc(x_out[t], 16)
                with loop(sp, 0, NB - 1) as b:
                    sequence(b, False)
                sequence(NB - 1, True)
                for t in range(ST):
                    sp.wait_ge(x_out[t], 16 * NB)

            @block.gpsimd
            def _(pool):
                def z_constants():
                    for i in range(2):
                        pad = ident[:, 0:2 * (63 - NZ)].rearrange("p (a z) -> p a z", a=2)
                        nc.gpsimd.tensor_tensor(za[i][:, :, NZ + 1:64], pad, pad, ALU.subtract)
                        nc.gpsimd.tensor_tensor(za[i][:, :, NZ], ones, ones, ALU.mult)
                        last = nc.gpsimd.tensor_tensor(zT_lo[i][:], ident[:], ident[:], ALU.subtract)
                    last.then_inc(z_static, 1)

                def rough_deviations(group, s, n):
                    pool.wait_ge(var_set, group + 1)
                    nc.gpsimd.tensor_tensor(var_eps[:, s:s + n], moments[:, s:s + n, 1],
                                            eps.broadcast_to([P, n]), ALU.add).then_inc(eps_added, 1)
                    pool.wait_ge(eps_added, group + 1)
                    nc.gpsimd.tensor_tensor(rough[:, s:s + n], var_eps[:, s:s + n],
                                            minus_half.broadcast_to([P, n]), ALU.pow).then_inc(rough_set, 1)

                def halves(b, n, half):
                    m = 32 * b + 2 * n + half
                    pool.wait_ge(q_rot_set, m + 1)
                    rot = q_tok[:, :, :, KVL:HD].rearrange("p t h (k f) -> p (t h) k f", k=2)
                    nc.gpsimd.tensor_tensor(rot, rot, q_sin[:, :, ::-1, :], ALU.add).then_inc(q_tok_set, 1)

                def steps(b, start, end):
                    group = GROUPS_0 + GROUPS * b
                    if end > FIRST:
                        rough_deviations(group if start == 0 else 0, FIRST, ST)
                    if start == 0:
                        pool.wait_ge(y_ps, 32 * b + 29)
                    z_constants()
                    if start == 0:
                        for i in range(2):
                            rough_deviations(group + (1 if end > FIRST else 0) + i, 2 * i, 2)
                    if end > DOWN:
                        for t in range(ST):
                            rough_deviations(group + 3 + t if start == 0 else 1 + t, DOWN + t, 1)
                        for half in range(2):
                            halves(b + 1, 0, half)

                def attend(b):
                    def work(g, u):
                        if within(g, u, SLOTS - 1):
                            n = 80 * b + BODY * g + u
                            pool.wait_ge(inv_sum_set, n + 1)
                            for m, (_, i, c) in enumerate(MEMBERS[u % UNITS]):
                                w = (i + 1) * P
                                last = nc.gpsimd.tensor_tensor(prob[u % RING][:, c:c + w], prob[u % RING][:, c:c + w],
                                                               inv_sum[:, u % RING, m:m + 1].broadcast_to([P, w]),
                                                               ALU.mult)
                            last.then_inc(prob_scaled, 1)
                        if u % UNITS in (0, 2) and within(g, u, UNITS * LAST_PAIR - 1):
                            halves(b, BODY_PAIRS * g + u // UNITS + 1, (u % UNITS) // 2)
                    attention((b, pool), work, 0)

                steps(-1, FIRST, STEPS)
                with loop(pool, 0, NB - 1) as b:
                    attend(b)
                    steps(b, 0, STEPS)
                attend(NB - 1)
                steps(NB - 1, 0, FIRST)

            @block.tensor
            def _(pe):
                def transpose_x(b, s):
                    pe.wait_ge(xn_set, 12 * b + 8 + s + 1)
                    for c in range(KC):
                        last = nc.tensor.transpose(X[0][:, c * P:(c + 1) * P],
                                                   xn[s % 2][:, c * P:(c + 1) * P], ident[:])
                    last.then_inc(xT_ps, 1)

                def wait_for_products(b, s, start):
                    m, updated, down = 12 * b + 8 + s, 8 * b + 4, 4 * (b + 1)
                    if start == 0 and s in (1, 2):
                        pe.wait_ge(y_added, 32 * b + 30 + s)
                    elif start + 3 <= s < DOWN + 2:
                        pe.wait_ge(x_updated, updated + s - 2)
                    elif s >= DOWN + 2:
                        pe.wait_ge(ckT_hi, down + s - DOWN - 1)
                        pe.wait_ge(ckT_lo, down + s - DOWN - 1)
                    pe.wait_ge(xT_hi_set, m + 1)
                    pe.wait_ge(xT_lo_set, m + 1)

                def ffn_products(s, half):
                    a, z = ((0, W0), (W0, WB))[half]
                    for c in range(KC):
                        for j, (xt, w) in enumerate(((xT_hi, wb_hi), (xT_hi, wb_lo), (xT_lo, wb_hi))):
                            last = nc.tensor.matmul(banks_of(s)[:, half, 0:z - a], xt[s % 2][:, c, :], w[:, c, a:z],
                                                    start=(c == 0 and j == 0), stop=(c == KC - 1 and j == 2))
                    if half == 0:
                        last.then_inc(z_ps, 1)

                def down_products(s, half):
                    for c in (2 * half, 2 * half + 1):
                        for j, (xt, w) in enumerate(((xT_hi, wd_hi), (xT_hi, wd_lo), (xT_lo, wd_hi))):
                            last = nc.tensor.matmul(banks_of(s)[:, 0, 0:DC], xt[s % 2][:, c, :], w[:, c, :],
                                                    start=(c == 0 and j == 0), stop=(c == KC - 1 and j == 2))
                    if half:
                        last.then_inc(down_ps, 1)

                def transpose_z(b, s):
                    pe.wait_ge(za_set, 8 * b + 4 + s + 1)
                    nc.tensor.transpose(Z[0][:, 0:P], za[s % 2][:].rearrange("p a z -> p (a z)"),
                                        ident[:]).then_inc(zT_ps, 1)

                def lora(b, s):
                    f = 8 * b + 4 + s
                    pe.wait_ge(zT_hi_set, f + 1)
                    pe.wait_ge(zT_lo_set, f + 1)
                    for j, zt in enumerate((zT_hi, zT_lo)):
                        for half in range(2):
                            last = nc.tensor.matmul(banks_of(s)[:, half, 0:OH], zt[s % 2][:],
                                                    lora_up[:, half * OH:(half + 1) * OH],
                                                    start=False, stop=(j == 1), skip_group_check=True)
                    last.then_inc(y_done, 1)

                def transpose_down(b, s):
                    d = 4 * (b + 1) + s - DOWN
                    pe.wait_ge(down_set, d + 1)
                    pe.wait_ge(k_rot_set, d + 1)
                    for a in range(3):
                        last = nc.tensor.transpose(banks_of(s)[:, 1, a * P:(a + 1) * P], down[s % 2][:, a, :], ident[:])
                    last.then_inc(ckT_ps, 1)

                def steps(b, start, end):
                    transpose_x(b, start)
                    for s in range(start, end):
                        products = ffn_products if s < DOWN else down_products
                        wait_for_products(b, s, start)
                        products(s, 0)
                        if s > start:
                            (transpose_z if s <= DOWN else transpose_down)(b, s - 1)
                        if s + 1 < end:
                            transpose_x(b, s + 1)
                        products(s, 1)
                        if start < s <= DOWN:
                            lora(b, s - 1)
                    if end == FIRST:
                        transpose_z(b, end - 1)
                        lora(b, end - 1)
                    else:
                        pe.wait_ge(x_updated, 8 * b + 4 + DOWN)
                        q_products(b + 1, 0, 0, True)
                        transpose_down(b, end - 1)
                        q_transposes(b + 1, 0, 0, True)
                        pe.wait_ge(ckT_hi, 4 * (b + 2))
                        pe.wait_ge(ckT_lo, 4 * (b + 2))
                        q_products(b + 1, 0, 1, False)
                        q_transposes(b + 1, 0, 1, False)

                def q_products(b, n, half, opening):
                    m = 32 * b + 2 * n + half
                    if not opening:
                        pe.wait_ge(q_lat_set, m)
                        pe.wait_ge(q_rot_set, m)
                    cols = [w[:, bass.ds(2 * n, 2), :].rearrange("p h r -> p (h r)") for w in (wq1_hi, wq1_lo, wq2)]
                    for tt in range(2):
                        rows = slice((2 * half + tt) * P, (2 * half + tt + 1) * P)
                        parts = ((cq_hi[:, 0, rows], cols[0]), (cq_hi[:, 0, rows], cols[1]), (cq_lo[:, 0, rows], cols[0]),
                                 (cq_hi[:, 1, rows], cols[2]), (cq_lo[:, 1, rows], cols[2]))
                        for j, (c, w) in enumerate(parts):
                            last = nc.tensor.matmul(q_ps[:, tt * 256:(tt + 1) * 256], c, w, start=(j == 0), stop=(j == 4))
                    last.then_inc(q_done, 1)

                def q_transposes(b, n, half, opening):
                    m = 32 * b + 2 * n + half
                    pe.wait_ge(q_tok_set, m + 1)
                    pe.wait_ge(q_lat_set, m + 1)
                    if not opening:
                        pe.wait_ge(qT_hi_set, m)
                        pe.wait_ge(qT_lo_set, m)
                    for h in range(2):
                        for tt in range(2):
                            last = nc.tensor.transpose(qT_ps[:, (2 * h + tt) * P:(2 * h + tt + 1) * P],
                                                       q_tok[:, tt, h, :], ident[:])
                    last.then_inc(qT_done, 1)

                def scores(b, g, u):
                    n = 80 * b + BODY * g + u
                    pair = 16 * b + BODY_PAIRS * g + u // UNITS
                    if u % UNITS == 0:
                        pe.wait_ge(qT_hi_set, 2 * pair + 2)
                        pe.wait_ge(qT_lo_set, 2 * pair + 2)
                    if known(g, u, 2):
                        pe.wait_ge(prob_set, n - 1)
                    par = (u // UNITS) % 2
                    for h, i, c in MEMBERS[u % UNITS]:
                        w, rows = (i + 1) * P, slice(i * P, (i + 1) * P)
                        s_out = score_ps[u % 2][:, c:c + w]
                        nc.tensor.matmul(s_out, qT_hi[par][:, h, rows], kT_hi[:, 0:w], start=True, stop=False)
                        nc.tensor.matmul(s_out, qT_hi[par][:, h, rows], kT_lo[:, 0:w], start=False, stop=False)
                        nc.tensor.matmul(score_ps[u % 2][:, c + w - P:c + w], ident_bf[:], causal[:],
                                         start=False, stop=False, skip_group_check=True)
                        last = nc.tensor.matmul(s_out, qT_lo[par][:, h, rows], kT_hi[:, 0:w], start=False, stop=True)
                    last.then_inc(scores_ps, 1)

                def bank_copies(b, g, v):
                    pair = 16 * b + BODY_PAIRS * g + v // UNITS
                    return 3 * pair + ACT_COPIES[v % UNITS], 2 * pair + DVE_COPIES[v % UNITS]

                def transpose_probs(b, g, v):
                    pe.wait_ge(prob_scaled, 80 * b + BODY * g + v + 1)
                    if known(g, v, 2):
                        by_act, by_dve = bank_copies(b, g, v - 2)
                        if (v - 2) % UNITS in ACT_BANKS:
                            pe.wait_ge(probT_by_act, by_act)
                        else:
                            pe.wait_ge(probT_by_dve, by_dve)
                    for h, i, c in MEMBERS[v % UNITS]:
                        for j in range(i + 1):
                            at = slice(c + j * P, c + (j + 1) * P)
                            last = nc.tensor.transpose(probT_ps[v % 2][:, at], prob[v % RING][:, at], ident[:])
                    last.then_inc(probT_done, 1)

                def pv(b, g, p, group):
                    pair = 16 * b + BODY_PAIRS * g + p
                    banks = [k for k in range(UNITS) if PV_GROUP[k] == group]
                    by_act, by_dve = bank_copies(b, g, UNITS * p + banks[-1])
                    pe.wait_ge(probT_by_act, by_act)
                    pe.wait_ge(probT_by_dve, by_dve)
                    if group == 0 and known(g, UNITS * p, UNITS):
                        pe.wait_ge(oT_hi_set, pair)
                        pe.wait_ge(oT_lo_set, pair)
                    where = {}
                    for k in banks:
                        for h, i, c in MEMBERS[k]:
                            where[i, h] = (probT[(UNITS * p + k) % RING], c)
                    for i in sorted({i for i, _ in where}, reverse=True):
                        for j in range(i + 1):
                            for h in range(2):
                                src, c = where[i, h]
                                last = nc.tensor.matmul(o_ps[64 * h:64 * h + 64, i * P:(i + 1) * P], ckv[:, j, :],
                                                        src[:, c + j * P:c + (j + 1) * P], start=(j == 0), stop=(j == i),
                                                        tile_position=(0, 64 * h))
                    last.then_inc(pv_done, 1)

                def output(b, g, two, t, bank=out_ps, alone=False):
                    n = 32 * b + 4 * two + t
                    if t == 0:
                        pe.wait_ge(oT_hi_set, 16 * b + 2 * two + 2)
                        pe.wait_ge(oT_lo_set, 16 * b + 2 * two + 2)
                    if not alone and not (isinstance(two, int) and two == 0 and t == 0):
                        pe.wait_ge(y_added, n)
                    rows = slice(t * P, (t + 1) * P)
                    for k in range(2):
                        w_hi, w_lo = (w[:, bass.ds(2 * two + k, 1), :].rearrange("p a o -> p (a o)")
                                      for w in (wo_hi, wo_lo))
                        for j, (o, w) in enumerate(((oT_hi, w_hi), (oT_hi, w_lo), (oT_lo, w_hi))):
                            last = nc.tensor.matmul(bank, o[k][:, rows], w, start=(k == 0 and j == 0),
                                                    stop=(k == 1 and j == 2))
                    last.then_inc(y_ps, 1)

                def attend(b):
                    def work(g, u):
                        k, p = u % UNITS, u // UNITS
                        if within(g, u, SLOTS - 1):
                            scores(b, g, u)
                        if known(g, u, T_LAG) and within(g, u, SLOTS - 1 + T_LAG):
                            transpose_probs(b, g, u - T_LAG)
                        queries = within(g, u, UNITS * LAST_PAIR - 1)
                        n = BODY_PAIRS * g + p + 1
                        if k in (0, 2) and queries:
                            q_products(b, n, k // 2, False)
                        if k in PV_SLOT and known(g, u, UNITS):
                            pv(b, g, p - 1, PV_SLOT[k])
                        if p % 2 == 1 and k in OUT_SLOT and known(g, u, 3 * UNITS) and within(g, u, SLOTS - 1):
                            output(b, g, output_index(g, p), OUT_SLOT[k])
                        if k in (1, 3) and queries:
                            q_transposes(b, n, k // 2, False)
                    attention((b, pe), work, TAIL)
                    for t in range(ST):
                        output(b, BODIES - 1, PAIRS // 2 - 1, t, last_out_ps[t], t > 0)

                steps(-1, FIRST, STEPS)
                with loop(pe, 0, NB - 1) as b:
                    attend(b)
                    steps(b, 0, STEPS)
                attend(NB - 1)
                steps(NB - 1, 0, FIRST)

            @block.scalar
            def _(act):
                def xT_high(b, s):
                    act.wait_ge(xT_ps, 12 * b + 8 + s + 1)
                    nc.scalar.activation(xT_hi[s % 2][:].rearrange("p c q -> p (c q)"), X[0],
                                         ACT.Copy).then_inc(xT_hi_set, 1)

                def z_high(b, s):
                    act.wait_ge(zT_ps, 8 * b + 4 + s + 1)
                    nc.scalar.activation(zT_hi[s % 2][:], Z[0][:, 0:P], ACT.Copy).then_inc(zT_hi_set, 1)

                def gate_exponentials(b, s):
                    act.wait_ge(max_set, 8 * b + 4 + s + 1)
                    nc.scalar.activation(logit_exp, logit, ACT.Exp, bias=neg_logit_max, scale=1.0,
                                         accum_out=logit_sum).then_inc(logit_exp_set, 1)

                def down_copies(b, s):
                    t, d = s - DOWN, 4 * (b + 1) + s - DOWN
                    act.wait_ge(k_cos_set, d + 1)
                    flat, bank = down[s % 2][:].rearrange("p a r -> p (a r)"), banks_of(s)[:, 0, :]
                    nc.scalar.activation(flat[:, 0:QL], bank[:, 0:QL], ACT.Copy)
                    nc.scalar.activation(flat[:, QL:2 * P + KVL], bank[:, P:QL + KVL], ACT.Copy)
                    nc.scalar.activation(ckv[:, t, :], bank[:, QL:QL + KVL], ACT.Copy).then_inc(down_set, 1)

                def ckT_high(b, s):
                    bank = banks_of(s)[:, 1, :]
                    rows = slice((s - DOWN) * P, (s - DOWN + 1) * P)
                    act.wait_ge(ckT_ps, 4 * (b + 1) + s - DOWN + 1)
                    nc.scalar.activation(cq_hi[:, :, rows], bank[:, 0:2 * P].rearrange("p (a q) -> p a q", a=2), ACT.Copy)
                    nc.scalar.activation(kT_hi[:, rows], bank[:, 2 * P:3 * P], ACT.Copy,
                                         scale=SCORE_SCALE).then_inc(ckT_hi, 1)

                def steps(b, start, end):
                    xT_high(b, start)
                    for s in range(start, end):
                        if s > start:
                            (z_high if s <= DOWN else ckT_high)(b, s - 1)
                        if s < DOWN:
                            gate_exponentials(b, s)
                        if s + 1 < end:
                            xT_high(b, s + 1)
                        if s >= DOWN:
                            down_copies(b, s)
                    if end == FIRST:
                        z_high(b, end - 1)
                    else:
                        q_latent(b + 1, 0, 0)
                        ckT_high(b, end - 1)
                        qT_high(b + 1, 0, 0, 0)
                        q_latent(b + 1, 0, 1)
                        qT_high(b + 1, 0, 1, 0)

                def q_latent(b, n, half):
                    m = 32 * b + 2 * n + half
                    act.wait_ge(q_rot_set, m + 1)
                    if not (isinstance(n, int) and n == 0 and half == 0):
                        act.wait_ge(qT_done, m)
                    nc.scalar.activation(q_tok[:, :, :, 0:KVL].rearrange("p t h r -> p (t h) r"),
                                         q_ps.rearrange("p (a r) -> p a r", r=HD)[:, :, 0:KVL],
                                         ACT.Copy).then_inc(q_lat_set, 1)

                def qT_high(b, n, half, par):
                    act.wait_ge(qT_done, 32 * b + 2 * n + half + 1)
                    nc.scalar.activation(qT_hi[par][:, :, half * 256:(half + 1) * 256],
                                         qT_ps.rearrange("p (h q) -> p h q", h=2), ACT.Copy).then_inc(qT_hi_set, 1)

                def oT_high(b, g, p):
                    act.wait_ge(pv_done, 3 * (16 * b + BODY_PAIRS * g + p - 1))
                    if known(g, UNITS * p, 4 * UNITS):
                        act.wait_ge(y_ps, 32 * b + ST * ((BODY_PAIRS // 2) * g + (p - 4) // 2) + ST)
                    nc.scalar.activation(oT_hi[p % 2][:], o_ps, ACT.Copy).then_inc(oT_hi_set, 1)

                def attend(b):
                    def work(g, u):
                        k, p = u % UNITS, u // UNITS
                        n1 = BODY_PAIRS * g + p + 1
                        queries = within(g, u, UNITS * LAST_PAIR - 1)
                        if k == 0 and known(g, u, 2 * UNITS):
                            oT_high(b, g, p)
                        if k in (2, 4) and queries:
                            qT_high(b, n1, k // 2 - 1, (p + 1) % 2)
                        if k in (1, 3) and queries:
                            q_latent(b, n1, k // 2)
                        if within(g, u, SLOTS - 1):
                            n = 80 * b + BODY * g + u
                            act.wait_ge(neg_max_set, n + 1)
                            if known(g, u, RING):
                                act.wait_ge(probT_done, n - RING + 1)
                            for m, (_, i, c) in enumerate(MEMBERS[k]):
                                w = (i + 1) * P
                                last = nc.scalar.activation(prob[u % RING][:, c:c + w], score_ps[u % 2][:, c:c + w],
                                                            ACT.Exp, bias=neg_max[:, u % RING, m:m + 1], scale=1.0,
                                                            accum_out=row_sum[:, u % RING, m:m + 1])
                            last.then_inc(prob_set, 1)
                        v = u - T_LAG
                        if known(g, u, T_LAG) and within(g, u, SLOTS - 1 + T_LAG) and v % UNITS in ACT_BANKS:
                            copy_probT(act, nc.scalar, b, g, v)
                    attention((b, act), work, TAIL)

                steps(-1, FIRST, STEPS)
                with loop(act, 0, NB - 1) as b:
                    attend(b)
                    steps(b, 0, STEPS)
                attend(NB - 1)
                steps(NB - 1, 0, FIRST)

            @block.vector
            def _(dve):
                def source(b, s):
                    return x_next if FIRST <= s < DOWN and not first(b + 1) else x_sb

                def row_stats(b, s, before=None):
                    if before is not None:
                        dve.wait_ge(stats_set, before)
                    if FIRST <= s < DOWN:
                        dve.wait_ge(x_in[s - FIRST], 16 * (b + 2))
                    nc.vector.bn_stats(stats[:, s % ST, :], source(b, s)[:, s % ST, :]).then_inc(stats_set, 1)

                def row_moments(s):
                    return nc.vector.bn_aggr(moments[:, s, :], stats[:, s % ST, :])

                def deviations(group, s, n, roughs=None, moments_of=None, stats_count=None):
                    at = slice(s, s + n)
                    if moments_of is not None:
                        dve.wait_ge(stats_set, stats_count)
                    dve.wait_ge(rough_set, group + 1 if roughs is None else roughs)
                    nc.vector.tensor_tensor(newton[:, at], rough[:, at], rough[:, at], ALU.mult).then_inc(newton_set, 1)
                    if moments_of is not None:
                        row_moments(moments_of).then_inc(var_set, 1)
                    dve.wait_ge(newton_set, 3 * group + 1)
                    nc.vector.tensor_tensor(newton[:, at], newton[:, at], var_eps[:, at], ALU.mult).then_inc(newton_set, 1)
                    dve.wait_ge(newton_set, 3 * group + 2)
                    nc.vector.tensor_scalar(newton[:, at], newton[:, at], -0.5, 1.5, ALU.mult, ALU.add).then_inc(newton_set, 1)
                    dve.wait_ge(newton_set, 3 * group + 3)
                    nc.vector.tensor_tensor(rstd[:, at], newton[:, at], rough[:, at], ALU.mult).then_inc(rstd_set, 1)
                    dve.wait_ge(rstd_set, group + 1)

                def norm(b, s, start):
                    if s >= start + 2:
                        dve.wait_ge(xT_ps, 12 * b + 8 + s - 1)
                    nc.vector.tensor_scalar(xn[s % 2][:], source(b, s)[:, s % ST, :], moments[:, s, 0:1],
                                            rstd[:, s:s + 1], ALU.subtract, ALU.mult).then_inc(xn_set, 1)

                def xT_low(b, s, stats_of=None):
                    dve.wait_ge(xT_hi_set, 12 * b + 8 + s + 1)
                    if stats_of is not None:
                        dve.wait_ge(stats_set, 12 * b + 8 + stats_of + 1)
                    nc.vector.tensor_tensor(xT_lo[s % 2][:].rearrange("p c q -> p (c q)"), X[0],
                                            f32(xT_hi[s % 2][:]).rearrange("p c q -> p (c q)"),
                                            ALU.subtract).then_inc(xT_lo_set, 1)

                def gate_logits(b, s):
                    f = 8 * b + 4 + s
                    dve.wait_ge(z_ps, f + 1)
                    nc.vector.tensor_tensor(logit, banks_of(s)[:, 0, OH + NZ:W0], prior_row, ALU.add).then_inc(logit_set, 1)
                    dve.wait_ge(logit_set, f + 1)
                    nc.vector.reduce_max(neg_logit_max, logit, AX, negate=True).then_inc(max_set, 1)

                def gate_rows(b, s, start):
                    f, bank = 8 * b + 4 + s, banks_of(s)
                    dve.wait_ge(logit_exp_set, f + 1)
                    nc.vector.reciprocal(inv_logit_sum, logit_sum).then_inc(sum_inv_set, 1)
                    dve.wait_ge(sum_inv_set, f + 1)
                    nc.vector.tensor_scalar(alpha, logit_exp, inv_logit_sum, LORA_SCALE,
                                            ALU.mult, ALU.mult).then_inc(alpha_set, 1)
                    if s == start:
                        dve.wait_ge(z_static, b + 2)
                    if s >= start + 2:
                        dve.wait_ge(zT_ps, f - 1)
                    dve.wait_ge(alpha_set, f + 1)
                    gate = alpha.unsqueeze(2).broadcast_to([P, NE, R])
                    for half in range(2):
                        last = nc.vector.tensor_tensor(za[s % 2][:, half, 0:NZ].rearrange("p (e r) -> p e r", e=NE),
                                                       bank[:, 0, OH:OH + NZ].rearrange("p (e r) -> p e r", e=NE),
                                                       gate, ALU.mult)
                    last.then_inc(za_set, 1)

                def z_low(b, s):
                    dve.wait_ge(zT_hi_set, 8 * b + 4 + s + 1)
                    nc.vector.tensor_tensor(zT_lo[s % 2][0:64, :], Z[0][0:64, 0:P], f32(zT_hi[s % 2][0:64, :]),
                                            ALU.subtract).then_inc(zT_lo_set, 1)

                def update_rows(b, s):
                    if FIRST <= s and not first(b + 1):
                        dve.wait_ge(x_out[s - FIRST], 16 * (b + 1))
                    dve.wait_ge(y_done, 8 * b + 4 + s + 1)
                    old, new = (x[:, s % ST, :].rearrange("p (a o) -> p a o", a=2) for x in (source(b, s), x_sb))
                    nc.vector.scalar_tensor_tensor(out=new, in0=banks_of(s)[:, :, 0:OH], scalar=0.5, in1=old,
                                                   op0=ALU.mult, op1=ALU.add).then_inc(x_updated, 1)

                def key_rotary(b, s):
                    t, d = s - DOWN, 4 * (b + 1) + s - DOWN
                    dve.wait_ge(down_ps, d + 1)
                    if t >= 2:
                        dve.wait_ge(ckT_ps, d - 1)
                    key = banks_of(s)[:, 0, QL + KVL:DC].rearrange("p (k f) -> p k f", k=2)
                    rot = down[s % 2][:, 2, KVL:HD].rearrange("p (k f) -> p k f", k=2)
                    nc.vector.tensor_tensor(rot, key, cos_sb[:, t, :].unsqueeze(1).broadcast_to([P, 2, HALF]), ALU.mult)
                    nc.vector.tensor_tensor(k_sin[:], key, sin_sb[:, t, :, :], ALU.mult).then_inc(k_cos_set, 1)
                    dve.wait_ge(k_cos_set, d + 1)
                    nc.vector.tensor_tensor(rot, rot, k_sin[:, ::-1, :], ALU.add).then_inc(k_rot_set, 1)

                def ckT_low(b, s):
                    bank = banks_of(s)[:, 1, :]
                    rows = slice((s - DOWN) * P, (s - DOWN + 1) * P)
                    dve.wait_ge(ckT_hi, 4 * (b + 1) + s - DOWN + 1)
                    nc.vector.tensor_tensor(cq_lo[:, 0, rows], bank[:, 0:P], f32(cq_hi[:, 0, rows]), ALU.subtract)
                    nc.vector.tensor_tensor(cq_lo[0:64, 1, rows], bank[0:64, P:2 * P], f32(cq_hi[0:64, 1, rows]),
                                            ALU.subtract)
                    nc.vector.scalar_tensor_tensor(out=kT_lo[:, rows], in0=bank[:, 2 * P:3 * P], scalar=SCORE_SCALE,
                                                   in1=f32(kT_hi[:, rows]), op0=ALU.mult,
                                                   op1=ALU.subtract).then_inc(ckT_lo, 1)

                def steps(b, start, end):
                    group = GROUPS_0 + GROUPS * b + 3 if start == 0 else 1
                    if start == FIRST:
                        for s in range(FIRST, DOWN):
                            row_stats(b, s, s - FIRST if s > FIRST else None)
                            if s > FIRST:
                                row_moments(s - 1)
                        dve.wait_ge(stats_set, ST)
                        row_moments(DOWN - 1).then_inc(var_set, 1)
                        deviations(0, FIRST, ST)
                    norm(b, start, start)
                    norm(b, start + 1, start)
                    if start == 0:
                        deviations(group - 2, 2, 2, roughs=group if end > FIRST else group - 1)
                    xT_low(b, start)
                    if start == 0 and end > FIRST:
                        deviations(group - 1, FIRST, ST, roughs=group - 2)
                    for s in range(start, end):
                        if s - 2 >= start and s - 2 < DOWN:
                            update_rows(b, s - 2)
                        if DOWN <= s + 1 < end:
                            deviations(group + s + 1 - DOWN, s + 1, 1)
                        if start < s < end - 1:
                            norm(b, s + 1, start)
                        if DOWN <= s + 2 < end:
                            dve.wait_ge(x_updated, 8 * b + 4 + s - 1)
                            row_stats(b, s + 2)
                        if s < DOWN:
                            gate_logits(b, s)
                        if s > start:
                            (z_low if s <= DOWN else ckT_low)(b, s - 1)
                        if s < DOWN:
                            gate_rows(b, s, start)
                        if s + 1 < end:
                            down_next = DOWN <= s + 2 < end
                            xT_low(b, s + 1, s + 2 if down_next else None)
                            if down_next:
                                row_moments(s + 2).then_inc(var_set, 1)
                        if s >= DOWN:
                            key_rotary(b, s)
                    if end == FIRST:
                        update_rows(b, end - 2)
                        z_low(b, end - 1)
                        update_rows(b, end - 1)
                    else:
                        q_rotary(b + 1, 0, 0)
                        ckT_low(b, end - 1)
                        qT_low(b + 1, 0, 0, 0)
                        q_rotary(b + 1, 0, 1)
                        qT_low(b + 1, 0, 1, 0)

                def q_rotary(b, n, half):
                    m = 32 * b + 2 * n + half
                    dve.wait_ge(q_done, m + 1)
                    if not (isinstance(n, int) and n == 0 and half == 0):
                        dve.wait_ge(qT_done, m)
                    for tt in range(2):
                        t = 2 * half + tt
                        q = q_ps[:, tt * 256:(tt + 1) * 256].rearrange("p (h r) -> p h r", h=2)[:, :, KVL:HD] \
                            .rearrange("p h (k f) -> p h k f", k=2)
                        nc.vector.tensor_tensor(q_tok[:, tt, :, KVL:HD].rearrange("p h (k f) -> p h k f", k=2), q,
                                                cos_sb[:, t, :].unsqueeze(1).unsqueeze(1).broadcast_to([P, 2, 2, HALF]),
                                                ALU.mult)
                        last = nc.vector.tensor_tensor(q_sin[:, 2 * tt:2 * tt + 2, :, :], q,
                                                       sin_sb[:, t, :, :].unsqueeze(1).broadcast_to([P, 2, 2, HALF]),
                                                       ALU.mult)
                    last.then_inc(q_rot_set, 1)

                def qT_low(b, n, half, par):
                    dve.wait_ge(qT_hi_set, 32 * b + 2 * n + half + 1)
                    at = slice(half * 256, (half + 1) * 256)
                    nc.vector.tensor_tensor(qT_lo[par][:, :, at], qT_ps.rearrange("p (h q) -> p h q", h=2),
                                            f32(qT_hi[par][:, :, at]), ALU.subtract).then_inc(qT_lo_set, 1)

                def inverse_sums(b, g, v):
                    n = 80 * b + BODY * g + v
                    dve.wait_ge(prob_set, n + 1)
                    k = len(MEMBERS[v % UNITS])
                    nc.vector.reciprocal(inv_sum[:, v % RING, 0:k], row_sum[:, v % RING, 0:k]).then_inc(inv_sum_set, 1)

                def add_output(b, two, t, bank=out_ps):
                    dve.wait_ge(y_ps, 32 * b + 4 * two + t + 1)
                    nc.vector.tensor_tensor(x_sb[:, t, :], bank, x_sb[:, t, :], ALU.add).then_inc(y_added, 1)

                def last_outputs(b, more):
                    group, count = GROUPS_0 + GROUPS * b, 12 * b + 8
                    if more:
                        for s in range(FIRST, DOWN):
                            row_stats(b, s, count + s - FIRST if s > FIRST else None)
                            if s > FIRST:
                                row_moments(s - 1)
                        dve.wait_ge(stats_set, count + ST)
                        count += ST
                    for t in range(ST):
                        if t:
                            dve.wait_ge(stats_set, count + t)
                        add_output(b, PAIRS // 2 - 1, t, last_out_ps[t])
                        if t:
                            done = row_moments(t - 1)
                            if t == 2:
                                done.then_inc(var_set, 1)
                        elif more:
                            row_moments(DOWN - 1).then_inc(var_set, 1)
                        dve.wait_ge(y_added, 32 * b + 29 + t)
                        row_stats(b, t)
                    deviations(group, 0, 2, group + 2 if more else group + 1, ST - 1, count + ST)

                def attend(b):
                    def work(g, u):
                        k, p = u % UNITS, u // UNITS
                        n1 = BODY_PAIRS * g + p + 1
                        queries = within(g, u, UNITS * LAST_PAIR - 1)
                        if k in (2, 4) and queries:
                            qT_low(b, n1, k // 2 - 1, (p + 1) % 2)
                        if within(g, u, SLOTS - 1):
                            dve.wait_ge(scores_ps, 80 * b + BODY * g + u + 1)
                            for m, (_, i, c) in enumerate(MEMBERS[k]):
                                last = nc.vector.reduce_max(neg_max[:, u % RING, m:m + 1],
                                                            score_ps[u % 2][:, c:c + (i + 1) * P], AX, negate=True)
                            last.then_inc(neg_max_set, 1)
                        if k == 0 and known(g, u, 2 * UNITS):
                            dve.wait_ge(oT_hi_set, 16 * b + BODY_PAIRS * g + p - 1)
                            nc.vector.tensor_tensor(oT_lo[p % 2][:], o_ps, f32(oT_hi[p % 2][:]),
                                                    ALU.subtract).then_inc(oT_lo_set, 1)
                        v = u - T_LAG
                        if known(g, u, T_LAG) and within(g, u, SLOTS - 1 + T_LAG) and v % UNITS not in ACT_BANKS:
                            copy_probT(dve, nc.vector, b, g, v)
                        if within(g, u, SLOTS - 1):
                            inverse_sums(b, g, u)
                        if k in (0, 2) and queries:
                            q_rotary(b, n1, k // 2)
                        if p % 2 == 1 and k in OUT_SLOT and known(g, u, 3 * UNITS) and within(g, u, SLOTS - 1):
                            add_output(b, output_index(g, p), OUT_SLOT[k])
                    attention((b, dve), work, TAIL)

                steps(-1, FIRST, STEPS)
                with loop(dve, 0, NB - 1) as b:
                    attend(b)
                    last_outputs(b, True)
                    steps(b, 0, STEPS)
                attend(NB - 1)
                last_outputs(NB - 1, False)
                steps(NB - 1, 0, FIRST)


def kernel(**inputs):
    import numpy as _np
    import concourse.bacc as _bacc
    from concourse import mybir as _mybir
    from concourse.bass_utils import run_bass_kernel_spmd as _run

    nc = _bacc.Bacc("TRN2", target_bir_lowering=False, num_devices=1)
    arrays, args = {}, []
    for name in _INS:
        a = _np.ascontiguousarray(inputs[name])
        arrays[f"in_{name}_dram"] = a
        args.append(nc.dram_tensor(f"in_{name}_dram", a.shape, _mybir.dt.from_np(a.dtype), kind="ExternalInput").ap())
    for name, a in zip(("rope_cos", "rope_sin"), rope_tables()):
        arrays[f"in_{name}_dram"] = a
        args.append(nc.dram_tensor(f"in_{name}_dram", a.shape, F32, kind="ExternalInput").ap())
    args.append(nc.dram_tensor("out_0_dram", (NB, S, D), F32, kind="ExternalOutput").ap())
    build(nc, *args)
    r = _run(nc, [arrays], core_ids=[0])
    return r.results[0]["out_0_dram"]
```

```python
from contextlib import ExitStack

import numpy as np

import concourse.bass as bass
from concourse import mybir

F32 = mybir.dt.float32
F32R = mybir.dt.float32r
BF16 = mybir.dt.bfloat16
I32 = mybir.dt.int32
ALU = mybir.AluOpType
ACT = mybir.ActivationFunctionType
AX = mybir.AxisListType.X

P = 128
NB, S, D = 4, 512, 512
ST = S // P
KC = D // P
H = 32
QL, KVL, DN, DR, DV = 192, 64, 128, 64, 128
HD = KVL + DR
HALF = DR // 2
NE, R = 4, 8
NZ = NE * R
EPS_LN = 1e-5
EPS_PRIOR = 1e-12
LORA_SCALE = 16.0 / 8.0
SCORE_SCALE = float(np.float32(1.0) / np.sqrt(np.float32(DN + DR)))
MASKED = -1e30
PAIRS = H // 2
STEPS = 3 * ST
FIRST, DOWN = ST, 2 * ST
OH = D // 2
W0 = OH + NZ + NE
WB = W0 + OH
DC = QL + KVL + DR

UNITS = 5
BODY_PAIRS = 4
BODY = UNITS * BODY_PAIRS
BODIES = PAIRS // BODY_PAIRS
MEMBERS = (
    ((0, 3, 0),),
    ((1, 3, 0),),
    ((0, 2, 0), (0, 0, 384)),
    ((1, 2, 0), (1, 0, 384)),
    ((0, 1, 0), (1, 1, 256)),
)
RING = 4
T_LAG = 3
PV_SLOT = {1: 0, 3: 1, 4: 2}
PV_GROUP = (0, 0, 1, 1, 2)
OUT_SLOT = {1: 0, 2: 1, 3: 2, 4: 3}
TAIL = UNITS + 1
ACT_BANKS = (0, 2, 4)
ACT_COPIES = (1, 1, 2, 2, 3)
DVE_COPIES = (0, 1, 1, 2, 2)


_INS = ["L0_attn_hidden_states", "L0_attn_w_q_down", "L0_attn_w_q_up_nope", "L0_attn_w_q_up_rope",
        "L0_attn_w_kv_down", "L0_attn_w_k_rope", "L0_attn_w_uk", "L0_attn_w_uv", "L0_attn_w_out",
        "L0_ffn_W_base", "L0_ffn_b_base", "L0_ffn_lora_A", "L0_ffn_lora_B", "L0_ffn_router_W",
        "L0_ffn_router_b", "L0_ffn_domain_prior", "L0_ffn_active"]


def rope_tables():
    f = np.float32
    freqs = f(1.0) / f(10000.0) ** (np.arange(0, DR, 2, dtype=f) / f(DR))
    wavelengths = f(2.0 * np.pi) / freqs
    ramp = np.clip((wavelengths / f(4096.0) - f(1.0)) / f(32.0 - 1.0), f(0.0), f(1.0))
    inv_freq = freqs / (f(1.0) - ramp + ramp * f(40.0))
    angle = np.arange(S, dtype=f)[:, None] * inv_freq[None, :]
    cos = np.cos(angle).astype(f).reshape(ST, P, HALF).transpose(1, 0, 2)
    sin = np.sin(angle).astype(f).reshape(ST, P, HALF).transpose(1, 0, 2)
    return np.ascontiguousarray(cos), np.ascontiguousarray(np.stack([sin, -sin], axis=2))


def build(nc, hidden, w_q_down, w_q_up_nope, w_q_up_rope, w_kv_down, w_k_rope, w_uk, w_uv, w_out,
          W_base, b_base, lora_A, lora_B, router_W, router_b, domain_prior, active,
          rope_cos, rope_sin, out):
    with ExitStack() as ctx:
        def sem(name):
            return ctx.enter_context(nc.semaphore(name))

        sbuf_start = (nc.sbuf_base + 31) // 32 * 32
        sbuf_end = nc.sbuf_usable_end
        cursor = [sbuf_start]

        def place(name, shape, dt, at=None):
            size = int(np.prod(shape[1:])) * mybir.dt.size(dt)
            size = (size + 31) // 32 * 32
            where = cursor if at is None else at
            t = nc.alloc_sbuf_tensor_at(name, list(shape), dt, offset=where[0])
            where[0] += size
            assert where[0] <= sbuf_end, (name, where[0] - sbuf_end)
            return t

        wb_hi = place("wb_hi", [P, KC, WB], F32R)
        wb_lo = place("wb_lo", [P, KC, WB], F32R)
        lora_up = place("lora_up", [P, D], F32R)
        wd_hi = place("wd_hi", [P, KC, DC], F32R)
        wd_lo = place("wd_lo", [P, KC, DC], F32R)
        wq1_hi = place("wq1_hi", [P, H, HD], F32R)
        wq1_lo = place("wq1_lo", [P, H, HD], F32R)
        wq2 = place("wq2", [P, H, HD], F32R)
        x_sb = place("x_sb", [P, ST, D], F32)
        cq_hi = place("cq_hi", [P, 2, S], F32R)
        cq_lo = place("cq_lo", [P, 2, S], F32R)
        kT_hi = place("kT_hi", [P, S], F32R)
        kT_lo = place("kT_lo", [P, S], F32R)
        ckv = place("ckv", [P, ST, KVL], F32)
        cos_sb = place("cos_sb", [P, ST, HALF], F32)
        sin_sb = place("sin_sb", [P, ST, 2, HALF], F32)
        ident = place("ident", [P, P], F32)
        ident_bf = place("ident_bf", [P, P], BF16)
        causal = place("causal", [P, P], BF16)
        small = place("small", [P, 56], F32)

        def columns(at, n):
            return small[:, at:at + n]

        prior_row, three_halves = columns(9, 4), columns(0, 1)
        logit, neg_logit_max, logit_exp, logit_sum = columns(13, 4), columns(17, 1), columns(18, 4), columns(22, 1)
        inv_logit_sum, alpha = columns(23, 1), columns(24, 4)
        neg_max = columns(28, 2 * RING).rearrange("p (r m) -> p r m", m=2)
        row_sum = columns(36, 2 * RING).rearrange("p (r m) -> p r m", m=2)
        inv_sum = columns(44, 2 * RING).rearrange("p (r m) -> p r m", m=2)
        ones, eps, minus_half = columns(52, 2), columns(54, 1), columns(55, 1)
        region_a = [cursor[0]]
        wo_hi = place("wo_hi", [P, PAIRS, D], F32R)
        wo_lo = place("wo_lo", [P, PAIRS, D], F32R)
        region_b0 = cursor[0]

        nope_a = place("nope_a", [P, H, DN], F32, region_a)
        nope_b = place("nope_b", [64, H, DN], F32, region_a)
        nopeT_a = [place(f"nopeT_a{i}", [P, 4, P], F32, region_a) for i in range(2)]
        nopeT_b = [place(f"nopeT_b{i}", [P, 4, 64], F32, region_a) for i in range(2)]
        uk_sb = place("uk_sb", [P, H, KVL], F32, region_a)
        rope_a = place("rope_a", [P, H, DR], F32, region_a)
        rope_bb = place("rope_bb", [P, H, DR], F32, region_a)
        assert region_a[0] <= region_b0
        rb = [region_b0]
        wbase_nat = place("wbase_nat", [P, KC, D], F32, rb)
        lora_nat = place("lora_nat", [NZ + NE, D], F32, rb)
        up_nat = place("up_nat", [P, KC, P], F32, rb)
        up_b = place("up_b", [P, KC, NE, R], F32, rb)
        down_nat = place("down_nat", [P, KC, DC], F32, rb)
        active_sb = place("active_sb", [1, NE], I32, rb)
        router_row = place("router_row", [P, NE], F32, rb)
        prior_raw = place("prior_raw", [P, NE], F32, rb)
        bias_nat = place("bias_nat", [P, KC], F32, rb)
        rb = [region_b0]
        xn = [place(f"xn{i}", [P, D], F32, rb) for i in range(2)]
        xT_hi = [place(f"xT_hi{i}", [P, KC, P], F32R, rb) for i in range(2)]
        xT_lo = [place(f"xT_lo{i}", [P, KC, P], F32R, rb) for i in range(2)]
        za = [place(f"za{i}", [P, 2, 64], F32, rb) for i in range(2)]
        zT_hi = [place(f"zT_hi{i}", [P, P], F32R, rb) for i in range(2)]
        zT_lo = [place(f"zT_lo{i}", [P, P], F32R, rb) for i in range(2)]
        down = [place(f"down{i}", [P, 3, P], F32, rb) for i in range(2)]
        k_sin = place("k_sin", [P, 2, HALF], F32, rb)
        rb = [region_b0]
        prob = [place(f"prob{i}", [P, S], F32, rb) for i in range(RING)]
        probT = [place(f"probT{i}", [P, S], F32, rb) for i in range(RING)]
        oT_hi = [place(f"oT_hi{i}", [P, S], F32R, rb) for i in range(2)]
        oT_lo = [place(f"oT_lo{i}", [P, S], F32R, rb) for i in range(2)]
        after_outputs = [rb[0]]
        q_tok = place("q_tok", [P, 2, 2, HD], F32, rb)
        q_sin = place("q_sin", [P, 4, 2, HALF], F32, rb)
        after_scores = [rb[0]]
        qT_hi = [place(f"qT_hi{i}", [P, 2, S], F32R, rb) for i in range(2)]
        qT_lo = [place(f"qT_lo{i}", [P, 2, S], F32R, rb) for i in range(2)]
        stats = place("stats", [P, ST, 6], F32, after_outputs)
        moments = place("moments", [P, STEPS, 2], F32, after_outputs)
        var_eps, rough, newton, rstd = (place(n, [P, STEPS], F32, after_outputs) for n in
                                        ("var_eps", "rough", "newton", "rstd"))
        uv_nat = [place(f"uv_nat{i}", [P, 4, KVL], F32, after_outputs) for i in range(2)]
        assert after_outputs[0] <= after_scores[0]
        fold_staging = [after_scores[0]]
        wout_nat = [place(f"wout_nat{i}", [P, 4, D], F32, fold_staging) for i in range(2)]
        x_next = place("x_next", [P, ST, D], F32, after_scores)

        Y = [ctx.enter_context(nc.psum_tensor(f"Y{i}", [P, 2, 512], F32)) for i in range(2)]
        XZ = [ctx.enter_context(nc.psum_tensor(f"XZ{i}", [P, 2, 512], F32)) for i in range(2)]
        X, Z = [xz[:, 0, :] for xz in XZ], [xz[:, 1, :] for xz in XZ]
        score_ps, probT_ps = X, Z
        o_ps, out_ps, q_ps, qT_ps = Y[0][:, 0, :], Y[0][:, 1, :], Y[1][:, 0, :], Y[1][:, 1, :]

        weights_ps = (Z[0], Y[1][:, 1, :])
        nopeTa_ps, nopeTb_ps, fold_banks = (X[0], Y[0][:, 0, :]), (X[1], Y[0][:, 1, :]), (Z[1], Y[1][:, 0, :])
        last_out_ps = (Y[0][:, 1, :], Y[1][:, 0, :], Y[1][:, 1, :], Y[0][:, 0, :])

        def f32(t):
            return t.bitcast(F32)

        active_in, x_in = sem("active_in"), [sem(f"x_in{t}") for t in range(ST)]
        tables_in, ffn_in, gather_in = sem("tables_in"), sem("ffn_in"), sem("gather_in")
        down_in, rope_in, uk_in = sem("down_in"), sem("rope_in"), sem("uk_in")
        nope_in = [sem(f"nope_in{i}") for i in range(2)]
        out_in = [sem(f"out_in{i}") for i in range(2)]
        ident_set, up_zeroed = sem("ident_set"), sem("up_zeroed")
        up_filled = sem("up_filled")
        baseT_ps, base_hi, base_lo = sem("baseT_ps"), sem("base_hi"), sem("base_lo")
        loraT_ps, lora_hi_set = sem("loraT_ps"), sem("lora_hi_set")
        upT_ps, up_hi = sem("upT_ps"), sem("up_hi")
        prior_eps, prior_ln = sem("prior_eps"), sem("prior_ln")
        down_hi_set, rope_hi_set = sem("down_hi_set"), sem("rope_hi_set")
        nopeT_ps, nopeTa_set, nopeTb_set = sem("nopeT_ps"), sem("nopeTa_set"), sem("nopeTb_set")
        fold_ps, fold_hi, fold_lo = sem("fold_ps"), sem("fold_hi"), sem("fold_lo")
        outw_ps, outw_hi, outw_lo = sem("outw_ps"), sem("outw_hi"), sem("outw_lo")

        stats_set = sem("stats_set")

        G4 = H // 4
        GATHERED = 5 * NE + 1

        def loop(eng, start, end):
            return nc.Fori(start, end, engines=(eng.engine,), hint_back_edge=True)

        def rounds(eng, n, body):
            body(0)
            with loop(eng, 1, n) as i:
                body(i)

        def pipelined(eng, opening, body, between):
            opening()
            body(0)
            between()
            with loop(eng, 1, G4 // 2 - 1) as i:
                body(i)
            body(G4 // 2 - 1)

        def final(g):
            return isinstance(g, int) and g == G4 - 1

        def first(i):
            return isinstance(i, int) and i == 0

        with nc.Block() as block:
            @block.sync
            def _(sp):
                sp.dma_start(active_sb[:], active.unsqueeze(0)).then_inc(active_in, 16)
                sp.dma_start(bias_nat[:], b_base.rearrange("(c p) -> p c", p=P),
                             allow_slow_non_contiguous=True).then_inc(gather_in, 16)
                sp.wait_ge(active_in, 16)
                for e in range(NE):
                    a = sp.value_load(active_sb[0:1, e:e + 1], min_val=0, max_val=lora_A.shape[0] - 1)
                    sp.dma_start(lora_nat[e * R:(e + 1) * R, :],
                                 lora_A[bass.ds(a, 1), :, :].rearrange("e r h -> (e r) h")).then_inc(gather_in, 16)
                    sp.dma_start(lora_nat[NZ + e:NZ + e + 1, :], router_W[bass.ds(a, 1), :]).then_inc(gather_in, 16)
                    sp.dma_start(up_b[:, :, e, :],
                                 lora_B[bass.ds(a, 1), :, :].rearrange("e (c p) r -> p (e c) r", p=P)
                                 ).then_inc(gather_in, 16)
                    sp.dma_start(router_row[:, e:e + 1],
                                 router_b[bass.ds(a, 1)].unsqueeze(0).broadcast_to([P, 1])).then_inc(gather_in, 16)
                    sp.dma_start(prior_raw[:, e:e + 1],
                                 domain_prior[bass.ds(a, 1)].unsqueeze(0).broadcast_to([P, 1])).then_inc(gather_in, 16)
                for t in range(ST):
                    sp.dma_start(x_sb[:, t, :], hidden[0, t * P:(t + 1) * P, :]).then_inc(x_in[t], 16)


            @block.gpsimd
            def _(pool):
                pool.memset(ident[:], 0.0).then_inc(ident_set, 1)
                pool.memset(causal[:], 0.0).then_inc(ident_set, 1)
                pool.memset(ones, 1.0)
                pool.memset(eps, EPS_LN)
                pool.memset(minus_half, -0.5)
                pool.memset(three_halves, 1.5)
                pool.memset(up_nat[:], 0.0).then_inc(up_zeroed, 1)
                pool.wait_ge(ident_set, 2)
                pool.affine_select(out=ident[:], in_=ident[:], compare_op=ALU.not_equal, fill=1.0, base=0,
                                   pattern=[[-1, P]], channel_multiplier=1).then_inc(ident_set, 1)
                pool.affine_select(out=causal[:], in_=causal[:], compare_op=ALU.is_ge, fill=MASKED, base=0,
                                   pattern=[[-1, P]], channel_multiplier=1)
                pool.wait_ge(ident_set, 3)
                pool.tensor_copy(ident_bf[:], ident[:])
                pool.wait_ge(rope_hi_set, 1)
                nc.gpsimd.tensor_tensor(wq1_lo[:, :, KVL:HD], rope_a[:], f32(wq1_hi[:, :, KVL:HD]),
                                        ALU.subtract)
                pool.wait_ge(down_hi_set, 1)
                nc.gpsimd.tensor_tensor(wd_lo[:], down_nat[:], f32(wd_hi[:]), ALU.subtract)

            @block.scalar
            def _(act):
                act.dma_start(wbase_nat[:], W_base.rearrange("(c p) h -> p c h", p=P)).then_inc(ffn_in, 16)
                act.dma_start(uk_sb[:], w_uk.rearrange("(h d) r -> d h r", d=DN)).then_inc(uk_in, 16)
                for half in range(2):
                    if half:
                        act.dma_start(rope_a[:], w_q_up_rope[0:P, :].rearrange("q (h d) -> q h d", d=DR)).then_inc(rope_in, 16)
                        for j in range(2):
                            act.dma_start(rope_bb[64 * j:64 * j + 64, :, :],
                                          w_q_up_rope[P:QL, :].rearrange("q (h d) -> q h d", d=DR)).then_inc(rope_in, 16)
                    heads, cols = slice(16 * half, 16 * half + 16), slice(16 * half * DN, 16 * (half + 1) * DN)
                    act.dma_start(nope_a[:, heads, :], w_q_up_nope[0:P, cols]
                                  .rearrange("q (h d) -> q h d", d=DN)).then_inc(nope_in[half], 16)
                    act.dma_start(nope_b[:, heads, :], w_q_up_nope[P:QL, cols]
                                  .rearrange("q (h d) -> q h d", d=DN)).then_inc(nope_in[half], 16)

                for c in range(KC):
                    act.wait_ge(baseT_ps, c + 1)
                    nc.scalar.activation(wb_hi[:, c, 0:OH], weights_ps[c % 2][:, 0:OH], ACT.Copy)
                    nc.scalar.activation(wb_hi[:, c, W0:WB], weights_ps[c % 2][:, OH:D], ACT.Copy).then_inc(base_hi, 1)

                act.dma_start(down_nat[:, :, 0:QL], w_q_down.rearrange("(c p) n -> p c n", p=P)).then_inc(down_in, 16)
                act.dma_start(down_nat[:, :, QL:QL + KVL],
                              w_kv_down.rearrange("(c p) n -> p c n", p=P)).then_inc(down_in, 16)
                act.dma_start(down_nat[:, :, QL + KVL:DC],
                              w_k_rope.rearrange("(c p) n -> p c n", p=P)).then_inc(down_in, 16)
                act.dma_start(cos_sb[:], rope_cos).then_inc(tables_in, 16)
                act.dma_start(sin_sb[:], rope_sin).then_inc(tables_in, 16)

                def rotary_hi():
                    act.wait_ge(rope_in, 48)
                    nc.scalar.activation(wq2[:, :, KVL:HD], rope_bb[:], ACT.Copy)
                    nc.scalar.activation(wq1_hi[:, :, KVL:HD], rope_a[:], ACT.Copy).then_inc(rope_hi_set, 1)

                def nopeTa_copy(g, j):
                    act.wait_ge(nopeT_ps, g + 1)
                    nc.scalar.activation(nopeT_a[j][:], nopeTa_ps[j].rearrange("p (h q) -> p h q", h=4),
                                         ACT.Copy).then_inc(nopeTa_set, 1)

                def query_hi(i):
                    for j in range(2):
                        g = 2 * i + j
                        if not final(g):
                            nopeTa_copy(g + 1, 1 - j)
                        act.wait_ge(fold_ps, g + 1)
                        nc.scalar.activation(wq1_hi[:, bass.ds(4 * g, 4), 0:KVL],
                                             fold_banks[j][:, 0:256].rearrange("p (h r) -> p h r", h=4), ACT.Copy)
                        nc.scalar.activation(wq2[:, bass.ds(4 * g, 4), 0:KVL],
                                             fold_banks[j][:, 256:512].rearrange("p (h r) -> p h r", h=4),
                                             ACT.Copy).then_inc(fold_hi, 1)
                pipelined(act, lambda: nopeTa_copy(0, 0), query_hi, rotary_hi)
                act.wait_ge(prior_eps, 1)
                nc.scalar.activation(prior_row, prior_raw[:], ACT.Ln).then_inc(prior_ln, 1)
                act.wait_ge(down_in, 48)
                nc.scalar.activation(wd_hi[:], down_nat[:], ACT.Copy).then_inc(down_hi_set, 1)
                act.wait_ge(loraT_ps, 1)
                nc.scalar.activation(wb_hi[:, :, OH:W0], weights_ps[1][:, 0:KC * (NZ + NE)].rearrange("p (c n) -> p c n", c=KC),
                                     ACT.Copy).then_inc(lora_hi_set, 1)
                act.wait_ge(upT_ps, 1)
                nc.scalar.activation(lora_up[:], weights_ps[0], ACT.Copy).then_inc(up_hi, 1)

            @block.tensor
            def _(pe):
                pe.wait_ge(ident_set, 3)
                pe.wait_ge(ffn_in, 16)
                for c in range(KC):
                    if c >= 2:
                        pe.wait_ge(base_hi, c - 1)
                        pe.wait_ge(base_lo, c - 1)
                    for o in range(KC):
                        last = nc.tensor.transpose(weights_ps[c % 2][:, o * P:(o + 1) * P],
                                                   wbase_nat[:, o, c * P:(c + 1) * P], ident[:])
                    last.then_inc(baseT_ps, 1)

                def transpose_nope(g, j):
                    for h in range(4):
                        nc.tensor.transpose(nopeTa_ps[j][:, h * P:(h + 1) * P],
                                            nope_a[:, 4 * g + h, :], ident[:])
                    for h in range(4):
                        last = nc.tensor.transpose(nopeTb_ps[j][:, h * 64:(h + 1) * 64],
                                                   nope_b[:, 4 * g + h, :],
                                                   ident[0:64, 0:64])
                    last.then_inc(nopeT_ps, 1)

                def fold_query(i):
                    for j in range(2):
                        g = 2 * i + j
                        if g + 1 == G4 // 2:
                            pe.wait_ge(nope_in[1], 32)
                        if not final(g):
                            transpose_nope(g + 1, 1 - j)
                        pe.wait_ge(nopeTa_set, g + 1)
                        pe.wait_ge(nopeTb_set, g + 1)
                        if not first(i):
                            pe.wait_ge(fold_hi, g - 1)
                            pe.wait_ge(fold_lo, g - 1)
                        for h in range(4):
                            uk = uk_sb[:, bass.ds(4 * g + h, 1), :].rearrange("p a r -> p (a r)")
                            for c, parts in enumerate((nopeT_a[j][:, h, 0:64], nopeT_a[j][:, h, 64:P])):
                                nc.tensor.matmul(fold_banks[j][64 * c:64 * c + 64, h * KVL:(h + 1) * KVL], parts, uk,
                                                 start=True, stop=True, tile_position=(0, 64 * c))
                            for c in range(2):
                                last = nc.tensor.matmul(fold_banks[j][64 * c:64 * c + 64, 256 + h * KVL:256 + (h + 1) * KVL],
                                                        nopeT_b[j][:, h, :], uk, start=True, stop=True,
                                                        tile_position=(0, 64 * c))
                        last.then_inc(fold_ps, 1)

                pe.wait_ge(uk_in, 16)
                pe.wait_ge(nope_in[0], 32)
                transpose_nope(0, 0)
                for i in range(G4 // 2):
                    fold_query(i)

                pe.wait_ge(gather_in, 16 * GATHERED)
                pe.wait_ge(base_lo, KC)
                for c in range(KC):
                    last = nc.tensor.transpose(weights_ps[1][:, c * (NZ + NE):(c + 1) * (NZ + NE)],
                                               lora_nat[:, c * P:(c + 1) * P], ident[0:NZ + NE, 0:NZ + NE])
                last.then_inc(loraT_ps, 1)
                pe.wait_ge(up_filled, 1)
                for o in range(KC):
                    last = nc.tensor.transpose(weights_ps[0][:, o * P:(o + 1) * P], up_nat[:, o, :], ident[:])
                last.then_inc(upT_ps, 1)

            @block.vector
            def _(dve):
                nc.vector.memset(f32(cq_lo[64:P, 1, :]), 0.0)
                for c in range(KC):
                    dve.wait_ge(base_hi, c + 1)
                    nc.vector.tensor_tensor(wb_lo[:, c, 0:OH], weights_ps[c % 2][:, 0:OH], f32(wb_hi[:, c, 0:OH]),
                                            ALU.subtract)
                    nc.vector.tensor_tensor(wb_lo[:, c, W0:WB], weights_ps[c % 2][:, OH:D], f32(wb_hi[:, c, W0:WB]),
                                            ALU.subtract).then_inc(base_lo, 1)
                def rotary_lo():
                    dve.wait_ge(rope_hi_set, 1)
                    nc.vector.tensor_tensor(wq2[64:P, :, KVL:HD], rope_bb[64:P, :, :], f32(wq2[64:P, :, KVL:HD]), ALU.subtract)

                def nopeTb_copy(g, j):
                    dve.wait_ge(nopeT_ps, g + 1)
                    nc.vector.tensor_copy(nopeT_b[j][:], nopeTb_ps[j][:, 0:256].rearrange("p (h q) -> p h q", h=4)
                                          ).then_inc(nopeTb_set, 1)

                def query_lo(i):
                    for j in range(2):
                        g = 2 * i + j
                        if not final(g):
                            nopeTb_copy(g + 1, 1 - j)
                        dve.wait_ge(fold_hi, g + 1)
                        heads = bass.ds(4 * g, 4)
                        nc.vector.tensor_tensor(wq1_lo[:, heads, 0:KVL],
                                                fold_banks[j][:, 0:256].rearrange("p (h r) -> p h r", h=4),
                                                f32(wq1_hi[:, heads, 0:KVL]), ALU.subtract)
                        nc.vector.tensor_tensor(wq2[64:P, heads, 0:KVL],
                                                fold_banks[j][64:P, 256:512].rearrange("p (h r) -> p h r", h=4),
                                                f32(wq2[64:P, heads, 0:KVL]), ALU.subtract).then_inc(fold_lo, 1)
                pipelined(dve, lambda: nopeTb_copy(0, 0), query_lo, rotary_lo)

                dve.wait_ge(tables_in, 32)
                dve.wait_ge(gather_in, 16 * GATHERED)
                dve.wait_ge(up_zeroed, 1)
                for j in range(2):
                    nc.vector.tensor_copy(up_nat[:, :, 64 * j:64 * j + NZ], up_b[:].rearrange("p c e r -> p c (e r)"))
                    last = nc.vector.tensor_copy(up_nat[:, :, 64 * j + NZ:64 * j + NZ + 1], bias_nat[:].unsqueeze(2))
                last.then_inc(up_filled, 1)
                nc.vector.tensor_scalar(prior_raw[:], prior_raw[:], EPS_PRIOR, None, ALU.add).then_inc(prior_eps, 1)
                for t in range(ST):
                    dve.wait_ge(x_in[t], 16)
                    nc.vector.bn_stats(stats[:, t, :], x_sb[:, t, :]).then_inc(stats_set, 1)
                dve.wait_ge(lora_hi_set, 1)
                nc.vector.tensor_tensor(wb_lo[:, :, OH:W0], weights_ps[1][:, 0:KC * (NZ + NE)]
                                        .rearrange("p (c n) -> p c n", c=KC), f32(wb_hi[:, :, OH:W0]),
                                        ALU.subtract)
                dve.wait_ge(up_hi, 1)
                nc.vector.tensor_tensor(lora_up[64:P, :], weights_ps[0][64:P, :], f32(lora_up[64:P, :]),
                                        ALU.subtract)

                dve.wait_ge(prior_ln, 1)
                nc.vector.tensor_tensor(prior_row, prior_row, router_row[:], ALU.add)

        xn_set = sem("xn_set")
        var_set, eps_added, rough_set = sem("var_set"), sem("eps_added"), sem("rough_set")
        newton_set, rstd_set = sem("newton_set"), sem("rstd_set")
        down_newton_set, down_rstd_set = sem("down_newton_set"), sem("down_rstd_set")
        xT_ps, xT_hi_set, xT_lo_set = sem("xT_ps"), sem("xT_hi_set"), sem("xT_lo_set")
        z_ps, logit_set, max_set, logit_exp_set = sem("z_ps"), sem("logit_set"), sem("max_set"), sem("logit_exp_set")
        sum_inv_set, alpha_set, za_set = sem("sum_inv_set"), sem("alpha_set"), sem("za_set")
        zT_ps, zT_hi_set, zT_lo_set = sem("zT_ps"), sem("zT_hi_set"), sem("zT_lo_set")
        y_done, x_updated, z_static = sem("y_done"), sem("x_updated"), sem("z_static")
        x_out = [sem(f"x_out{t}") for t in range(ST)]
        down_ps, down_set, k_cos_set, k_rot_set = sem("down_ps"), sem("down_set"), sem("k_cos_set"), sem("k_rot_set")
        ckT_ps, ckT_hi, ckT_lo = sem("ckT_ps"), sem("ckT_hi"), sem("ckT_lo")
        scores_ps, neg_max_set, prob_set = sem("scores_ps"), sem("neg_max_set"), sem("prob_set")
        inv_sum_set, prob_scaled, probT_done = sem("inv_sum_set"), sem("prob_scaled"), sem("probT_done")
        probT_by_act, probT_by_dve = sem("probT_by_act"), sem("probT_by_dve")
        pv_done = sem("pv_done")
        oT_hi_set, oT_lo_set = sem("oT_hi_set"), sem("oT_lo_set")
        q_done, q_lat_set, q_rot_set, q_tok_set = sem("q_done"), sem("q_lat_set"), sem("q_rot_set"), sem("q_tok_set")
        qT_done, qT_hi_set, qT_lo_set = sem("qT_done"), sem("qT_hi_set"), sem("qT_lo_set")
        y_ps, y_added = sem("y_ps"), sem("y_added")

        GROUPS_0, GROUPS = 1 + ST, 3 + ST

        def banks_of(s, opening=False):
            if opening:
                return (Y[1], XZ[1])[s % 2]
            if s >= DOWN:
                return (Y[0], XZ[1])[s % 2]
            return (XZ[1], Y[1], Y[0])[s % 3]

        def attention(b, slot_work, tail):
            for u in range(BODY):
                slot_work(0, u)
            with loop(b[1], 1, BODIES - 1) as g:
                for u in range(BODY):
                    slot_work(g, u)
            for u in range(BODY + tail):
                slot_work(BODIES - 1, u)

        def known(g, u, least):
            return not isinstance(g, int) or BODY * g + u >= least

        def within(g, u, most):
            return not isinstance(g, int) or BODY * g + u <= most

        def output_index(g, p):
            return (BODY_PAIRS // 2) * g + (p - 3) // 2

        def copy_probT(eng, do, b, g, v):
            pair = 16 * b + BODY_PAIRS * g + v // UNITS
            eng.wait_ge(probT_done, 80 * b + BODY * g + v + 1)
            if known(g, v, RING):
                w = v - RING
                eng.wait_ge(pv_done, 3 * (16 * b + BODY_PAIRS * g + w // UNITS) + PV_GROUP[w % UNITS] + 1)
            if eng.engine == nc.scalar.engine:
                do.activation(probT[v % RING][:], probT_ps[v % 2][:], ACT.Copy).then_inc(probT_by_act, 1)
            else:
                do.tensor_copy(probT[v % RING][:], probT_ps[v % 2][:]).then_inc(probT_by_dve, 1)

        SLOTS = UNITS * PAIRS
        LAST_PAIR = PAIRS - 1

        with nc.Block() as block:
            @block.sync
            def _(sp):
                def sequence(b, last):
                    if not last:
                        sp.wait_ge(scores_ps, SLOTS * (b + 1))
                        for t in range(ST):
                            sp.dma_start(x_next[:, t, :], hidden[bass.ds(b + 1, 1), t * P:(t + 1) * P, :]
                                         .rearrange("a p d -> (a p) d")).then_inc(x_in[t], 16)
                    for t in range(ST):
                        sp.wait_ge(x_updated, 8 * b + 4 + t + 1)
                        sp.dma_start(out[bass.ds(b, 1), t * P:(t + 1) * P, :].rearrange("a p d -> (a p) d"),
                                     x_sb[:, t, :]).then_inc(x_out[t], 16)
                def load_out(i):
                    for j in range(2):
                        g = 2 * i + j
                        if not first(i):
                            sp.wait_ge(outw_ps, g - 1)
                        rows = bass.ds(g * (4 * DV), 4 * DV)
                        sp.dma_start(uv_nat[j][:], w_uv[rows, :]
                                     .rearrange("(h d) r -> d h r", d=DV)).then_inc(out_in[j], 16)
                        sp.dma_start(wout_nat[j][:], w_out[rows, :]
                                     .rearrange("(h d) o -> d h o", d=DV)).then_inc(out_in[j], 16)
                rounds(sp, G4 // 2, load_out)
                with loop(sp, 0, NB - 1) as b:
                    sequence(b, False)
                sequence(NB - 1, True)
                for t in range(ST):
                    sp.wait_ge(x_out[t], 16 * NB)

            @block.gpsimd
            def _(pool):
                def z_constants():
                    for i in range(2):
                        pad = ident[:, 0:2 * (63 - NZ)].rearrange("p (a z) -> p a z", a=2)
                        nc.gpsimd.tensor_tensor(za[i][:, :, NZ + 1:64], pad, pad, ALU.subtract)
                        nc.gpsimd.tensor_tensor(za[i][:, :, NZ], ones, ones, ALU.mult)
                        last = nc.gpsimd.tensor_tensor(zT_lo[i][:], ident[:], ident[:], ALU.subtract)
                    last.then_inc(z_static, 1)

                def rough_deviations(group, s, n):
                    pool.wait_ge(var_set, group + 1)
                    nc.gpsimd.tensor_tensor(var_eps[:, s:s + n], moments[:, s:s + n, 1],
                                            eps.broadcast_to([P, n]), ALU.add).then_inc(eps_added, 1)
                    pool.wait_ge(eps_added, group + 1)
                    nc.gpsimd.tensor_tensor(rough[:, s:s + n], var_eps[:, s:s + n],
                                            minus_half.broadcast_to([P, n]), ALU.pow).then_inc(rough_set, 1)

                def down_deviations(b, s):
                    d, at = 4 * (b + 1) + s - DOWN, slice(s, s + 1)
                    group = GROUPS_0 + GROUPS * (b + 1) - ST + s - DOWN
                    rough_deviations(group, s, 1)
                    pool.wait_ge(rough_set, group + 1)
                    nc.gpsimd.tensor_tensor(newton[:, at], rough[:, at], rough[:, at], ALU.mult).then_inc(down_newton_set, 1)
                    pool.wait_ge(down_newton_set, 4 * d + 1)
                    nc.gpsimd.tensor_tensor(newton[:, at], newton[:, at], var_eps[:, at], ALU.mult).then_inc(down_newton_set, 1)
                    pool.wait_ge(down_newton_set, 4 * d + 2)
                    nc.gpsimd.tensor_tensor(newton[:, at], newton[:, at], minus_half, ALU.mult).then_inc(down_newton_set, 1)
                    pool.wait_ge(down_newton_set, 4 * d + 3)
                    nc.gpsimd.tensor_tensor(newton[:, at], newton[:, at], three_halves, ALU.add).then_inc(down_newton_set, 1)
                    pool.wait_ge(down_newton_set, 4 * d + 4)
                    nc.gpsimd.tensor_tensor(rstd[:, at], newton[:, at], rough[:, at], ALU.mult).then_inc(down_rstd_set, 1)

                def halves(b, n, half):
                    m = 32 * b + 2 * n + half
                    pool.wait_ge(q_rot_set, m + 1)
                    rot = q_tok[:, :, :, KVL:HD].rearrange("p t h (k f) -> p (t h) k f", k=2)
                    nc.gpsimd.tensor_tensor(rot, rot, q_sin[:, :, ::-1, :], ALU.add).then_inc(q_tok_set, 1)

                def steps(b, start, end):
                    group = GROUPS_0 + GROUPS * b
                    if end > FIRST:
                        rough_deviations(group if start == 0 else 0, FIRST, ST)
                    if start == 0:
                        rough_deviations(group + (1 if end > FIRST else 0), 0, 2)
                        pool.wait_ge(y_ps, 32 * b + 29)
                    z_constants()
                    if start == 0:
                        rough_deviations(group + (2 if end > FIRST else 1), 2, 2)
                    if end > DOWN:
                        for t in range(ST):
                            down_deviations(b, DOWN + t)
                        for half in range(2):
                            halves(b + 1, 0, half)

                def attend(b):
                    def work(g, u):
                        if u % UNITS in (0, 2) and within(g, u, UNITS * LAST_PAIR - 1):
                            halves(b, BODY_PAIRS * g + u // UNITS + 1, (u % UNITS) // 2)
                        if within(g, u, SLOTS - 1):
                            n = 80 * b + BODY * g + u
                            pool.wait_ge(inv_sum_set, n + 1)
                            for m, (_, i, c) in enumerate(MEMBERS[u % UNITS]):
                                w = (i + 1) * P
                                last = nc.gpsimd.tensor_tensor(prob[u % RING][:, c:c + w], prob[u % RING][:, c:c + w],
                                                               inv_sum[:, u % RING, m:m + 1].broadcast_to([P, w]),
                                                               ALU.mult)
                            last.then_inc(prob_scaled, 1)
                    attention((b, pool), work, 0)

                steps(-1, FIRST, STEPS)
                with loop(pool, 0, NB - 1) as b:
                    attend(b)
                    steps(b, 0, STEPS)
                attend(NB - 1)
                steps(NB - 1, 0, FIRST)

            @block.tensor
            def _(pe):
                def transpose_x(b, s):
                    pe.wait_ge(xn_set, 12 * b + 8 + s + 1)
                    for c in range(KC):
                        last = nc.tensor.transpose(X[0][:, c * P:(c + 1) * P],
                                                   xn[s % 2][:, c * P:(c + 1) * P], ident[:])
                    last.then_inc(xT_ps, 1)

                def wait_for_products(b, s, start):
                    m, updated, down = 12 * b + 8 + s, 8 * b + 4, 4 * (b + 1)
                    if start == FIRST:
                        if start + 2 <= s < DOWN + 2:
                            pe.wait_ge(x_updated, updated + s - 1)
                        elif s >= DOWN + 2:
                            pe.wait_ge(ckT_hi, down + s - DOWN - 1)
                            pe.wait_ge(ckT_lo, down + s - DOWN - 1)
                    elif start == 0 and s in (1, 2):
                        pe.wait_ge(y_added, 32 * b + 30 + s)
                    elif start + 3 <= s < DOWN + 2:
                        pe.wait_ge(x_updated, updated + s - 2)
                    elif s >= DOWN + 2:
                        pe.wait_ge(ckT_hi, down + s - DOWN - 1)
                        pe.wait_ge(ckT_lo, down + s - DOWN - 1)
                    pe.wait_ge(xT_hi_set, m + 1)
                    pe.wait_ge(xT_lo_set, m + 1)

                def ffn_products(b, s, half):
                    a, z = ((0, W0), (W0, WB))[half]
                    for c in range(KC):
                        for j, (xt, w) in enumerate(((xT_hi, wb_hi), (xT_hi, wb_lo), (xT_lo, wb_hi))):
                            last = nc.tensor.matmul(banks_of(s, first(b + 1))[:, half, 0:z - a], xt[s % 2][:, c, :], w[:, c, a:z],
                                                    start=(c == 0 and j == 0), stop=(c == KC - 1 and j == 2))
                    if half == 0:
                        last.then_inc(z_ps, 1)

                def down_products(b, s, half):
                    for c in (2 * half, 2 * half + 1):
                        for j, (xt, w) in enumerate(((xT_hi, wd_hi), (xT_hi, wd_lo), (xT_lo, wd_hi))):
                            last = nc.tensor.matmul(banks_of(s, first(b + 1))[:, 0, 0:DC], xt[s % 2][:, c, :], w[:, c, :],
                                                    start=(c == 0 and j == 0), stop=(c == KC - 1 and j == 2))
                    if half:
                        last.then_inc(down_ps, 1)

                def transpose_z(b, s):
                    pe.wait_ge(za_set, 8 * b + 4 + s + 1)
                    nc.tensor.transpose(Z[0][:, 0:P], za[s % 2][:].rearrange("p a z -> p (a z)"),
                                        ident[:]).then_inc(zT_ps, 1)

                def lora(b, s):
                    f = 8 * b + 4 + s
                    pe.wait_ge(zT_hi_set, f + 1)
                    pe.wait_ge(zT_lo_set, f + 1)
                    for j, zt in enumerate((zT_hi, zT_lo)):
                        for half in range(2):
                            last = nc.tensor.matmul(banks_of(s, first(b + 1))[:, half, 0:OH], zt[s % 2][:],
                                                    lora_up[:, half * OH:(half + 1) * OH],
                                                    start=False, stop=(j == 1), skip_group_check=True)
                    last.then_inc(y_done, 1)

                def transpose_down(b, s):
                    d = 4 * (b + 1) + s - DOWN
                    pe.wait_ge(down_set, d + 1)
                    pe.wait_ge(k_rot_set, d + 1)
                    for a in range(3):
                        last = nc.tensor.transpose(banks_of(s, first(b + 1))[:, 1, a * P:(a + 1) * P], down[s % 2][:, a, :], ident[:])
                    last.then_inc(ckT_ps, 1)

                def fold_output(g):
                    pe.wait_ge(out_in[g % 2], 32 * (g // 2 + 1))
                    if g:
                        pe.wait_ge(outw_hi, g)
                        pe.wait_ge(outw_lo, g)
                    for h in range(4):
                        c = 64 * (h % 2)
                        last = nc.tensor.matmul(Y[0][c:c + 64, h // 2, :], uv_nat[g % 2][:, h, :],
                                                wout_nat[g % 2][:, h, :], start=True, stop=True, tile_position=(0, c))
                    last.then_inc(outw_ps, 1)

                def steps(b, start, end):
                    transpose_x(b, start)
                    for s in range(start, end):
                        products = ffn_products if s < DOWN else down_products
                        wait_for_products(b, s, start)
                        products(b, s, 0)
                        if s > start:
                            (transpose_z if s <= DOWN else transpose_down)(b, s - 1)
                        if s + 1 < end:
                            transpose_x(b, s + 1)
                        if start == FIRST:
                            fold_output(s - FIRST)
                        products(b, s, 1)
                        if start < s <= DOWN:
                            lora(b, s - 1)
                    if end == FIRST:
                        transpose_z(b, end - 1)
                        lora(b, end - 1)
                    else:
                        pe.wait_ge(x_updated, 8 * b + 4 + DOWN)
                        if start == FIRST:
                            pe.wait_ge(ckT_hi, ST - 1)
                            pe.wait_ge(ckT_lo, ST - 1)
                        q_products(b + 1, 0, 0, True)
                        transpose_down(b, end - 1)
                        q_transposes(b + 1, 0, 0, True)
                        pe.wait_ge(ckT_hi, 4 * (b + 2))
                        pe.wait_ge(ckT_lo, 4 * (b + 2))
                        q_products(b + 1, 0, 1, False)
                        q_transposes(b + 1, 0, 1, False)

                def q_products(b, n, half, opening):
                    m = 32 * b + 2 * n + half
                    if not opening:
                        pe.wait_ge(q_lat_set, m)
                        pe.wait_ge(q_rot_set, m)
                    cols = [w[:, bass.ds(2 * n, 2), :].rearrange("p h r -> p (h r)") for w in (wq1_hi, wq1_lo, wq2)]
                    for tt in range(2):
                        rows = slice((2 * half + tt) * P, (2 * half + tt + 1) * P)
                        parts = ((cq_hi[:, 0, rows], cols[0]), (cq_hi[:, 0, rows], cols[1]), (cq_lo[:, 0, rows], cols[0]),
                                 (cq_hi[:, 1, rows], cols[2]), (cq_lo[:, 1, rows], cols[2]))
                        for j, (c, w) in enumerate(parts):
                            last = nc.tensor.matmul(q_ps[:, tt * 256:(tt + 1) * 256], c, w, start=(j == 0), stop=(j == 4))
                    last.then_inc(q_done, 1)

                def q_transposes(b, n, half, opening):
                    m = 32 * b + 2 * n + half
                    pe.wait_ge(q_tok_set, m + 1)
                    pe.wait_ge(q_lat_set, m + 1)
                    if not opening:
                        pe.wait_ge(qT_hi_set, m)
                        pe.wait_ge(qT_lo_set, m)
                    for h in range(2):
                        for tt in range(2):
                            last = nc.tensor.transpose(qT_ps[:, (2 * h + tt) * P:(2 * h + tt + 1) * P],
                                                       q_tok[:, tt, h, :], ident[:])
                    last.then_inc(qT_done, 1)

                def scores(b, g, u):
                    n = 80 * b + BODY * g + u
                    pair = 16 * b + BODY_PAIRS * g + u // UNITS
                    if u % UNITS == 0:
                        pe.wait_ge(qT_hi_set, 2 * pair + 2)
                        pe.wait_ge(qT_lo_set, 2 * pair + 2)
                    if known(g, u, 2):
                        pe.wait_ge(prob_set, n - 1)
                    par = (u // UNITS) % 2
                    members = [(c, (i + 1) * P, qT_hi[par][:, h, i * P:(i + 1) * P], qT_lo[par][:, h, i * P:(i + 1) * P])
                               for h, i, c in MEMBERS[u % UNITS]]
                    bank = score_ps[u % 2]
                    ends = [c + w for c, w, _, _ in members]
                    step, n = (ends[1] - ends[0] if len(ends) == 2 else P), len(ends)
                    diagonals = bank[:, ends[0] - P:ends[0] - P + (n - 1) * step + P] if step == P else \
                        bank.rearrange("p (a q) -> p a q", q=step)[:, :, step - P:step]
                    mask = causal[:].unsqueeze(1).broadcast_to([P, n, P])
                    if step == P:
                        diagonals = diagonals.rearrange("p (a q) -> p a q", q=P)
                    nc.tensor.matmul(diagonals, ident_bf[:], mask, start=True, stop=False, skip_group_check=True)
                    for c, w, high, low in members:
                        nc.tensor.matmul(bank[:, c:c + w], high, kT_hi[:, 0:w], start=False, stop=False,
                                         skip_group_check=True)
                        nc.tensor.matmul(bank[:, c:c + w], high, kT_lo[:, 0:w], start=False, stop=False,
                                         skip_group_check=True)
                        last = nc.tensor.matmul(bank[:, c:c + w], low, kT_hi[:, 0:w], start=False, stop=True,
                                                skip_group_check=True)
                    last.then_inc(scores_ps, 1)

                def bank_copies(b, g, v):
                    pair = 16 * b + BODY_PAIRS * g + v // UNITS
                    return 3 * pair + ACT_COPIES[v % UNITS], 2 * pair + DVE_COPIES[v % UNITS]

                def transpose_probs(b, g, v):
                    pe.wait_ge(prob_scaled, 80 * b + BODY * g + v + 1)
                    if known(g, v, 2):
                        by_act, by_dve = bank_copies(b, g, v - 2)
                        if (v - 2) % UNITS in ACT_BANKS:
                            pe.wait_ge(probT_by_act, by_act)
                        else:
                            pe.wait_ge(probT_by_dve, by_dve)
                    for h, i, c in MEMBERS[v % UNITS]:
                        for j in range(i + 1):
                            at = slice(c + j * P, c + (j + 1) * P)
                            last = nc.tensor.transpose(probT_ps[v % 2][:, at], prob[v % RING][:, at], ident[:])
                    last.then_inc(probT_done, 1)

                def pv(b, g, p, group):
                    pair = 16 * b + BODY_PAIRS * g + p
                    banks = [k for k in range(UNITS) if PV_GROUP[k] == group]
                    by_act, by_dve = bank_copies(b, g, UNITS * p + banks[-1])
                    pe.wait_ge(probT_by_act, by_act)
                    pe.wait_ge(probT_by_dve, by_dve)
                    if group == 0 and known(g, UNITS * p, UNITS):
                        pe.wait_ge(oT_hi_set, pair)
                        pe.wait_ge(oT_lo_set, pair)
                    where = {}
                    for k in banks:
                        for h, i, c in MEMBERS[k]:
                            where[i, h] = (probT[(UNITS * p + k) % RING], c)
                    for i in sorted({i for i, _ in where}, reverse=True):
                        for j in range(i + 1):
                            for h in range(2):
                                src, c = where[i, h]
                                last = nc.tensor.matmul(o_ps[64 * h:64 * h + 64, i * P:(i + 1) * P], ckv[:, j, :],
                                                        src[:, c + j * P:c + (j + 1) * P], start=(j == 0), stop=(j == i),
                                                        tile_position=(0, 64 * h))
                    last.then_inc(pv_done, 1)

                def output(b, g, two, t):
                    n = 32 * b + 4 * two + t
                    if t == 0:
                        pe.wait_ge(oT_hi_set, 16 * b + 2 * two + 2)
                        pe.wait_ge(oT_lo_set, 16 * b + 2 * two + 2)
                    if not (isinstance(two, int) and two == 0 and t == 0):
                        pe.wait_ge(y_added, n)
                    for k in range(2):
                        last = output_products(two, t, k, out_ps)
                    last.then_inc(y_ps, 1)

                def output_products(two, t, k, bank):
                    rows = slice(t * P, (t + 1) * P)
                    w_hi, w_lo = (w[:, bass.ds(2 * two + k, 1), :].rearrange("p a o -> p (a o)") for w in (wo_hi, wo_lo))
                    for j, (o, w) in enumerate(((oT_hi, w_hi), (oT_hi, w_lo), (oT_lo, w_hi))):
                        last = nc.tensor.matmul(bank, o[k][:, rows], w, start=(k == 0 and j == 0), stop=(k == 1 and j == 2))
                    return last

                def last_outputs(b):
                    two = PAIRS // 2 - 1
                    pe.wait_ge(y_added, 32 * b + 4 * two)
                    pe.wait_ge(oT_hi_set, 16 * b + PAIRS - 1)
                    pe.wait_ge(oT_lo_set, 16 * b + PAIRS - 1)
                    for t in range(ST - 1):
                        output_products(two, t, 0, last_out_ps[t])
                    pe.wait_ge(oT_hi_set, 16 * b + PAIRS)
                    pe.wait_ge(oT_lo_set, 16 * b + PAIRS)
                    for t in range(ST):
                        if t == ST - 1:
                            output_products(two, t, 0, last_out_ps[t])
                        output_products(two, t, 1, last_out_ps[t]).then_inc(y_ps, 1)

                def attend(b):
                    def work(g, u):
                        k, p = u % UNITS, u // UNITS
                        if within(g, u, SLOTS - 1):
                            scores(b, g, u)
                        queries = within(g, u, UNITS * LAST_PAIR - 1)
                        n = BODY_PAIRS * g + p + 1
                        if k in (0, 2) and queries:
                            q_products(b, n, k // 2, False)
                        if known(g, u, T_LAG) and within(g, u, SLOTS - 1 + T_LAG):
                            transpose_probs(b, g, u - T_LAG)
                        if k in PV_SLOT and known(g, u, UNITS):
                            pv(b, g, p - 1, PV_SLOT[k])
                        if p % 2 == 1 and k in OUT_SLOT and known(g, u, 3 * UNITS) and within(g, u, SLOTS - 1):
                            output(b, g, output_index(g, p), OUT_SLOT[k])
                        if k in (1, 3) and queries:
                            q_transposes(b, n, k // 2, False)
                    attention((b, pe), work, TAIL)
                    last_outputs(b)

                steps(-1, FIRST, STEPS)
                with loop(pe, 0, NB - 1) as b:
                    attend(b)
                    steps(b, 0, STEPS)
                attend(NB - 1)
                steps(NB - 1, 0, FIRST)

            @block.scalar
            def _(act):
                def xT_high(b, s):
                    act.wait_ge(xT_ps, 12 * b + 8 + s + 1)
                    nc.scalar.activation(xT_hi[s % 2][:].rearrange("p c q -> p (c q)"), X[0],
                                         ACT.Copy).then_inc(xT_hi_set, 1)

                def z_high(b, s):
                    act.wait_ge(zT_ps, 8 * b + 4 + s + 1)
                    nc.scalar.activation(zT_hi[s % 2][:], Z[0][:, 0:P], ACT.Copy).then_inc(zT_hi_set, 1)

                def gate_exponentials(b, s):
                    act.wait_ge(max_set, 8 * b + 4 + s + 1)
                    nc.scalar.activation(logit_exp, logit, ACT.Exp, bias=neg_logit_max, scale=1.0,
                                         accum_out=logit_sum).then_inc(logit_exp_set, 1)

                def down_copies(b, s):
                    t, d = s - DOWN, 4 * (b + 1) + s - DOWN
                    act.wait_ge(k_cos_set, d + 1)
                    flat, bank = down[s % 2][:].rearrange("p a r -> p (a r)"), banks_of(s, first(b + 1))[:, 0, :]
                    nc.scalar.activation(flat[:, 0:QL], bank[:, 0:QL], ACT.Copy)
                    nc.scalar.activation(flat[:, QL:2 * P + KVL], bank[:, P:QL + KVL], ACT.Copy)
                    nc.scalar.activation(ckv[:, t, :], bank[:, QL:QL + KVL], ACT.Copy).then_inc(down_set, 1)

                def ckT_high(b, s):
                    bank = banks_of(s, first(b + 1))[:, 1, :]
                    rows = slice((s - DOWN) * P, (s - DOWN + 1) * P)
                    act.wait_ge(ckT_ps, 4 * (b + 1) + s - DOWN + 1)
                    nc.scalar.activation(cq_hi[:, :, rows], bank[:, 0:2 * P].rearrange("p (a q) -> p a q", a=2), ACT.Copy)
                    nc.scalar.activation(kT_hi[:, rows], bank[:, 2 * P:3 * P], ACT.Copy,
                                         scale=SCORE_SCALE).then_inc(ckT_hi, 1)

                def output_hi(g):
                    act.wait_ge(outw_ps, g + 1)
                    nc.scalar.activation(wo_hi[:, 2 * g:2 * g + 2, :], Y[0][:], ACT.Copy).then_inc(outw_hi, 1)

                def steps(b, start, end):
                    xT_high(b, start)
                    for s in range(start, end):
                        if s > start:
                            (z_high if s <= DOWN else ckT_high)(b, s - 1)
                        if s < DOWN:
                            gate_exponentials(b, s)
                        if s + 1 < end:
                            xT_high(b, s + 1)
                        if start == FIRST:
                            output_hi(s - FIRST)
                        if s >= DOWN:
                            down_copies(b, s)
                    if end == FIRST:
                        z_high(b, end - 1)
                    else:
                        q_latent(b + 1, 0, 0)
                        ckT_high(b, end - 1)
                        qT_high(b + 1, 0, 0, 0)
                        q_latent(b + 1, 0, 1)
                        qT_high(b + 1, 0, 1, 0)

                def q_latent(b, n, half):
                    m = 32 * b + 2 * n + half
                    act.wait_ge(q_rot_set, m + 1)
                    if not (isinstance(n, int) and n == 0 and half == 0):
                        act.wait_ge(qT_done, m)
                    nc.scalar.activation(q_tok[:, :, :, 0:KVL].rearrange("p t h r -> p (t h) r"),
                                         q_ps.rearrange("p (a r) -> p a r", r=HD)[:, :, 0:KVL],
                                         ACT.Copy).then_inc(q_lat_set, 1)

                def qT_high(b, n, half, par):
                    act.wait_ge(qT_done, 32 * b + 2 * n + half + 1)
                    nc.scalar.activation(qT_hi[par][:, :, half * 256:(half + 1) * 256],
                                         qT_ps.rearrange("p (h q) -> p h q", h=2), ACT.Copy).then_inc(qT_hi_set, 1)

                def oT_high(b, g, p):
                    act.wait_ge(pv_done, 3 * (16 * b + BODY_PAIRS * g + p - 1))
                    if known(g, UNITS * p, 4 * UNITS):
                        act.wait_ge(y_ps, 32 * b + ST * ((BODY_PAIRS // 2) * g + (p - 4) // 2) + ST)
                    nc.scalar.activation(oT_hi[p % 2][:], o_ps, ACT.Copy).then_inc(oT_hi_set, 1)

                def attend(b):
                    def work(g, u):
                        k, p = u % UNITS, u // UNITS
                        n1 = BODY_PAIRS * g + p + 1
                        queries = within(g, u, UNITS * LAST_PAIR - 1)
                        if k == 0 and known(g, u, 2 * UNITS):
                            oT_high(b, g, p)
                        if k in (2, 4) and queries:
                            qT_high(b, n1, k // 2 - 1, (p + 1) % 2)
                        if k in (1, 3) and queries:
                            q_latent(b, n1, k // 2)
                        if within(g, u, SLOTS - 1):
                            n = 80 * b + BODY * g + u
                            act.wait_ge(neg_max_set, n + 1)
                            if known(g, u, RING):
                                act.wait_ge(probT_done, n - RING + 1)
                            for m, (_, i, c) in enumerate(MEMBERS[k]):
                                w = (i + 1) * P
                                last = nc.scalar.activation(prob[u % RING][:, c:c + w], score_ps[u % 2][:, c:c + w],
                                                            ACT.Exp, bias=neg_max[:, u % RING, m:m + 1], scale=1.0,
                                                            accum_out=row_sum[:, u % RING, m:m + 1])
                            last.then_inc(prob_set, 1)
                        v = u - T_LAG
                        if known(g, u, T_LAG) and within(g, u, SLOTS - 1 + T_LAG) and v % UNITS in ACT_BANKS:
                            copy_probT(act, nc.scalar, b, g, v)
                    attention((b, act), work, TAIL)

                steps(-1, FIRST, STEPS)
                with loop(act, 0, NB - 1) as b:
                    attend(b)
                    steps(b, 0, STEPS)
                attend(NB - 1)
                steps(NB - 1, 0, FIRST)

            @block.vector
            def _(dve):
                def source(b, s):
                    return x_next if FIRST <= s < DOWN and not first(b + 1) else x_sb

                def row_stats(b, s, before=None):
                    if before is not None:
                        dve.wait_ge(stats_set, before)
                    if FIRST <= s < DOWN:
                        dve.wait_ge(x_in[s - FIRST], 16 * (b + 2))
                    nc.vector.bn_stats(stats[:, s % ST, :], source(b, s)[:, s % ST, :]).then_inc(stats_set, 1)

                def row_moments(s):
                    return nc.vector.bn_aggr(moments[:, s, :], stats[:, s % ST, :])

                def deviations(group, s, n, roughs):
                    at = slice(s, s + n)
                    dve.wait_ge(rough_set, roughs)
                    nc.vector.tensor_tensor(newton[:, at], rough[:, at], rough[:, at], ALU.mult).then_inc(newton_set, 1)
                    dve.wait_ge(newton_set, 3 * group + 1)
                    nc.vector.tensor_tensor(newton[:, at], newton[:, at], var_eps[:, at], ALU.mult).then_inc(newton_set, 1)
                    dve.wait_ge(newton_set, 3 * group + 2)
                    nc.vector.tensor_scalar(newton[:, at], newton[:, at], -0.5, 1.5, ALU.mult, ALU.add).then_inc(newton_set, 1)
                    dve.wait_ge(newton_set, 3 * group + 3)
                    nc.vector.tensor_tensor(rstd[:, at], newton[:, at], rough[:, at], ALU.mult).then_inc(rstd_set, 1)
                    dve.wait_ge(rstd_set, group + 1)

                def norm(b, s, start):
                    if s >= start + 2:
                        dve.wait_ge(xT_ps, 12 * b + 8 + s - 1)
                    nc.vector.tensor_scalar(xn[s % 2][:], source(b, s)[:, s % ST, :], moments[:, s, 0:1],
                                            rstd[:, s:s + 1], ALU.subtract, ALU.mult).then_inc(xn_set, 1)

                def xT_low(b, s, stats_count=None):
                    dve.wait_ge(xT_hi_set, 12 * b + 8 + s + 1)
                    if stats_count is not None:
                        dve.wait_ge(stats_set, stats_count)
                    nc.vector.tensor_tensor(xT_lo[s % 2][:].rearrange("p c q -> p (c q)"), X[0],
                                            f32(xT_hi[s % 2][:]).rearrange("p c q -> p (c q)"),
                                            ALU.subtract).then_inc(xT_lo_set, 1)

                def gate_logits(b, s):
                    f = 8 * b + 4 + s
                    dve.wait_ge(z_ps, f + 1)
                    nc.vector.tensor_tensor(logit, banks_of(s, first(b + 1))[:, 0, OH + NZ:W0], prior_row, ALU.add).then_inc(logit_set, 1)
                    dve.wait_ge(logit_set, f + 1)
                    nc.vector.reduce_max(neg_logit_max, logit, AX, negate=True).then_inc(max_set, 1)

                def gate_rows(b, s, start):
                    f, bank = 8 * b + 4 + s, banks_of(s, first(b + 1))
                    dve.wait_ge(logit_exp_set, f + 1)
                    nc.vector.reciprocal(inv_logit_sum, logit_sum).then_inc(sum_inv_set, 1)
                    dve.wait_ge(sum_inv_set, f + 1)
                    nc.vector.tensor_scalar(alpha, logit_exp, inv_logit_sum, LORA_SCALE,
                                            ALU.mult, ALU.mult).then_inc(alpha_set, 1)
                    if s == start:
                        dve.wait_ge(z_static, b + 2)
                    if s >= start + 2:
                        dve.wait_ge(zT_ps, f - 1)
                    dve.wait_ge(alpha_set, f + 1)
                    gate = alpha.unsqueeze(2).broadcast_to([P, NE, R])
                    for half in range(2):
                        last = nc.vector.tensor_tensor(za[s % 2][:, half, 0:NZ].rearrange("p (e r) -> p e r", e=NE),
                                                       bank[:, 0, OH:OH + NZ].rearrange("p (e r) -> p e r", e=NE),
                                                       gate, ALU.mult)
                    last.then_inc(za_set, 1)

                def z_low(b, s):
                    dve.wait_ge(zT_hi_set, 8 * b + 4 + s + 1)
                    nc.vector.tensor_tensor(zT_lo[s % 2][0:64, :], Z[0][0:64, 0:P], f32(zT_hi[s % 2][0:64, :]),
                                            ALU.subtract).then_inc(zT_lo_set, 1)

                def update_rows(b, s):
                    if FIRST <= s and not first(b + 1):
                        dve.wait_ge(x_out[s - FIRST], 16 * (b + 1))
                    dve.wait_ge(y_done, 8 * b + 4 + s + 1)
                    old, new = (x[:, s % ST, :].rearrange("p (a o) -> p a o", a=2) for x in (source(b, s), x_sb))
                    nc.vector.scalar_tensor_tensor(out=new, in0=banks_of(s, first(b + 1))[:, :, 0:OH], scalar=0.5, in1=old,
                                                   op0=ALU.mult, op1=ALU.add).then_inc(x_updated, 1)

                def key_rotary(b, s):
                    t, d = s - DOWN, 4 * (b + 1) + s - DOWN
                    dve.wait_ge(down_ps, d + 1)
                    if t >= 2:
                        dve.wait_ge(ckT_ps, d - 1)
                    key = banks_of(s, first(b + 1))[:, 0, QL + KVL:DC].rearrange("p (k f) -> p k f", k=2)
                    rot = down[s % 2][:, 2, KVL:HD].rearrange("p (k f) -> p k f", k=2)
                    nc.vector.tensor_tensor(rot, key, cos_sb[:, t, :].unsqueeze(1).broadcast_to([P, 2, HALF]), ALU.mult)
                    nc.vector.tensor_tensor(k_sin[:], key, sin_sb[:, t, :, :], ALU.mult).then_inc(k_cos_set, 1)
                    dve.wait_ge(k_cos_set, d + 1)
                    nc.vector.tensor_tensor(rot, rot, k_sin[:, ::-1, :], ALU.add).then_inc(k_rot_set, 1)

                def ckT_low(b, s):
                    bank = banks_of(s, first(b + 1))[:, 1, :]
                    rows = slice((s - DOWN) * P, (s - DOWN + 1) * P)
                    dve.wait_ge(ckT_hi, 4 * (b + 1) + s - DOWN + 1)
                    nc.vector.tensor_tensor(cq_lo[:, 0, rows], bank[:, 0:P], f32(cq_hi[:, 0, rows]), ALU.subtract)
                    nc.vector.tensor_tensor(cq_lo[0:64, 1, rows], bank[0:64, P:2 * P], f32(cq_hi[0:64, 1, rows]),
                                            ALU.subtract)
                    nc.vector.scalar_tensor_tensor(out=kT_lo[:, rows], in0=bank[:, 2 * P:3 * P], scalar=SCORE_SCALE,
                                                   in1=f32(kT_hi[:, rows]), op0=ALU.mult,
                                                   op1=ALU.subtract).then_inc(ckT_lo, 1)

                def output_lo(g):
                    dve.wait_ge(outw_hi, g + 1)
                    nc.vector.tensor_tensor(wo_lo[:, 2 * g:2 * g + 2, :], Y[0][:], f32(wo_hi[:, 2 * g:2 * g + 2, :]),
                                            ALU.subtract).then_inc(outw_lo, 1)

                def steps(b, start, end):
                    group, roughs = 1 + 3 * b, GROUPS_0 + GROUPS * b
                    if start == FIRST:
                        dve.wait_ge(stats_set, ST)
                        for s in range(FIRST, DOWN):
                            last = row_moments(s)
                        last.then_inc(var_set, 1)
                        deviations(0, FIRST, ST, 1)
                    norm(b, start, start)
                    norm(b, start + 1, start)
                    if start == 0:
                        dve.wait_ge(y_added, 32 * (b + 1))
                        for t in (2, 3):
                            row_stats(b, t)
                    xT_low(b, start, 12 * b + 8 + (2 * ST if end > FIRST else ST) if start == 0 else None)
                    if start == 0:
                        row_moments(2)
                        row_moments(3).then_inc(var_set, 1)
                        if end > FIRST:
                            deviations(group + 1, FIRST, ST, roughs + 1)
                            deviations(group + 2, 2, 2, roughs + 3)
                        else:
                            deviations(group + 1, 2, 2, roughs + 2)
                    for s in range(start, end):
                        if s - 2 >= start and s - 2 < DOWN:
                            update_rows(b, s - 2)
                        if DOWN <= s + 1 < end:
                            dve.wait_ge(down_rstd_set, 4 * (b + 1) + s + 2 - DOWN)
                        if start < s < end - 1:
                            norm(b, s + 1, start)
                        if DOWN <= s + 2 < end:
                            dve.wait_ge(x_updated, 8 * b + 4 + s - 1)
                            row_stats(b, s + 2)
                        if DOWN <= s + 2 < end:
                            dve.wait_ge(stats_set, 12 * b + 8 + s + 3)
                        if s < DOWN:
                            gate_logits(b, s)
                            if DOWN <= s + 2 < end:
                                row_moments(s + 2).then_inc(var_set, 1)
                        if s > start:
                            (z_low if s <= DOWN else ckT_low)(b, s - 1)
                            if DOWN <= s and s + 2 < end:
                                row_moments(s + 2).then_inc(var_set, 1)
                        if s < DOWN:
                            gate_rows(b, s, start)
                        if s + 1 < end:
                            xT_low(b, s + 1)
                        if start == FIRST:
                            output_lo(s - FIRST)
                        if s >= DOWN:
                            key_rotary(b, s)
                    if end == FIRST:
                        update_rows(b, end - 2)
                        z_low(b, end - 1)
                        update_rows(b, end - 1)
                    else:
                        q_rotary(b + 1, 0, 0)
                        ckT_low(b, end - 1)
                        qT_low(b + 1, 0, 0, 0)
                        q_rotary(b + 1, 0, 1)
                        qT_low(b + 1, 0, 1, 0)

                def q_rotary(b, n, half):
                    m = 32 * b + 2 * n + half
                    dve.wait_ge(q_done, m + 1)
                    if not (isinstance(n, int) and n == 0 and half == 0):
                        dve.wait_ge(qT_done, m)
                    for tt in range(2):
                        t = 2 * half + tt
                        q = q_ps[:, tt * 256:(tt + 1) * 256].rearrange("p (h r) -> p h r", h=2)[:, :, KVL:HD] \
                            .rearrange("p h (k f) -> p h k f", k=2)
                        nc.vector.tensor_tensor(q_tok[:, tt, :, KVL:HD].rearrange("p h (k f) -> p h k f", k=2), q,
                                                cos_sb[:, t, :].unsqueeze(1).unsqueeze(1).broadcast_to([P, 2, 2, HALF]),
                                                ALU.mult)
                        last = nc.vector.tensor_tensor(q_sin[:, 2 * tt:2 * tt + 2, :, :], q,
                                                       sin_sb[:, t, :, :].unsqueeze(1).broadcast_to([P, 2, 2, HALF]),
                                                       ALU.mult)
                    last.then_inc(q_rot_set, 1)

                def qT_low(b, n, half, par):
                    dve.wait_ge(qT_hi_set, 32 * b + 2 * n + half + 1)
                    at = slice(half * 256, (half + 1) * 256)
                    nc.vector.tensor_tensor(qT_lo[par][:, :, at], qT_ps.rearrange("p (h q) -> p h q", h=2),
                                            f32(qT_hi[par][:, :, at]), ALU.subtract).then_inc(qT_lo_set, 1)

                def inverse_sums(b, g, v):
                    n = 80 * b + BODY * g + v
                    dve.wait_ge(prob_set, n + 1)
                    k = len(MEMBERS[v % UNITS])
                    nc.vector.reciprocal(inv_sum[:, v % RING, 0:k], row_sum[:, v % RING, 0:k]).then_inc(inv_sum_set, 1)

                def add_output(b, two, t, bank=out_ps):
                    dve.wait_ge(y_ps, 32 * b + 4 * two + t + 1)
                    nc.vector.tensor_tensor(x_sb[:, t, :], bank, x_sb[:, t, :], ALU.add).then_inc(y_added, 1)

                def last_outputs(b, more):
                    count = 12 * b + 8 + (ST if more else 0)
                    for t in range(ST):
                        if t in (1, 2):
                            dve.wait_ge(stats_set, count + t)
                        add_output(b, PAIRS // 2 - 1, t, last_out_ps[t])
                        if t in (1, 2):
                            done = row_moments(t - 1)
                            if t == 2:
                                done.then_inc(var_set, 1)
                        if t < 2:
                            dve.wait_ge(y_added, 32 * b + 29 + t)
                            row_stats(b, t)
                    deviations(1 + 3 * b, 0, 2, GROUPS_0 + GROUPS * b + (2 if more else 1))

                def next_stats(b):
                    count = 12 * b + 8
                    for s in range(FIRST, DOWN):
                        row_stats(b, s, count + s - FIRST if s > FIRST else None)
                        if s > FIRST:
                            row_moments(s - 1)
                    dve.wait_ge(stats_set, count + ST)

                def attend(b, more):
                    def work(g, u):
                        k, p = u % UNITS, u // UNITS
                        last_slot = first(BODIES - 1 - g) and u == BODY + TAIL - 1
                        if last_slot and more:
                            next_stats(b)
                        n1 = BODY_PAIRS * g + p + 1
                        queries = within(g, u, UNITS * LAST_PAIR - 1)
                        if k in (2, 4) and queries:
                            qT_low(b, n1, k // 2 - 1, (p + 1) % 2)
                        if within(g, u, SLOTS - 1):
                            dve.wait_ge(scores_ps, 80 * b + BODY * g + u + 1)
                            for m, (_, i, c) in enumerate(MEMBERS[k]):
                                last = nc.vector.reduce_max(neg_max[:, u % RING, m:m + 1],
                                                            score_ps[u % 2][:, c:c + (i + 1) * P], AX, negate=True)
                            last.then_inc(neg_max_set, 1)
                        if k in (0, 2) and queries:
                            q_rotary(b, n1, k // 2)
                        if k == 0 and known(g, u, 2 * UNITS):
                            dve.wait_ge(oT_hi_set, 16 * b + BODY_PAIRS * g + p - 1)
                            nc.vector.tensor_tensor(oT_lo[p % 2][:], o_ps, f32(oT_hi[p % 2][:]),
                                                    ALU.subtract).then_inc(oT_lo_set, 1)
                        if last_slot and more:
                            row_moments(DOWN - 1).then_inc(var_set, 1)
                        v = u - T_LAG
                        if known(g, u, T_LAG) and within(g, u, SLOTS - 1 + T_LAG) and v % UNITS not in ACT_BANKS:
                            copy_probT(dve, nc.vector, b, g, v)
                        if within(g, u, SLOTS - 1):
                            inverse_sums(b, g, u)
                        if p % 2 == 1 and k in OUT_SLOT and known(g, u, 3 * UNITS) and within(g, u, SLOTS - 1):
                            add_output(b, output_index(g, p), OUT_SLOT[k])
                    attention((b, dve), work, TAIL)

                steps(-1, FIRST, STEPS)
                with loop(dve, 0, NB - 1) as b:
                    attend(b, True)
                    last_outputs(b, True)
                    steps(b, 0, STEPS)
                attend(NB - 1, False)
                last_outputs(NB - 1, False)
                steps(NB - 1, 0, FIRST)


def kernel(**inputs):
    import numpy as _np
    import concourse.bacc as _bacc
    from concourse import mybir as _mybir
    from concourse.bass_utils import run_bass_kernel_spmd as _run

    nc = _bacc.Bacc("TRN2", target_bir_lowering=False, num_devices=1)
    arrays, args = {}, []
    for name in _INS:
        a = _np.ascontiguousarray(inputs[name])
        arrays[f"in_{name}_dram"] = a
        args.append(nc.dram_tensor(f"in_{name}_dram", a.shape, _mybir.dt.from_np(a.dtype), kind="ExternalInput").ap())
    for name, a in zip(("rope_cos", "rope_sin"), rope_tables()):
        arrays[f"in_{name}_dram"] = a
        args.append(nc.dram_tensor(f"in_{name}_dram", a.shape, F32, kind="ExternalInput").ap())
    args.append(nc.dram_tensor("out_0_dram", (NB, S, D), F32, kind="ExternalOutput").ap())
    build(nc, *args)
    r = _run(nc, [arrays], core_ids=[0])
    return r.results[0]["out_0_dram"]
```
